# Optimizing a Trainium2 kernel written in Bass

```python
import numpy as np
import jax
import jax.numpy as jnp

def _softmax(x, axis=-1):
    return jax.nn.softmax(x, axis=axis)

def _gelu(x):
    return jax.nn.gelu(x, approximate=True)

def _silu(x):
    return jax.nn.silu(x)

def _sigmoid(x):
    return jax.nn.sigmoid(x)

def _layernorm(x, axis=-1, eps=1e-05):
    m = jnp.mean(x, axis=axis, keepdims=True)
    v = jnp.var(x, axis=axis, keepdims=True)
    return (x - m) / jnp.sqrt(v + eps)

def _scatter_add(tgt, idx, src, axis=0):
    return tgt.at[idx].add(src)

def _segment_sum(src, seg, n):
    return jax.ops.segment_sum(src, seg, n)
kernel_name = 'mk_lm_tower_d1_tok_ids768_r4_eb8435'

def setup_inputs(seed: int=0):
    np.random.seed(seed)
    _w = jnp.asarray

    def _rec_inputs():
        import jax
        import jax.numpy as jnp
        _rk = jax.random.key(seed)
        x = jax.random.randint(jax.random.fold_in(_rk, 1), (4, 1024), 0, 31999, jnp.int32)
        mask_BS_i2_0 = jnp.where(jnp.ones((4, 1024), dtype=bool), 2, 0).astype(jnp.int32)
        return (x, mask_BS_i2_0)
    x, mask_BS_i2_0 = _rec_inputs()

    def _L0_tok_setup():
        import jax, jax.numpy as jnp
        import numpy as np
        VOCAB = 8000
        DIM = 192
        BATCH = 8
        SEQ = 512

        def _sinusoidal_pos(seq_len, dim):
            pos = jnp.arange(seq_len, dtype=jnp.float32)[:, None]
            ids = jnp.arange(dim, dtype=jnp.float32)[None, :]
            even_exp = jnp.floor(ids / 2.0) * 2.0 / dim
            angle = pos / jnp.power(10000.0, even_exp)
            return jnp.where(jnp.arange(dim) % 2 == 0, jnp.sin(angle), jnp.cos(angle))
        key = jax.random.key(seed)
        k1, k2, k3, k4 = jax.random.split(key, 4)
        input_tensor = jax.random.randint(k1, (BATCH, SEQ), 0, VOCAB)
        segment_label = jax.random.randint(k2, (BATCH, SEQ), 0, 3)
        token_table = jax.random.normal(k3, (VOCAB, DIM), dtype=jnp.float32) * 0.02
        segm_table = jax.random.normal(k4, (3, DIM), dtype=jnp.float32) * 0.02
        token_table = token_table.at[0].set(0.0)
        segm_table = segm_table.at[0].set(0.0)
        return {'input_tensor': input_tensor, 'segment_label': segment_label, 'token_table': token_table, 'segm_table': segm_table}
    _L0_tok_all = _L0_tok_setup()
    _L0_tok_in = {k: v for k, v in _L0_tok_all.items() if k in ('token_table', 'segm_table')}
    del _L0_tok_all

    def _L0_attn_setup():
        import jax, jax.numpy as jnp
        import numpy as np
        import math
        D_MODEL = 192
        N_HEADS = 12
        D_HEAD = D_MODEL // N_HEADS
        LATENT = 128
        HIDDEN = 512
        B, L = (1, 512)

        def _w(key, shape, scale=0.02):
            return jax.random.normal(key, shape, dtype=jnp.float32) * scale

        def rmsnorm(x, w, eps=1e-06):
            xf = x.astype(jnp.float32)
            rms = jax.lax.rsqrt(jnp.mean(xf * xf, axis=-1, keepdims=True) + eps)
            return w * (xf * rms).astype(x.dtype)

        def rope(x):
            Lx, Dh = (x.shape[1], x.shape[3])
            inv_freq = 1.0 / 10000.0 ** (jnp.arange(0, Dh, 2, dtype=jnp.float32) / Dh)
            t = jnp.arange(Lx, dtype=jnp.float32)
            freqs = jnp.outer(t, inv_freq)
            emb = jnp.concatenate([freqs, freqs], -1)
            cos = jnp.cos(emb)[None, :, None, :]
            sin = jnp.sin(emb)[None, :, None, :]
            x1, x2 = jnp.split(x, 2, axis=-1)
            x_rot = jnp.concatenate([-x2, x1], axis=-1)
            return x * cos + x_rot * sin
        key = jax.random.key(seed)
        ks = jax.random.split(key, 12)
        return {'x': jax.random.normal(ks[0], (B, L, D_MODEL), dtype=jnp.float32), 'ln_w': jnp.ones((D_MODEL,), jnp.float32), 'w_comp': _w(ks[1], (D_MODEL, LATENT)), 'w_qkv': _w(ks[2], (LATENT, 3 * D_MODEL)), 'w_reso': _w(ks[3], (LATENT, N_HEADS * 4)), 'qn_w': jnp.ones((D_HEAD,), jnp.float32), 'kn_w': jnp.ones((D_HEAD,), jnp.float32), 'w_outgate': _w(ks[4], (LATENT, D_MODEL)), 'head_decay': jnp.linspace(-3.0, 1.0, N_HEADS, dtype=jnp.float32), 'temperature': jnp.ones((1,), jnp.float32) * 0.5, 'w_proj': _w(ks[5], (D_MODEL, D_MODEL)), 'memn_w': jnp.ones((D_MODEL,), jnp.float32), 'ffn_ln_w': jnp.ones((D_MODEL,), jnp.float32), 'w1': _w(ks[6], (D_MODEL, HIDDEN)), 'w2': _w(ks[7], (D_MODEL, HIDDEN)), 'w3': _w(ks[8], (HIDDEN, D_MODEL))}
    _L0_attn_all = _L0_attn_setup()
    _L0_attn_in = {k: v for k, v in _L0_attn_all.items() if k in ('ln_w', 'w_comp', 'w_qkv', 'w_reso', 'qn_w', 'kn_w', 'w_outgate', 'head_decay', 'temperature', 'w_proj', 'memn_w', 'ffn_ln_w', 'w1', 'w2', 'w3')}
    del _L0_attn_all

    def _L0_ffn_setup():
        import jax, jax.numpy as jnp
        import numpy as np
        SEQ, BATCH, EMBED = (256, 2, 192)
        E = 16
        FFN_H = 384
        K_SHARED = 1
        K_ROUTE = 3
        LN_EPS = 1e-05
        NEG_INF = -1000000000.0
        key = jax.random.key(seed)
        ks = jax.random.split(key, 4)
        x = jax.random.normal(ks[0], (SEQ, BATCH, EMBED), dtype=jnp.float32)
        gate_w = jax.random.normal(ks[1], (EMBED, E), dtype=jnp.float32) * 0.02
        gate_b = jnp.zeros((E,), jnp.float32)
        fc1_w = jax.random.normal(ks[2], (E, EMBED, FFN_H), dtype=jnp.float32) * 0.02
        fc1_b = jnp.zeros((E, FFN_H), jnp.float32)
        ln_w = jnp.ones((E, FFN_H), jnp.float32)
        ln_b = jnp.zeros((E, FFN_H), jnp.float32)
        fc2_w = jax.random.normal(ks[3], (E, FFN_H, EMBED), dtype=jnp.float32) * 0.02
        fc2_b = jnp.zeros((E, EMBED), jnp.float32)
        return {'x': x, 'gate_w': gate_w, 'gate_b': gate_b, 'fc1_w': fc1_w, 'fc1_b': fc1_b, 'ln_w': ln_w, 'ln_b': ln_b, 'fc2_w': fc2_w, 'fc2_b': fc2_b}
    _L0_ffn_all = _L0_ffn_setup()
    _L0_ffn_in = {k: v for k, v in _L0_ffn_all.items() if k in ('gate_w', 'gate_b', 'fc1_w', 'fc1_b', 'ln_w', 'ln_b', 'fc2_w', 'fc2_b')}
    del _L0_ffn_all
    return {'x': x, 'mask_BS_i2_0': mask_BS_i2_0, 'L0_tok_token_table': _L0_tok_in['token_table'], 'L0_tok_segm_table': _L0_tok_in['segm_table'], 'L0_attn_ln_w': _L0_attn_in['ln_w'], 'L0_attn_w_comp': _L0_attn_in['w_comp'], 'L0_attn_w_qkv': _L0_attn_in['w_qkv'], 'L0_attn_w_reso': _L0_attn_in['w_reso'], 'L0_attn_qn_w': _L0_attn_in['qn_w'], 'L0_attn_kn_w': _L0_attn_in['kn_w'], 'L0_attn_w_outgate': _L0_attn_in['w_outgate'], 'L0_attn_head_decay': _L0_attn_in['head_decay'], 'L0_attn_temperature': _L0_attn_in['temperature'], 'L0_attn_w_proj': _L0_attn_in['w_proj'], 'L0_attn_memn_w': _L0_attn_in['memn_w'], 'L0_attn_ffn_ln_w': _L0_attn_in['ffn_ln_w'], 'L0_attn_w1': _L0_attn_in['w1'], 'L0_attn_w2': _L0_attn_in['w2'], 'L0_attn_w3': _L0_attn_in['w3'], 'L0_ffn_gate_w': _L0_ffn_in['gate_w'], 'L0_ffn_gate_b': _L0_ffn_in['gate_b'], 'L0_ffn_fc1_w': _L0_ffn_in['fc1_w'], 'L0_ffn_fc1_b': _L0_ffn_in['fc1_b'], 'L0_ffn_ln_w': _L0_ffn_in['ln_w'], 'L0_ffn_ln_b': _L0_ffn_in['ln_b'], 'L0_ffn_fc2_w': _L0_ffn_in['fc2_w'], 'L0_ffn_fc2_b': _L0_ffn_in['fc2_b']}

def reference(x, mask_BS_i2_0, L0_tok_token_table, L0_tok_segm_table, L0_attn_ln_w, L0_attn_w_comp, L0_attn_w_qkv, L0_attn_w_reso, L0_attn_qn_w, L0_attn_kn_w, L0_attn_w_outgate, L0_attn_head_decay, L0_attn_temperature, L0_attn_w_proj, L0_attn_memn_w, L0_attn_ffn_ln_w, L0_attn_w1, L0_attn_w2, L0_attn_w3, L0_ffn_gate_w, L0_ffn_gate_b, L0_ffn_fc1_w, L0_ffn_fc1_b, L0_ffn_ln_w, L0_ffn_ln_b, L0_ffn_fc2_w, L0_ffn_fc2_b):
    import jax
    import jax.numpy as jnp

    def _L0_tok_ref(input_tensor, segment_label, token_table, segm_table):
        import jax, jax.numpy as jnp
        import numpy as np
        VOCAB = 8000
        DIM = 192
        BATCH = 8
        SEQ = 512

        def _sinusoidal_pos(seq_len, dim):
            pos = jnp.arange(seq_len, dtype=jnp.float32)[:, None]
            ids = jnp.arange(dim, dtype=jnp.float32)[None, :]
            even_exp = jnp.floor(ids / 2.0) * 2.0 / dim
            angle = pos / jnp.power(10000.0, even_exp)
            return jnp.where(jnp.arange(dim) % 2 == 0, jnp.sin(angle), jnp.cos(angle))
        batch, seq = input_tensor.shape
        pos = _sinusoidal_pos(seq, token_table.shape[1])
        tokens_embed = token_table[input_tensor]
        segments_embed = segm_table[segment_label]
        return segments_embed + pos[None, :, :] + tokens_embed

    def _L0_attn_ref(x, ln_w, w_comp, w_qkv, w_reso, qn_w, kn_w, w_outgate, head_decay, temperature, w_proj, memn_w, ffn_ln_w, w1, w2, w3):
        import jax, jax.numpy as jnp
        import numpy as np
        import math
        D_MODEL = 192
        N_HEADS = 12
        D_HEAD = D_MODEL // N_HEADS
        LATENT = 128
        HIDDEN = 512
        B, L = (1, 512)

        def _w(key, shape, scale=0.02):
            return jax.random.normal(key, shape, dtype=jnp.float32) * scale

        def rmsnorm(x, w, eps=1e-06):
            xf = x.astype(jnp.float32)
            rms = jax.lax.rsqrt(jnp.mean(xf * xf, axis=-1, keepdims=True) + eps)
            return w * (xf * rms).astype(x.dtype)

        def rope(x):
            Lx, Dh = (x.shape[1], x.shape[3])
            inv_freq = 1.0 / 10000.0 ** (jnp.arange(0, Dh, 2, dtype=jnp.float32) / Dh)
            t = jnp.arange(Lx, dtype=jnp.float32)
            freqs = jnp.outer(t, inv_freq)
            emb = jnp.concatenate([freqs, freqs], -1)
            cos = jnp.cos(emb)[None, :, None, :]
            sin = jnp.sin(emb)[None, :, None, :]
            x1, x2 = jnp.split(x, 2, axis=-1)
            x_rot = jnp.concatenate([-x2, x1], axis=-1)
            return x * cos + x_rot * sin
        Bx, Lx, D = x.shape
        H, Dh = (N_HEADS, D_HEAD)
        x_norm = rmsnorm(x, ln_w)
        latent = jax.nn.silu(x_norm @ w_comp)
        qkv = latent @ w_qkv
        q, k, v = jnp.split(qkv, 3, axis=-1)
        q = q.reshape(Bx, Lx, H, Dh)
        k = k.reshape(Bx, Lx, H, Dh)
        v = v.reshape(Bx, Lx, H, Dh)
        q = rope(rmsnorm(q, qn_w))
        k = rope(rmsnorm(k, kn_w))
        q_f = jax.nn.elu(q.astype(jnp.float32)) + 1.0
        k_f = jax.nn.elu(k.astype(jnp.float32)) + 1.0
        v_f = v.astype(jnp.float32)
        params = (latent @ w_reso).reshape(Bx, Lx, H, 4)
        sem_amp = jax.nn.sigmoid(params[..., 0])
        sem_phase = jax.nn.sigmoid(params[..., 1]) * math.pi
        ctx_amp = jax.nn.sigmoid(params[..., 2])
        ctx_phase = jax.nn.sigmoid(params[..., 3]) * math.pi
        raw_decay = 0.3 + 0.65 * jax.nn.sigmoid(head_decay.reshape(1, 1, H))
        decay_rate = jnp.clip(raw_decay, 1e-05, 0.999)
        dt = 1.0 - decay_rate
        base_gate = jax.nn.sigmoid(sem_amp * ctx_amp * jnp.cos(sem_phase - ctx_phase) * temperature)
        gate = jnp.clip(base_gate * 1.2 - 0.1, 0.05, 0.95)
        kv_input = jnp.einsum('blhd,blhe->blhde', k_f, v_f) * gate[..., None, None]
        kv_input = kv_input * dt[..., None, None]
        z_input = k_f * dt[..., None]
        log_decay = jnp.log(decay_rate)[..., None]
        cum_log_decay = jnp.cumsum(jnp.broadcast_to(log_decay, (Bx, Lx, H, 1)), axis=1)
        df = jnp.exp(cum_log_decay)
        safe_df_z = df + 1e-08
        kv_states = jnp.cumsum(kv_input / safe_df_z[..., None], axis=1) * df[..., None]
        z_states = jnp.cumsum(z_input / safe_df_z, axis=1) * df
        out_num = jnp.einsum('blhd,blhde->blhe', q_f, kv_states)
        den = jnp.clip(jnp.sum(q_f * z_states, axis=-1, keepdims=True), 1e-05, None)
        out = (out_num / den).reshape(Bx, Lx, D)
        out = rmsnorm(out, memn_w)
        attn_out = out @ w_proj * jax.nn.silu(latent @ w_outgate)
        x = x + attn_out
        xn = rmsnorm(x, ffn_ln_w)
        ffn_out = jax.nn.silu(xn @ w1) * (xn @ w2) @ w3
        return x + ffn_out

    def _L0_ffn_ref(x, gate_w, gate_b, fc1_w, fc1_b, ln_w, ln_b, fc2_w, fc2_b):
        import jax, jax.numpy as jnp
        import numpy as np
        SEQ, BATCH, EMBED = (256, 2, 192)
        E = 16
        FFN_H = 384
        K_SHARED = 1
        K_ROUTE = 3
        LN_EPS = 1e-05
        NEG_INF = -1000000000.0
        S, B, D = x.shape
        T = S * B
        xf = x.reshape(T, D)
        scores = xf @ gate_w + gate_b
        scores = scores.at[:, :K_SHARED].set(NEG_INF)
        probs = jax.nn.softmax(scores, axis=-1)
        topv, topi = jax.lax.top_k(probs, K_ROUTE)
        combine = jnp.zeros((T, E), xf.dtype)
        combine = combine.at[jnp.arange(T)[:, None], topi].add(topv)
        combine = combine.at[:, :K_SHARED].add(1.0)
        h = jnp.einsum('td,edh->eth', xf, fc1_w) + fc1_b[:, None, :]
        h = jax.nn.gelu(h, approximate=False)
        mu = h.mean(-1, keepdims=True)
        var = h.var(-1, keepdims=True)
        h = (h - mu) * jax.lax.rsqrt(var + LN_EPS) * ln_w[:, None, :] + ln_b[:, None, :]
        y = jnp.einsum('eth,ehd->etd', h, fc2_w) + fc2_b[:, None, :]
        out = jnp.einsum('te,etd->td', combine, y)
        return out.reshape(S, B, D)
    h = _L0_tok_ref(x, mask_BS_i2_0, L0_tok_token_table, L0_tok_segm_table)
    h = h + _L0_attn_ref(_layernorm(h, axis=-1), L0_attn_ln_w, L0_attn_w_comp, L0_attn_w_qkv, L0_attn_w_reso, L0_attn_qn_w, L0_attn_kn_w, L0_attn_w_outgate, L0_attn_head_decay, L0_attn_temperature, L0_attn_w_proj, L0_attn_memn_w, L0_attn_ffn_ln_w, L0_attn_w1, L0_attn_w2, L0_attn_w3)
    h = h + _L0_ffn_ref(_layernorm(h, axis=-1), L0_ffn_gate_w, L0_ffn_gate_b, L0_ffn_fc1_w, L0_ffn_fc1_b, L0_ffn_ln_w, L0_ffn_ln_b, L0_ffn_fc2_w, L0_ffn_fc2_b)
    return h

_drawn_inputs = setup_inputs


def setup_inputs(seed=0):
    import zlib

    import numpy as np

    out = dict(_drawn_inputs(seed))
    spreads = {'L0_attn_ln_w': (1.0, 0.6),
     'L0_attn_qn_w': (1.0, 0.6),
     'L0_attn_kn_w': (1.0, 0.6),
     'L0_attn_memn_w': (1.0, 0.6),
     'L0_attn_ffn_ln_w': (1.0, 0.6),
     'L0_ffn_gate_b': (0.0, 2.0),
     'L0_ffn_fc1_b': (0.0, 0.434),
     'L0_ffn_ln_w': (1.0, 0.6),
     'L0_ffn_ln_b': (0.0, 2.0),
     'L0_ffn_fc2_b': (0.0, 0.724)}
    factors = {'L0_attn_w_comp': 8.0,
     'L0_attn_w_qkv': 8.0,
     'L0_attn_w_reso': 8.0,
     'L0_attn_w_outgate': 8.0,
     'L0_attn_head_decay': 8.0,
     'L0_attn_w_proj': 8.0,
     'L0_attn_w1': 4.903,
     'L0_attn_w2': 4.841,
     'L0_attn_w3': 4.978,
     'L0_ffn_gate_w': 8.0}
    for name, (base, spread) in spreads.items():
        noise = np.random.default_rng([zlib.crc32(name.encode()), seed]).standard_normal(out[name].shape)
        drawn = base * np.exp(spread * noise) if base else spread * noise
        out[name] = jnp.asarray(drawn.astype(out[name].dtype))
    for name, factor in factors.items():
        out[name] = (out[name] * factor).astype(out[name].dtype)
    return out
```

```python
from collections import namedtuple
from contextlib import ExitStack

import numpy as np

import concourse.bass as bass
from concourse import mybir

ALU = mybir.AluOpType
ACT = mybir.ActivationFunctionType
AX = mybir.AxisListType
F32 = mybir.dt.float32
I32 = mybir.dt.int32
U32 = mybir.dt.uint32

P = 128
NB, L, D = 4, 1024, 192
NT = NB * L // P
NG = L // P
G = NB
HD = D // 2
VOCAB, NSEG = 8000, 3
LAT, H, DH = 128, 12, 16
DV = DH + 1
HID = 512
E, FH = 16, 384
FK = FH // P
TOPK = 3
REGION = NB * L + P
SLOTS = TOPK * NB * L
RT = SLOTS // P + (E - 2)
PI = float(np.pi)
PRIME = 4


def done(i, n=1, k=0):
    return i * n + k + 1 + PRIME


def prev(i, n=1):
    return i * n + PRIME


def dma_done(i, n=1, k=0):
    return (i * n + k + 1) * 16 + PRIME


def named(kind, values):
    return namedtuple(kind, list(values))(*values.values())


def wait_alone(eng, sem, value):
    if not isinstance(value, int):
        value = eng.snap(eng.to_reg(value))
    eng.wait_ge(sem, PRIME)
    eng.wait_ge(sem, value)


def program(nc, x, seg, tok_table, seg_table, ln_w, w_comp, w_qkv, w_reso, qn_w, kn_w, w_outgate,
            head_decay, temperature, w_proj, memn_w, ffn_ln_w, w1, w2, w3, gate_w, gate_b, fc1_w,
            fc1_b, eln_w, eln_b, fc2_w, fc2_b, c_pos, c_rope, c_mats, c_rows, c_lpos, out):
    x_rows = nc.dram_tensor("x_rows", (E * REGION, D), F32).ap()
    y_rows = nc.dram_tensor("y_rows", ((NT + RT) * P, D), F32).ap()

    with ExitStack() as top:
        def sbuf(ctx, name, shape, dt=F32):
            return ctx.enter_context(nc.sbuf_tensor(name, shape, dt))

        in_use = []

        def sems(*names):
            made = named("Semaphores", {n: nc.alloc_semaphore(name=n) for n in names})
            in_use.extend(made)
            return made

        def release_sems():
            nc.clear_and_free_semaphores(in_use)
            nc.all_engine_barrier()
            in_use.clear()

        def prime(eng, *ss):
            for s in ss:
                eng.sem_inc(s, PRIME)

        bank = [top.enter_context(nc.psum_tensor(f"bank{k}", [P, 512], F32)) for k in range(8)]

        hbuf = sbuf(top, "hbuf", [P, NT, D])
        x1buf = sbuf(top, "x1buf", [P, NT, D])
        W1 = sbuf(top, "W1", [HD + 1, E, 2, FH])
        W2 = sbuf(top, "W2", [P, E, FK, D])
        B2 = sbuf(top, "B2", [E, D])
        mats = sbuf(top, "mats", [P, 4, P])
        ident, causal, strict, ones = (mats[:, k, :] for k in range(4))
        rows = sbuf(top, "rows", [P, 256])
        lpos = sbuf(top, "lpos", [P, NG + 1])
        neghalf = sbuf(top, "neghalf", [P, 96])
        fcol = sbuf(top, "fcol", [HD, 2])
        picked = sbuf(top, "picked", [P, NT, TOPK])
        place = sbuf(top, "place", [P, NT, TOPK])
        score3 = sbuf(top, "score3", [P, NT, TOPK])
        scores = sbuf(top, "scores", [P, NT, E])
        chosen = sbuf(top, "chosen", [P, E])
        y_row = sbuf(top, "y_row", [P, E])

        with ExitStack() as att:
            latT = sbuf(att, "latT", [P, NT * P])
            gates = sbuf(att, "gates", [P, NT, H])
            scale = sbuf(att, "scale", [P, NG, 2 * H])
            rope = sbuf(att, "rope", [P, 2, 2, NG, DH])
            wqkv = sbuf(att, "wqkv", [P, 3 * D])
            wog = sbuf(att, "wog", [P, D])
            wproj = sbuf(att, "wproj", [HD, 2, D])
            with ExitStack() as emb:
                params = sbuf(emb, "params", [P, NT, 4 * H])
                wcomp = sbuf(emb, "wcomp", [HD, 2, LAT])
                wreso = sbuf(emb, "wreso", [P, 4 * H])
                pos = sbuf(emb, "pos", [P, NG, D])
                temp = sbuf(emb, "temp", [P, 1])
                tok_id = sbuf(emb, "tok_id", [P, NG, NB], I32)
                seg_hot = sbuf(emb, "seg_hot", [P, NG, NB, NSEG])
                segw = sbuf(emb, "segw", [NB * NSEG, NB, D])
                setup(nc, sbuf, sems, bank, locals())
                embed(nc, sbuf, sems, prime, bank, locals())
                write_gates(nc, sbuf, sems, locals())
            attend(nc, sbuf, sems, prime, bank, locals())
        release_sems()
        ffn(nc, sbuf, sems, prime, bank, locals())
        experts(nc, sbuf, sems, prime, bank, locals())
        combine(nc, sbuf, sems, prime, bank, locals())
        release_sems()


def halves(w):
    return w.rearrange("(k d) n -> d k n", k=2)


def setup(nc, sbuf, sems, bank, v):
    v = named("Shared", v)
    with ExitStack() as ctx:
        cols = sbuf(ctx, "cols", [HD, 2, 2])
        qkn = sbuf(ctx, "qkn", [P, 2, DH])
        cs = sbuf(ctx, "cs", [P, 2, NG, DH])
        ln_rows = sbuf(ctx, "ln_rows", [E * FK, 2, P])
        lnT = sbuf(ctx, "lnT", [P, 2, E * FK])
        lnw, lnb = (lnT[:, k, :].rearrange("p (e k) -> p e k", k=FK) for k in range(2))
        col_rows = sbuf(ctx, "col_rows", [2 * 3, HD])
        id_rows = sbuf(ctx, "id_rows", [NT, 2, P], I32)
        idf = sbuf(ctx, "idf", [NT, 2, P])
        idg = sbuf(ctx, "idg", [NT, P])
        lnb_diag = sbuf(ctx, "lnb_diag", [P, E, FK, E])
        b2 = sbuf(ctx, "b2", [E, D])
        dec = sbuf(ctx, "dec", [P, 6, H])
        df = sbuf(ctx, "df", [P, NG, H])
        dfe = sbuf(ctx, "dfe", [P, NG, H])
        seg_id = sbuf(ctx, "seg_id", [P, NG, NB])
        s = sems("seg_clear", "ld_small", "ld_ids", "ld_ln", "ids_clean", "turned", "ld_w", "ld_fc1", "ld_fc2", "ld_const", "folded", "ids_ok",
                 "b2_sum", "b2_ok", "w2_scaled", "col_sum", "centred", "decay_in", "tanh_ok", "ln_ok",
                 "df_in", "df_ok", "chain", "bias_used")
        block = ctx.enter_context(nc.Block())

        @block.sync
        def _(sp):
            bc = lambda a, n: a.rearrange("(o n) -> o n", o=1).broadcast_to([P, n])
            for k, a in enumerate((v.x, v.seg)):
                sp.dma_start(id_rows[:, k, :], a.rearrange("b (c p) -> (b c) p", p=P)).then_inc(s.ld_ids, 16)
            sp.dma_start(v.mats[:], v.c_mats).then_inc(s.ld_const, 16)
            sp.dma_start(v.rows[:], v.c_rows.broadcast_to([P, 256])).then_inc(s.ld_const, 16)
            sp.dma_start(v.lpos[:], v.c_lpos).then_inc(s.ld_const, 16)
            sp.dma_start(v.pos[:], v.c_pos.rearrange("(c p) d -> p c d", p=P)).then_inc(s.ld_const, 16)
            for k in range(2):
                sp.dma_start(cs[:, k], v.c_rope[k].rearrange("(c p) d -> p c d", p=P)).then_inc(s.ld_const, 16)
            sp.dma_start(dec[:, 0, :], bc(v.head_decay, H)).then_inc(s.ld_small, 16)
            sp.dma_start(v.temp[:], bc(v.temperature, 1)).then_inc(s.ld_small, 16)
            for k, a in enumerate((v.qn_w, v.kn_w)):
                sp.dma_start(qkn[:, k, :], bc(a, DH)).then_inc(s.ld_small, 16)
            for k, a in enumerate((v.ln_w, v.memn_w, v.ffn_ln_w)):
                sp.dma_start(col_rows[2 * k:2 * k + 2, :], a.rearrange("(k d) -> k d", k=2)).then_inc(s.ld_small, 16)
            sp.dma_start(v.wcomp[:], halves(v.w_comp)).then_inc(s.ld_w, 16)
            sp.dma_start(v.wproj[:], halves(v.w_proj)).then_inc(s.ld_w, 16)
            sp.dma_start(v.wqkv[:], v.w_qkv).then_inc(s.ld_w, 16)
            sp.dma_start(v.wog[:], v.w_outgate).then_inc(s.ld_w, 16)
            sp.dma_start(v.wreso[:], v.w_reso).then_inc(s.ld_w, 16)
            sp.wait_ge(s.seg_clear, 1)
            for b in range(NB):
                sp.dma_start(v.segw[b * NSEG:(b + 1) * NSEG, b, :], v.seg_table).then_inc(s.ld_w, 16)
            sp.wait_ge(s.ld_w, 9 * 16)

        @block.scalar
        def _(act):
            for k, a in enumerate((v.eln_w, v.eln_b)):
                act.dma_start(ln_rows[:, k, :], a.rearrange("e (k p) -> (e k) p", p=P)).then_inc(s.ld_ln, 16)
            act.dma_start(v.W2[:], v.fc2_w.rearrange("e (k p) n -> p e k n", p=P)).then_inc(s.ld_fc2, 16)
            act.dma_start(b2[:], v.fc2_b).then_inc(s.ld_fc2, 16)
            for k in range(2):
                act.dma_start(v.W1[0:HD, :, k, :],
                              v.fc1_w[:, k * HD:(k + 1) * HD, :].rearrange("e d n -> d e n")).then_inc(s.ld_fc1, 16)
            act.dma_start(v.W1[HD:HD + 1, :, 0, :], v.fc1_b.rearrange("(o e) n -> o e n", o=1)).then_inc(s.ld_fc1, 16)
            act.wait_ge(s.ld_small, 7 * 16)
            act.activation(dec[:, 1, :], dec[:, 0, :], ACT.Tanh, scale=0.5).then_inc(s.tanh_ok, 1)
            act.wait_ge(s.decay_in, 1)
            act.activation(dec[:, 3, :], dec[:, 2, :], ACT.Ln).then_inc(s.ln_ok, 1)
            act.wait_ge(s.df_in, 1)
            act.activation(df[:], df[:], ACT.Exp).then_inc(s.df_ok, 1)
            act.wait_ge(s.ld_fc1, 3 * 16)

        @block.tensor
        def _(pe):
            pe.wait_ge(s.ld_const, 6 * 16)
            pe.wait_ge(s.ld_ln, 2 * 16)
            pe.wait_ge(s.ld_small, 7 * 16)
            n = E * FK
            for k in range(2):
                pe.transpose(bank[3][:, k * n:(k + 1) * n], ln_rows[:, k, :], v.ident[0:n, 0:n])
            pe.transpose(bank[3][0:HD, 2 * n:2 * n + 6], col_rows[:], v.ident[0:6, 0:6]).then_inc(s.turned, 1)
            pe.wait_ge(s.ids_clean, 1)
            for k in range(2):
                mm = pe.transpose(bank[4][:, k * NT:(k + 1) * NT], idf[:, k, :], v.ident[0:NT, 0:NT])
            mm.then_inc(s.turned, 1)
            pe.wait_ge(s.bias_used, 1)
            for e in range(E):
                for k in range(FK):
                    mm = pe.matmul(bank[0][0:E, 0:D], lnb_diag[:, e, k, :], v.W2[:, e, k, :],
                                   start=(e == 0 and k == 0), stop=(e == E - 1 and k == FK - 1))
            mm.then_inc(s.b2_sum, 1)
            for e in range(E):
                pe.wait_ge(s.w2_scaled, e + 1)
                if e >= 2:
                    pe.wait_ge(s.centred, e - 1)
                for k in range(FK):
                    mm = pe.matmul(bank[1 + e % 2][:, 0:D], v.ones, v.W2[:, e, k, :],
                                   start=(k == 0), stop=(k == FK - 1))
                mm.then_inc(s.col_sum, 1)

        @block.gpsimd
        def _(pool):
            pool.memset(v.segw[:], 0.0).then_inc(s.seg_clear, 1)
            pool.memset(v.neghalf[:], -0.5)
            pool.memset(v.chosen[:], 0.0)

        @block.vector
        def _(dve):
            n = [0]

            def link(ins):
                n[0] += 1
                ins.then_inc(s.chain, 1)
                dve.wait_ge(s.chain, n[0])

            dve.wait_ge(s.ld_ids, 2 * 16)
            for k, size in enumerate((VOCAB, NSEG)):
                link(dve.tensor_copy(idf[:, k], id_rows[:, k]))
                link(dve.tensor_scalar(idg[:], idf[:, k], 0.0, float(size), ALU.is_lt, ALU.mult))
                link(dve.tensor_tensor(idf[:, k], idf[:, k], idg[:], ALU.add))
                link(dve.tensor_scalar(idf[:, k], idf[:, k], 0.0, float(size - 1), ALU.max, ALU.min))
            dve.sem_inc(s.ids_clean, 1)
            dve.wait_ge(s.turned, 1)
            n2 = 2 * E * FK
            link(dve.tensor_copy(lnT[:].rearrange("p a n -> p (a n)"), bank[3][:, 0:n2]))
            link(dve.tensor_copy(cols[:].rearrange("d a k -> d (a k)"), bank[3][0:HD, n2:n2 + 4]))
            link(dve.tensor_copy(v.fcol[:], bank[3][0:HD, n2 + 4:n2 + 6]))
            dve.wait_ge(s.turned, 2)

            def by_group(k):
                return bank[4][:, k * NT:(k + 1) * NT].rearrange("p (b c) -> p c b", b=NB)
            link(dve.tensor_copy(v.tok_id[:], by_group(0)))
            link(dve.tensor_copy(seg_id[:], by_group(1)))
            for k in range(NSEG):
                link(dve.tensor_scalar(v.seg_hot[:, :, :, k], seg_id[:], float(k), None, ALU.is_equal))
            dve.wait_ge(s.tanh_ok, 1)
            link(dve.tensor_scalar(dec[:, 2, :], dec[:, 1, :], 0.325, 0.625, ALU.mult, ALU.add))
            link(dve.tensor_scalar(dec[:, 2, :], dec[:, 2, :], 1e-5, 0.999, ALU.max, ALU.min))
            dve.tensor_scalar(dec[:, 4, :], dec[:, 2, :], -1.0, 1.0, ALU.mult, ALU.add).then_inc(s.decay_in, 1)
            dve.wait_ge(s.ln_ok, 1)
            logd = dec[:, 3:4, :].broadcast_to([P, NG, H])
            lp = v.lpos[:, 0:NG].rearrange("p (c o) -> p c o", o=1).broadcast_to([P, NG, H])
            dve.tensor_tensor(df[:], logd, lp, ALU.mult).then_inc(s.df_in, 1)
            dve.wait_ge(s.df_ok, 1)
            dve.tensor_copy(v.scale[:, :, 0:H], df[:])
            link(dve.tensor_scalar(dfe[:], df[:], 1e-8, None, ALU.add))
            link(dve.reciprocal(dfe[:], dfe[:]))
            dt_b = dec[:, 4:5, :].broadcast_to([P, NG, H])
            link(dve.tensor_tensor(v.scale[:, :, H:], dfe[:], dt_b, ALU.mult))
            hf = DH // 2
            for k in range(2):
                for c in range(2):
                    link(dve.tensor_tensor(v.rope[:, k, c], cs[:, k],
                                           qkn[:, c:c + 1, :].broadcast_to([P, NG, DH]), ALU.mult))
            dve.wait_ge(s.ld_w, 9 * 16)
            for k in range(2):
                dve.tensor_scalar(v.wcomp[:, k], v.wcomp[:, k], cols[:, 0, k:k + 1], None, ALU.mult)
                dve.tensor_scalar(v.wproj[:, k], v.wproj[:, k], cols[:, 1, k:k + 1], 0.5, ALU.mult, ALU.mult)
            dve.wait_ge(s.ld_fc2, 2 * 16)
            eye = v.rows[:, 0:E]
            for e in range(E):
                for k in range(FK):
                    ins = dve.tensor_scalar(lnb_diag[:, e, k, :], eye, float(e), lnb[:, e, k:k + 1],
                                            ALU.is_equal, ALU.mult)
            ins.then_inc(s.bias_used, 1)
            dve.wait_ge(s.b2_sum, 1)
            dve.tensor_tensor(v.B2[:], bank[0][0:E, 0:D], b2[:], ALU.add).then_inc(s.b2_ok, 1)

            def centre(e):
                dve.wait_ge(s.col_sum, e + 1)
                total = bank[1 + e % 2][:, 0:D].rearrange("p (o n) -> p o n", o=1).broadcast_to([P, FK, D])
                dve.scalar_tensor_tensor(v.W2[:, e], total, -1.0 / FH, v.W2[:, e],
                                         ALU.mult, ALU.add).then_inc(s.centred, 1)

            for e in range(E):
                for k in range(FK):
                    ins = dve.tensor_scalar(v.W2[:, e, k, :], v.W2[:, e, k, :], lnw[:, e, k:k + 1], None, ALU.mult)
                ins.then_inc(s.w2_scaled, 1)
                if e:
                    centre(e - 1)
            centre(E - 1)
            dve.wait_ge(s.centred, E)


def embed(nc, sbuf, sems, prime, bank, v):
    v = named("Shared", v)
    with ExitStack() as ctx:
        tok = sbuf(ctx, "tok", [P, 2, G, D])
        NS = NB * NSEG
        hotS = sbuf(ctx, "hotS", [P, NS])
        hotT = sbuf(ctx, "hotT", [NS, P])
        stat = sbuf(ctx, "stat", [P, G, 6])
        mv = sbuf(ctx, "mv", [P, G, 2])
        va, rs, r2, m2, m2e, p2 = (sbuf(ctx, n, [P, G]) for n in ("va", "rs", "r2", "m2", "m2e", "p2"))
        xs = sbuf(ctx, "xs", [P, G, D])
        xT = sbuf(ctx, "xT", [HD, 2, G * P])
        latS = sbuf(ctx, "latS", [P, G * P])
        s = sems("tok0", "tok1", "seg_one", "seg_T", "seg_Ts", "seg_mm", "pos_add", "h_ok", "stats", "moments", "va_ok", "rs_ok",
                 "r2_ok", "m2_ok", "m2e_ok", "p2_ok", "x_ok", "xs_ok", "xT_mm", "xT_a", "xT_v", "lat_mm",
                 "lat_ok", "lat_kept", "par_mm", "par_ok")
        block = ctx.enter_context(nc.Block())
        own = dict(
            dve=(s.seg_one, s.pos_add, s.h_ok, s.stats, s.moments, s.x_ok, s.xT_v, s.par_ok),
            act=(s.seg_Ts, s.xs_ok, s.xT_a, s.lat_ok), pe=(s.seg_T, s.seg_mm, s.xT_mm, s.lat_mm, s.par_mm),
            pool=(s.va_ok, s.rs_ok, s.r2_ok, s.m2_ok, s.m2e_ok, s.p2_ok, s.lat_kept))

        @block.gpsimd
        def _(pool):
            prime(pool, *own["pool"])

            def gather(c, slot):
                for b in range(NB):
                    pool.indirect_dma_start(
                        tok[:, slot, b, :], None, v.tok_table,
                        bass.IndirectOffsetOnAxis(ap=v.tok_id[:, c, b:b + 1], axis=0)).then_inc(
                            (s.tok0, s.tok1)[slot], 16)

            def norm(i):
                var = mv[:, :, 1]
                wait_alone(pool, s.moments, done(i, G, G - 1))
                pool.wait_ge(s.xs_ok, prev(i, G))
                pool.tensor_scalar(va[:], var, 1e-5, None, ALU.add).then_inc(s.va_ok, 1)
                pool.wait_ge(s.va_ok, done(i))
                pool.tensor_tensor(rs[:], va[:], v.neghalf[:, 0:G], ALU.pow).then_inc(s.rs_ok, 1)
                pool.wait_ge(s.rs_ok, done(i))
                pool.tensor_tensor(r2[:], rs[:], rs[:], ALU.mult).then_inc(s.r2_ok, 1)
                pool.wait_ge(s.r2_ok, done(i))
                pool.tensor_tensor(m2[:], r2[:], var, ALU.mult).then_inc(s.m2_ok, 1)
                wait_alone(pool, s.m2_ok, done(i))
                pool.tensor_scalar(m2e[:], m2[:], 1e-6, None, ALU.add).then_inc(s.m2e_ok, 1)
                pool.wait_ge(s.m2e_ok, done(i))
                pool.tensor_tensor(p2[:], m2e[:], v.neghalf[:, 0:G], ALU.pow).then_inc(s.p2_ok, 1)

            def keep(i):
                pool.wait_ge(s.lat_ok, done(i))
                pool.tensor_copy(v.latT[:, bass.ds(i * (G * P), G * P)], latS[:]).then_inc(s.lat_kept, 1)

            gather(0, 0)
            gather(1, 1)
            for c in range(NG):
                norm(c)
                keep(c)
                if c + 2 < NG:
                    pool.wait_ge(s.h_ok, done(c, 2, 1))
                    gather(c + 2, c % 2)

        @block.vector
        def _(dve):
            prime(dve, *own["dve"])

            def group(i, slot, turn):
                dve.wait_ge(s.seg_T, prev(i))
                dve.tensor_copy(hotS[:], v.seg_hot[:, bass.ds(i, 1), :, :].rearrange("p o b k -> p (o b k)")
                                ).then_inc(s.seg_one, 1)
                dve.wait_ge((s.tok0, s.tok1)[slot], (turn + 1) * (NB * 16))
                t = tok[:, slot]
                dve.tensor_tensor(t, t, v.pos[:, bass.ds(i, 1), :].broadcast_to([P, G, D]),
                                  ALU.add).then_inc(s.pos_add, 1)
                dve.wait_ge(s.pos_add, done(i))
                dve.wait_ge(s.seg_mm, done(i))
                for k in range(2):
                    dve.tensor_tensor(v.hbuf[:, bass.ds(i * G + 2 * k, 2), :], t[:, 2 * k:2 * k + 2, :],
                                      bank[k][:, 0:2 * D].rearrange("p (b d) -> p b d", b=2),
                                      ALU.add).then_inc(s.h_ok, 1)
                wait_alone(dve, s.h_ok, done(i, 2, 1))
                h = [v.hbuf[:, bass.ds(i * G + b, 1), :].rearrange("p o d -> p (o d)") for b in range(G)]
                for b in range(G):
                    dve.bn_stats(stat[:, b, :], h[b]).then_inc(s.stats, 1)
                for b in range(G):
                    wait_alone(dve, s.stats, done(i, G, b))
                    dve.bn_aggr(mv[:, b, :], stat[:, b, :]).then_inc(s.moments, 1)
                dve.wait_ge(s.rs_ok, done(i))
                for b in range(G):
                    dve.tensor_scalar(v.x1buf[:, bass.ds(i * G + b, 1), :].rearrange("p o d -> p (o d)"), h[b],
                                      mv[:, b, 0:1], rs[:, b:b + 1], ALU.subtract, ALU.mult).then_inc(s.x_ok, 1)
                dve.wait_ge(s.xT_mm, done(i))
                dve.tensor_copy(xT[:, 1, :], bank[3][0:HD, :]).then_inc(s.xT_v, 1)
                dve.wait_ge(s.par_mm, done(i))
                dve.tensor_copy(v.params[:, bass.ds(i * G, G), :],
                                bank[5][:, 0:G * 4 * H].rearrange("p (b n) -> p b n", b=G)).then_inc(s.par_ok, 1)

            with dve.Fori(0, NG // 2, 1) as j:
                group(j * 2, 0, j)
                group(j * 2 + 1, 1, j)

        @block.scalar
        def _(act):
            prime(act, *own["act"])
            with act.Fori(0, NG, 1) as i:
                act.wait_ge(s.seg_T, done(i))
                act.wait_ge(s.seg_mm, prev(i))
                act.activation(hotT[:], bank[6][0:NS, 0:P], ACT.Copy).then_inc(s.seg_Ts, 1)
                act.wait_ge(s.p2_ok, done(i))
                act.wait_ge(s.xT_mm, prev(i))
                for b in range(G):
                    act.wait_ge(s.x_ok, done(i, G, b))
                    act.activation(xs[:, b, :], v.x1buf[:, bass.ds(i * G + b, 1), :].rearrange("p o d -> p (o d)"),
                                   ACT.Copy, scale=p2[:, b:b + 1]).then_inc(s.xs_ok, 1)
                act.wait_ge(s.xT_mm, done(i))
                act.activation(xT[:, 0, :], bank[2][0:HD, :], ACT.Copy).then_inc(s.xT_a, 1)
                act.wait_ge(s.lat_mm, done(i))
                act.wait_ge(s.lat_kept, prev(i))
                act.wait_ge(s.par_mm, prev(i))
                act.activation(latS[:], bank[4][:], ACT.Silu).then_inc(s.lat_ok, 1)

        @block.tensor
        def _(pe):
            prime(pe, *own["pe"])
            with pe.Fori(0, NG, 1) as i:
                pe.wait_ge(s.seg_one, done(i))
                pe.wait_ge(s.seg_Ts, prev(i))
                pe.transpose(bank[6][0:NS, 0:P], hotS[:], v.ident).then_inc(s.seg_T, 1)
                pe.wait_ge(s.seg_Ts, done(i))
                pe.wait_ge(s.h_ok, prev(i, 2))
                for k in range(2):
                    mm = pe.matmul(bank[k][:, 0:2 * D], hotT[:],
                                   v.segw[:, 2 * k:2 * k + 2, :].rearrange("s b d -> s (b d)"), start=True, stop=True)
                mm.then_inc(s.seg_mm, 1)
                pe.wait_ge(s.xT_a, prev(i))
                pe.wait_ge(s.xT_v, prev(i))
                for b in range(G):
                    pe.wait_ge(s.xs_ok, done(i, G, b))
                    for k in range(2):
                        mm = pe.transpose(bank[2 + k][0:HD, b * P:(b + 1) * P], xs[:, b, k * HD:(k + 1) * HD], v.ident)
                mm.then_inc(s.xT_mm, 1)
                pe.wait_ge(s.xT_a, done(i))
                pe.wait_ge(s.xT_v, done(i))
                pe.wait_ge(s.lat_ok, prev(i))
                for k in range(2):
                    mm = pe.matmul(bank[4][:], v.wcomp[:, k, :], xT[:, k, :], start=(k == 0), stop=(k == 1))
                mm.then_inc(s.lat_mm, 1)
                pe.wait_ge(s.lat_ok, done(i))
                pe.wait_ge(s.par_ok, prev(i))
                for b in range(G):
                    mm = pe.matmul(bank[5][:, b * 4 * H:(b + 1) * 4 * H], latS[:, b * P:(b + 1) * P], v.wreso[:],
                                   start=True, stop=True)
                mm.then_inc(s.par_mm, 1)


def write_gates(nc, sbuf, sems, v):
    v = named("Shared", v)
    n = NT * H
    with ExitStack() as ctx:
        th = sbuf(ctx, "th", [P, NT * H, 4])
        ph = sbuf(ctx, "ph", [P, n])
        amp = sbuf(ctx, "amp", [P, n])
        s = sems("g_tanh", "g_phase", "g_sin", "g_cos", "g_chain", "g_prod", "g_sig", "g_ok")
        block = ctx.enter_context(nc.Block())

        @block.scalar
        def _(act):
            act.activation(th[:].rearrange("p n k -> p (n k)"), v.params[:].rearrange("p t n -> p (t n)"),
                           ACT.Tanh, scale=0.5).then_inc(s.g_tanh, 1)
            act.wait_ge(s.g_phase, 1)
            act.activation(ph[:], ph[:], ACT.Sin, scale=PI / 4).then_inc(s.g_sin, 1)
            act.wait_ge(s.g_prod, 1)
            act.activation(amp[:], amp[:], ACT.Tanh, scale=v.temp[:, 0:1]).then_inc(s.g_sig, 1)

        @block.vector
        def _(dve):
            dve.wait_ge(s.g_tanh, 1)
            dve.tensor_tensor(ph[:], th[:, :, 1], th[:, :, 3], ALU.subtract).then_inc(s.g_phase, 1)
            dve.tensor_scalar(amp[:], th[:, :, 2], 1.0, None, ALU.add).then_inc(s.g_chain, 1)
            dve.wait_ge(s.g_chain, 1)
            dve.scalar_tensor_tensor(amp[:], th[:, :, 0], 1.0, amp[:], ALU.add, ALU.mult).then_inc(s.g_chain, 1)
            dve.wait_ge(s.g_sin, 1)
            dve.tensor_tensor(ph[:], ph[:], ph[:], ALU.mult).then_inc(s.g_cos, 1)
            dve.wait_ge(s.g_cos, 1)
            dve.tensor_scalar(ph[:], ph[:], -0.25, 0.125, ALU.mult, ALU.add).then_inc(s.g_cos, 1)
            dve.wait_ge(s.g_cos, 2)
            dve.wait_ge(s.g_chain, 2)
            dve.tensor_tensor(amp[:], amp[:], ph[:], ALU.mult).then_inc(s.g_prod, 1)
            dve.wait_ge(s.g_sig, 1)
            dve.tensor_scalar(amp[:], amp[:], 0.6, 0.5, ALU.mult, ALU.add).then_inc(s.g_chain, 1)
            dve.wait_ge(s.g_chain, 3)
            dve.tensor_scalar(v.gates[:].rearrange("p t h -> p (t h)"), amp[:], 0.05, 0.95,
                              ALU.max, ALU.min).then_inc(s.g_ok, 1)
            dve.wait_ge(s.g_ok, 1)


def attend(nc, sbuf, sems, prime, bank, v):
    v = named("Shared", v)
    NQ = 2 * H
    HB = H // 4
    hf = DH // 2
    with ExitStack() as ctx:
        latA = sbuf(ctx, "latA", [P, G * P])
        ssum = sbuf(ctx, "ssum", [P, NQ])
        ms = sbuf(ctx, "ms", [P, NQ])
        rn = sbuf(ctx, "rn", [P, NQ])
        qn = sbuf(ctx, "qn", [P, 2, H, DH])
        t1 = sbuf(ctx, "t1", [P, 2, H, DH])
        rot = sbuf(ctx, "rot", [P, NQ, DH])
        neg = sbuf(ctx, "neg", [P, NQ * DH])
        sq = neg
        fpad = sbuf(ctx, "fpad", [P, 2, NQ, 2 * DH])
        vaug = sbuf(ctx, "vaug", [P, 2, H, DV])
        og = sbuf(ctx, "og", [P, 2, D])
        qkT = sbuf(ctx, "qkT", [P, 2, HB * P])
        att = sbuf(ctx, "att", [P, 4, HB * P])
        state = sbuf(ctx, "state", [P, NB, HB * 4 * DV])
        stmp = sbuf(ctx, "stmp", [P, HB * 4 * DV])
        bd = sbuf(ctx, "bd", [P, HB, 4, DV])
        den = sbuf(ctx, "den", [P, H])
        rden = sbuf(ctx, "rden", [P, H])
        on = sbuf(ctx, "on", [P, D])
        osq = sbuf(ctx, "osq", [P, D])
        oss = sbuf(ctx, "oss", [P, 1])
        oms = sbuf(ctx, "oms", [P, 1])
        orn = sbuf(ctx, "orn", [P, 1])
        oT = sbuf(ctx, "oT", [HD, 2 * P])
        upd = sbuf(ctx, "upd", [P, D])
        s = sems("a_zero", "a_lat", "a_qk", "a_vo", "a_sq", "a_sum", "a_ms", "a_rn", "a_qn", "a_t1", "a_t2",
                 "a_rot", "a_neg", "a_exp", "a_f", "a_fp", "a_vaug", "a_tanh", "a_og", "a_T", "a_qT", "a_kT",
                 "a_s", "a_mask", "a_supd", "a_stmp", "a_state", "a_o", "a_den", "a_rden", "a_on", "a_osq",
                 "a_oms", "a_orn", "a_oT", "a_oTs", "a_proj", "a_upd", "a_x1")
        own = dict(
            dve=(s.a_lat, s.a_sum, s.a_qn, s.a_t1, s.a_t2, s.a_rot, s.a_neg, s.a_f, s.a_fp, s.a_vaug, s.a_og,
                 s.a_qT, s.a_mask, s.a_stmp, s.a_state, s.a_den, s.a_rden, s.a_on, s.a_oTs, s.a_upd),
            act=(s.a_sq, s.a_exp, s.a_tanh, s.a_kT, s.a_osq),
            pe=(s.a_qk, s.a_vo, s.a_T, s.a_s, s.a_supd, s.a_o, s.a_oT, s.a_proj),
            pool=(s.a_ms, s.a_rn, s.a_oms, s.a_orn, s.a_x1))
        QK, VO, TQ, TK, S0, S1, OB, RB = bank
        block = ctx.enter_context(nc.Block())

        @block.gpsimd
        def _(pool):
            prime(pool, *own["pool"])
            pool.memset(fpad[:], 0.0).then_inc(s.a_zero, 1)
            pool.memset(state[:], 0.0).then_inc(s.a_zero, 1)
            pool.memset(bd[:], 1.0).then_inc(s.a_zero, 1)
            pool.wait_ge(s.a_zero, 3)
            pool.affine_select(out=bd[:], in_=bd[:], compare_op=ALU.is_ge, fill=0.0, base=0,
                               pattern=[[0, HB], [-2 * DH, 4], [0, DV]], channel_multiplier=1).then_inc(s.a_zero, 1)
            pool.wait_ge(s.a_zero, 4)
            pool.affine_select(out=bd[:], in_=bd[:], compare_op=ALU.is_ge, fill=0.0, base=DH - 1,
                               pattern=[[0, HB], [2 * DH, 4], [0, DV]], channel_multiplier=-1).then_inc(s.a_zero, 1)

            def head_norm(i, b):
                wait_alone(pool, s.a_sum, done(i, NB, b))
                pool.tensor_scalar(ms[:], ssum[:], 1.0 / DH, 1e-6, ALU.mult, ALU.add).then_inc(s.a_ms, 1)
                pool.wait_ge(s.a_ms, done(i, NB, b))
                pool.wait_ge(s.a_qn, done(i, NB, b - 1))
                pool.tensor_tensor(rn[:], ms[:], v.neghalf[:, 0:NQ], ALU.pow).then_inc(s.a_rn, 1)

            with pool.Fori(0, NG, 1) as i:
                head_norm(i, 0)
                for b in range(NB):
                    if b + 1 < NB:
                        head_norm(i, b + 1)
                    wait_alone(pool, s.a_osq, done(i, NB, b))
                    pool.tensor_scalar(oms[:], oss[:], 1.0 / D, 1e-6, ALU.mult, ALU.add).then_inc(s.a_oms, 1)
                    pool.wait_ge(s.a_oms, done(i, NB, b))
                    pool.wait_ge(s.a_upd, done(i, NB, b - 1))
                    pool.tensor_tensor(orn[:], oms[:], v.neghalf[:, 0:1], ALU.pow).then_inc(s.a_orn, 1)
                    pool.wait_ge(s.a_upd, done(i, NB, b))
                    xr = v.x1buf[:, bass.ds(i * NB + b, 1), :].rearrange("p o d -> p (o d)")
                    pool.tensor_tensor(xr, xr, upd[:], ALU.add).then_inc(s.a_x1, 1)

        @block.scalar
        def _(act):
            prime(act, *own["act"])

            def front(i, b):
                act.wait_ge(s.a_qk, done(i, NB, b))
                act.wait_ge(s.a_f, done(i, NB, b - 1))
                act.activation(sq[:], QK[:, 0:2 * D], ACT.Square).then_inc(s.a_sq, 1)
                act.wait_ge(s.a_neg, done(i, NB, b))
                act.activation(neg[:], neg[:], ACT.Exp).then_inc(s.a_exp, 1)
                act.wait_ge(s.a_vaug, done(i, NB, b))
                act.wait_ge(s.a_upd, done(i, NB, b - 2))
                act.activation(og[:, b % 2], VO[:, D:2 * D], ACT.Tanh, scale=0.5).then_inc(s.a_tanh, 1)

            with act.Fori(0, NG, 1) as i:
                front(i, 0)
                for b in range(NB):
                    act.wait_ge(s.a_T, done(i, NB, b))
                    act.wait_ge(s.a_o, done(i, NB, b - 1))
                    act.activation(qkT[:, 1, :], TK[:, 0:HB * P], ACT.Copy).then_inc(s.a_kT, 1)
                    if b + 1 < NB:
                        front(i, b + 1)
                    act.wait_ge(s.a_on, done(i, NB, b))
                    act.wait_ge(s.a_oms, done(i, NB, b - 1))
                    act.activation(osq[:], on[:], ACT.Square, accum_out=oss[:]).then_inc(s.a_osq, 1)

        @block.tensor
        def _(pe):
            prime(pe, *own["pe"])

            def project(i, b):
                lat = latA[:, b * P:(b + 1) * P]
                pe.wait_ge(s.a_qn, done(i, NB, b - 1))
                pe.matmul(QK[:, 0:2 * D], lat, v.wqkv[:, 0:2 * D], start=True, stop=True).then_inc(s.a_qk, 1)
                pe.wait_ge(s.a_vaug, done(i, NB, b - 1))
                pe.wait_ge(s.a_og, done(i, NB, b - 1))
                pe.matmul(VO[:, 0:D], lat, v.wqkv[:, 2 * D:3 * D], start=True, stop=True)
                pe.matmul(VO[:, D:2 * D], lat, v.wog[:], start=True, stop=True).then_inc(s.a_vo, 1)

            def head_scores(i, b, half):
                pe.wait_ge(s.a_mask, done(i, 4 * NB, 4 * b + 2 * half - 1))
                for g in range(HB):
                    for jj in range(2):
                        j = 2 * half + jj
                        r = slice(32 * j, 32 * j + DH)
                        mm = pe.matmul((S0, S1)[jj][:, g * P:(g + 1) * P], qkT[r, 1, g * P:(g + 1) * P],
                                       qkT[r, 0, g * P:(g + 1) * P], start=True, stop=True)
                mm.then_inc(s.a_s, 1)

            def tail(i, b):
                pe.wait_ge(s.a_on, done(i, NB, b))
                pe.wait_ge(s.a_upd, done(i, NB, b - 1))
                for k in range(2):
                    mm = pe.transpose(RB[0:HD, k * P:(k + 1) * P], on[:, k * HD:(k + 1) * HD], v.ident)
                mm.then_inc(s.a_oT, 1)
                pe.wait_ge(s.a_oTs, done(i, NB, b))
                for k in range(2):
                    mm = pe.matmul(RB[:, 2 * P:2 * P + D], oT[:, k * P:(k + 1) * P], v.wproj[:, k, :],
                                   start=(k == 0), stop=(k == 1))
                mm.then_inc(s.a_proj, 1)

            with pe.Fori(0, NG, 1) as i:
                pe.wait_ge(s.a_lat, done(i))
                project(i, 0)
                for b in range(NB):
                    pe.wait_ge(s.a_fp, done(i, NB, b))
                    pe.wait_ge(s.a_qT, done(i, NB, b - 1))
                    pe.wait_ge(s.a_kT, done(i, NB, b - 1))
                    for k, t in enumerate((TQ, TK)):
                        for g in range(HB):
                            blk = fpad[:, b % 2, k * H + 4 * g:k * H + 4 * g + 4, :].rearrange("p h d -> p (h d)")
                            mm = pe.transpose(t[:, g * P:(g + 1) * P], blk, v.ident)
                    mm.then_inc(s.a_T, 1)
                    if b + 1 < NB:
                        project(i, b + 1)
                    pe.wait_ge(s.a_qT, done(i, NB, b))
                    pe.wait_ge(s.a_kT, done(i, NB, b))
                    head_scores(i, b, 0)
                    pe.wait_ge(s.a_vaug, done(i, NB, b))
                    pe.wait_ge(s.a_stmp, done(i, NB, b - 1))
                    pe.wait_ge(s.a_on, done(i, NB, b - 1))
                    for g in range(HB):
                        blk = fpad[:, b % 2, H + 4 * g:H + 4 * g + 4, :].rearrange("p h d -> p (h d)")
                        mm = pe.matmul(OB[:, 256 + g * 4 * DV:256 + (g + 1) * 4 * DV], blk,
                                       vaug[:, b % 2, 4 * g:4 * g + 4, :].rearrange("p h d -> p (h d)"),
                                       start=True, stop=True)
                    mm.then_inc(s.a_supd, 1)
                    head_scores(i, b, 1)
                    pe.wait_ge(s.a_state, done(i, NB, b - NB))
                    pe.wait_ge(s.a_stmp, done(i, NB, b))
                    for g in range(HB):
                        pe.matmul(OB[:, g * 4 * DV:(g + 1) * 4 * DV], qkT[:, 0, g * P:(g + 1) * P],
                                  state[:, b, g * 4 * DV:(g + 1) * 4 * DV],
                                  start=(g == 0), stop=False, skip_group_check=True)
                    pe.wait_ge(s.a_mask, done(i, 4 * NB, 4 * b + 3))
                    for h in range(H):
                        g, j = h // 4, h % 4
                        mm = pe.matmul(OB[:, h * DV:(h + 1) * DV], att[:, j, g * P:(g + 1) * P],
                                       vaug[:, b % 2, h, :], start=False, stop=(h == H - 1), skip_group_check=True)
                    mm.then_inc(s.a_o, 1)
                    tail(i, b)

        @block.vector
        def _(dve):
            prime(dve, *own["dve"])
            dve.wait_ge(s.a_zero, 5)
            dve.memset(vaug[:], 1.0)

            def front(i, b):
                dve.wait_ge(s.a_sq, done(i, NB, b))
                dve.wait_ge(s.a_ms, done(i, NB, b - 1))
                dve.tensor_reduce(ssum[:], sq[:].rearrange("p (h d) -> p h d", d=DH), AX.X, ALU.add).then_inc(s.a_sum, 1)
                dve.wait_ge(s.a_vo, done(i, NB, b))
                dve.wait_ge(s.a_o, done(i, NB, b - 2))
                dve.tensor_tensor(vaug[:, b % 2, :, 0:DH], VO[:, 0:D].rearrange("p (h d) -> p h d", d=DH),
                                  v.gates[:, bass.ds(i * NB + b, 1), :].rearrange("p o (h u) -> p (o h) u", u=1)
                                  .broadcast_to([P, H, DH]), ALU.mult).then_inc(s.a_vaug, 1)
                dve.wait_ge(s.a_rn, done(i, NB, b))
                qk = QK[:, 0:2 * D].rearrange("p (h d) -> p h d", d=DH)
                dve.tensor_tensor(qn[:].rearrange("p a h d -> p (a h) d"), qk,
                                  rn[:].rearrange("p (h u) -> p h u", u=1).broadcast_to([P, NQ, DH]),
                                  ALU.mult).then_inc(s.a_qn, 1)
                dve.wait_ge(s.a_qn, done(i, NB, b))

                def table(k):
                    return v.rope[:, k, :, bass.ds(i, 1), :].broadcast_to([P, 2, H, DH])
                dve.tensor_tensor(t1[:], qn[:], table(0), ALU.mult).then_inc(s.a_t1, 1)
                dve.tensor_tensor(qn[:], qn[:], table(1), ALU.mult).then_inc(s.a_t2, 1)
                dve.wait_ge(s.a_t1, done(i, NB, b))
                dve.wait_ge(s.a_t2, done(i, NB, b))
                a = t1[:].rearrange("p a h d -> p (a h) d")
                c = qn[:].rearrange("p a h d -> p (a h) d")
                dve.tensor_tensor(rot[:, :, 0:hf], a[:, :, 0:hf], c[:, :, hf:], ALU.add).then_inc(s.a_rot, 1)
                dve.tensor_tensor(rot[:, :, hf:], a[:, :, hf:], c[:, :, 0:hf], ALU.add).then_inc(s.a_rot, 1)
                dve.wait_ge(s.a_rot, done(i, 2 * NB, 2 * b + 1))
                rflat = rot[:].rearrange("p h d -> p (h d)")
                dve.tensor_scalar(neg[:], rflat, 0.0, None, ALU.min).then_inc(s.a_neg, 1)
                dve.wait_ge(s.a_exp, done(i, NB, b))
                dve.scalar_tensor_tensor(rflat, rflat, 0.0, neg[:], ALU.max, ALU.add).then_inc(s.a_f, 1)
                dve.wait_ge(s.a_f, done(i, NB, b))
                dve.wait_ge(s.a_supd, done(i, NB, b - 2))
                dve.tensor_tensor(fpad[:, b % 2, :, 0:DH], rot[:],
                                  v.scale[:, bass.ds(i, 1), :].rearrange("p o (h u) -> p (o h) u", u=1)
                                  .broadcast_to([P, NQ, DH]), ALU.mult).then_inc(s.a_fp, 1)
                dve.wait_ge(s.a_tanh, done(i, NB, b))
                dve.scalar_tensor_tensor(og[:, b % 2], og[:, b % 2], 1.0, VO[:, D:2 * D],
                                         ALU.add, ALU.mult).then_inc(s.a_og, 1)

            def mask(i, b, half):
                dve.wait_ge(s.a_s, done(i, 2 * NB, 2 * b + half))
                if half == 0:
                    dve.wait_ge(s.a_o, done(i, NB, b - 1))
                for jj in range(2):
                    dve.tensor_tensor(att[:, 2 * half + jj, :].rearrange("p (g n) -> p g n", g=HB),
                                      (S0, S1)[jj][:, 0:HB * P].rearrange("p (g n) -> p g n", g=HB),
                                      v.causal.rearrange("p (o n) -> p o n", o=1).broadcast_to([P, HB, P]),
                                      ALU.mult).then_inc(s.a_mask, 1)

            with dve.Fori(0, NG, 1) as i:
                dve.wait_ge(s.a_vo, prev(i, NB))
                dve.tensor_copy(latA[:], v.latT[:, bass.ds(i * (G * P), G * P)]).then_inc(s.a_lat, 1)
                front(i, 0)
                for b in range(NB):
                    dve.wait_ge(s.a_T, done(i, NB, b))
                    dve.wait_ge(s.a_o, done(i, NB, b - 1))
                    dve.tensor_copy(qkT[:, 0, :], TQ[:, 0:HB * P]).then_inc(s.a_qT, 1)
                    mask(i, b, 0)
                    dve.wait_ge(s.a_supd, done(i, NB, b))
                    dve.tensor_tensor(stmp[:], OB[:, 256:256 + HB * 4 * DV], bd[:].rearrange("p g j d -> p (g j d)"),
                                      ALU.mult).then_inc(s.a_stmp, 1)
                    mask(i, b, 1)
                    if b + 1 < NB:
                        front(i, b + 1)
                    dve.wait_ge(s.a_o, done(i, NB, b))
                    num = OB[:, 0:H * DV].rearrange("p (h d) -> p h d", d=DV)
                    dve.tensor_scalar(den[:], num[:, :, DH], 1e-5, None, ALU.max).then_inc(s.a_den, 1)
                    dve.tensor_tensor(state[:, b, :], state[:, b, :], stmp[:], ALU.add).then_inc(s.a_state, 1)
                    dve.wait_ge(s.a_den, done(i, NB, b))
                    dve.reciprocal(rden[:], den[:]).then_inc(s.a_rden, 1)
                    dve.wait_ge(s.a_rden, done(i, NB, b))
                    dve.wait_ge(s.a_oT, done(i, NB, b - 1))
                    dve.wait_ge(s.a_osq, done(i, NB, b - 1))
                    dve.tensor_tensor(on[:].rearrange("p (h d) -> p h d", d=DH), num[:, :, 0:DH],
                                      rden[:].rearrange("p (h u) -> p h u", u=1).broadcast_to([P, H, DH]),
                                      ALU.mult).then_inc(s.a_on, 1)
                    dve.wait_ge(s.a_oT, done(i, NB, b))
                    dve.wait_ge(s.a_proj, done(i, NB, b - 1))
                    dve.tensor_copy(oT[:], RB[0:HD, 0:2 * P]).then_inc(s.a_oTs, 1)
                    dve.wait_ge(s.a_proj, done(i, NB, b))
                    dve.wait_ge(s.a_orn, done(i, NB, b))
                    dve.wait_ge(s.a_x1, done(i, NB, b - 1))
                    dve.scalar_tensor_tensor(upd[:], RB[:, 2 * P:2 * P + D], orn[:, 0:1], og[:, b % 2],
                                             ALU.mult, ALU.mult).then_inc(s.a_upd, 1)


def ffn(nc, sbuf, sems, prime, bank, v):
    v = named("Shared", v)
    NH = HID // P
    with ExitStack() as ctx:
        fsq = sbuf(ctx, "fsq", [P, D])
        ss = sbuf(ctx, "ss", [P, G])
        fms = sbuf(ctx, "fms", [P, G])
        frn = sbuf(ctx, "frn", [P, G])
        xn = sbuf(ctx, "xn", [P, G, D])
        xnT = sbuf(ctx, "xnT", [HD, 2, G * P])
        act_a = sbuf(ctx, "act_a", [P, 2, G * P])
        u = sbuf(ctx, "u", [P, NH, G * P])
        stat = sbuf(ctx, "fstat", [P, G, 6])
        mv = sbuf(ctx, "fmv", [P, G, 2])
        va = sbuf(ctx, "fva", [P, G])
        rs = sbuf(ctx, "frs", [P, G])
        xf = sbuf(ctx, "xf", [P, 2, G, D])
        xfT = sbuf(ctx, "xfT", [HD + 1, 2, G * P])
        top8 = sbuf(ctx, "top8", [P, G, 8])
        idx8 = sbuf(ctx, "idx8", [P, G, 8], U32)
        sc = sbuf(ctx, "sc", [P, G, E])
        hot = sbuf(ctx, "hot", [P, G, TOPK, E])
        hot_s = sbuf(ctx, "hot_s", [P, G, TOPK, E])
        mask = sbuf(ctx, "mask", [P, G, E])
        before = sbuf(ctx, "before", [P, G, E])
        region = sbuf(ctx, "region", [P, E])
        spare = sbuf(ctx, "spare", [2, E])
        rank = sbuf(ctx, "rank", [P, G, E])
        slot_f = sbuf(ctx, "slot_f", [P, G, TOPK])
        slot_i = sbuf(ctx, "slot_i", [P, 2, G, TOPK], I32)
        s = sems("ld_f", "f_fold", "f_const", "f_sq", "f_ms", "f_rn", "f_xn", "f_xT", "f_xTa", "f_xTv", "f_ab", "f_silu", "f_u",
                 "f_w3", "f_hx", "f_h", "f_stat", "f_mv", "f_va", "f_rs", "f_xf", "f_fT", "f_fTa", "f_fTv",
                 "f_gate", "f_score", "f_top", "f_idx", "f_pick", "f_hot", "f_m1", "f_mask", "f_run", "f_rank",
                 "f_place", "f_hs", "f_slot", "f_keep", "f_int", "f_store0", "f_store1", "f_send0", "f_send1")
        own = dict(
            dve=(s.f_xn, s.f_xTv, s.f_u, s.f_h, s.f_stat, s.f_mv, s.f_xf, s.f_fTv, s.f_score, s.f_top, s.f_idx,
                 s.f_pick, s.f_hot, s.f_m1, s.f_mask, s.f_run, s.f_place, s.f_hs, s.f_slot, s.f_keep, s.f_int),
            act=(s.f_sq, s.f_xTa, s.f_silu, s.f_fTa), pe=(s.f_xT, s.f_ab, s.f_w3, s.f_fT, s.f_gate, s.f_rank),
            pool=(s.f_ms, s.f_rn, s.f_hx, s.f_va, s.f_rs), sp=(s.f_store0, s.f_store1))
        XA, XB, A0, B0, A1, B1, Y0, Y1 = bank
        w12 = sbuf(ctx, "w12", [HD, 2, 2 * HID])
        w3s = sbuf(ctx, "w3s", [P, HID // P, D])
        gw = sbuf(ctx, "gw", [HD + 1, 2, E])
        block = ctx.enter_context(nc.Block())

        def row(t, k):
            return t[:, bass.ds(k, 1), :].rearrange("p o d -> p (o d)")

        @block.sync
        def _(sp):
            sp.dma_start(w12[:, :, 0:HID], halves(v.w1)).then_inc(s.ld_f, 16)
            sp.dma_start(w12[:, :, HID:], halves(v.w2)).then_inc(s.ld_f, 16)
            sp.dma_start(w3s[:], v.w3.rearrange("(k p) n -> p k n", p=P)).then_inc(s.ld_f, 16)
            sp.dma_start(gw[0:HD], halves(v.gate_w)).then_inc(s.ld_f, 16)
            sp.dma_start(gw[HD:HD + 1, 0, :], v.gate_b.rearrange("(o n) -> o n", o=1)).then_inc(s.ld_f, 16)
            prime(sp, *own["sp"])
            with sp.Fori(0, NG // 2, 1) as j:
                for half in range(2):
                    i = j * 2 + half
                    store = (s.f_store0, s.f_store1)[half]
                    sp.wait_ge(s.f_xf, done(i, G, G - 1))
                    sp.dma_start(v.x_rows[bass.ds(i * (G * P), G * P), :].rearrange("(b p) d -> p b d", p=P),
                                 xf[:, half]).then_inc(store, 16)
            sp.wait_ge(s.f_store0, dma_done(NG // 2 - 1))
            sp.wait_ge(s.f_store1, dma_done(NG // 2 - 1))

        @block.gpsimd
        def _(pool):
            prime(pool, *own["pool"])
            NS = G * TOPK
            for k, send in enumerate((s.f_send0, s.f_send1)):
                pool.dma_start(spare[k:k + 1, :], v.c_rows[:, 0:E]).then_inc(send, 16)

            def send(i, half):
                wait_alone(pool, s.f_int, done(i))
                for b in range(G):
                    for k in range(TOPK):
                        pool.indirect_dma_start(
                            v.x_rows, bass.IndirectOffsetOnAxis(ap=slot_i[:, half, b, k:k + 1], axis=0),
                            xf[:, half, b, :], None).then_inc((s.f_send0, s.f_send1)[half], 16)

            with pool.Fori(0, NG // 2, 1) as j:
                for half in range(2):
                    i = j * 2 + half
                    wait_alone(pool, s.f_sq, done(i, G, G - 1))
                    pool.tensor_scalar(fms[:], ss[:], 1.0 / D, 1e-6, ALU.mult, ALU.add).then_inc(s.f_ms, 1)
                    pool.wait_ge(s.f_ms, done(i))
                    pool.wait_ge(s.f_xn, prev(i, G))
                    pool.tensor_tensor(frn[:], fms[:], v.neghalf[:, 0:G], ALU.pow).then_inc(s.f_rn, 1)
                    pool.wait_ge(s.f_xn, done(i, G, G - 1))
                    hx = v.hbuf[:, bass.ds(i * G, G), :]
                    pool.tensor_tensor(hx, hx, v.x1buf[:, bass.ds(i * G, G), :], ALU.add).then_inc(s.f_hx, 1)
                    wait_alone(pool, s.f_mv, done(i, G, G - 1))
                    pool.tensor_scalar(va[:], mv[:, :, 1], 1e-5, None, ALU.add).then_inc(s.f_va, 1)
                    pool.wait_ge(s.f_va, done(i))
                    pool.wait_ge(s.f_xf, prev(i, G))
                    pool.tensor_tensor(rs[:], va[:], v.neghalf[:, 0:G], ALU.pow).then_inc(s.f_rs, 1)
                    send(i, half)
            pool.wait_ge(s.f_send0, (NG // 2 * NS + 1) * 16)
            pool.wait_ge(s.f_send1, (NG // 2 * NS + 1) * 16)

        @block.scalar
        def _(act):
            prime(act, *own["act"])
            with act.Fori(0, NG, 1) as i:
                act.wait_ge(s.f_ms, prev(i))
                for b in range(G):
                    act.wait_ge(s.f_sq, done(i, G, b - 1))
                    act.activation(fsq[:], row(v.x1buf, i * G + b), ACT.Square,
                                   accum_out=ss[:, b:b + 1]).then_inc(s.f_sq, 1)
                act.wait_ge(s.f_xT, done(i))
                act.wait_ge(s.f_ab, prev(i, NH))
                act.activation(xnT[:, 0, :], XA[0:HD, :], ACT.Copy).then_inc(s.f_xTa, 1)
                for k in range(NH):
                    act.wait_ge(s.f_ab, done(i, NH, k))
                    act.wait_ge(s.f_u, done(i, NH, k - 2))
                    act.activation(act_a[:, k % 2, :], (A0, A1)[k % 2][:], ACT.Silu).then_inc(s.f_silu, 1)
                act.wait_ge(s.f_fT, done(i))
                act.wait_ge(s.f_gate, prev(i))
                act.activation(xfT[0:HD, 0, :], XA[0:HD, :], ACT.Copy).then_inc(s.f_fTa, 1)

        @block.tensor
        def _(pe):
            prime(pe, *own["pe"])
            pe.wait_ge(s.f_const, 1)
            pe.wait_ge(s.f_fold, 2)
            pe.wait_ge(s.ld_f, 5 * 16)

            def turn(src, i, ready, signal):
                for b in range(G):
                    pe.wait_ge(ready, done(i, G, b))
                    for k in range(2):
                        mm = pe.transpose((XA, XB)[k][0:HD, b * P:(b + 1) * P], src[:, b, k * HD:(k + 1) * HD], v.ident)
                mm.then_inc(signal, 1)

            def group(i, half):
                pe.wait_ge(s.f_fTa, prev(i))
                pe.wait_ge(s.f_fTv, prev(i))
                turn(xn, i, s.f_xn, s.f_xT)
                pe.wait_ge(s.f_xTa, done(i))
                pe.wait_ge(s.f_xTv, done(i))
                pe.wait_ge(s.f_score, prev(i))
                pe.wait_ge(s.f_place, prev(i))
                for k in range(NH):
                    pe.wait_ge(s.f_u, done(i, NH, k - 2))
                    for n, dst in enumerate(((A0, A1)[k % 2], (B0, B1)[k % 2])):
                        for c in range(2):
                            w = w12[:, c, n * HID + k * P:n * HID + (k + 1) * P]
                            mm = pe.matmul(dst[:], w, xnT[:, c, :], start=(c == 0), stop=(c == 1))
                    mm.then_inc(s.f_ab, 1)
                pe.wait_ge(s.f_h, prev(i, 2))
                pe.wait_ge(s.f_u, done(i, NH, NH - 1))
                for b in range(G):
                    for k in range(NH):
                        mm = pe.matmul((Y0, Y1)[b // 2][:, (b % 2) * D:(b % 2 + 1) * D], u[:, k, b * P:(b + 1) * P],
                                       w3s[:, k, :], start=(k == 0), stop=(k == NH - 1))
                    if b % 2:
                        mm.then_inc(s.f_w3, 1)
                turn(xf[:, half], i, s.f_xf, s.f_fT)
                pe.wait_ge(s.f_fTa, done(i))
                pe.wait_ge(s.f_fTv, done(i))
                for b in range(G):
                    pe.matmul(A0[:, b * E:(b + 1) * E], xfT[:, 0, b * P:(b + 1) * P], gw[:, 0, :],
                              start=True, stop=False)
                    mm = pe.matmul(A0[:, b * E:(b + 1) * E], xfT[0:HD, 1, b * P:(b + 1) * P], gw[0:HD, 1, :],
                                   start=False, stop=True)
                mm.then_inc(s.f_gate, 1)
                pe.wait_ge(s.f_run, done(i, G, G - 1))
                pe.matmul(B0[:, 0:G * E], v.ones, before[:].rearrange("p b e -> p (b e)"), start=True, stop=False)
                pe.matmul(B0[:, 0:G * E], v.strict, mask[:].rearrange("p b e -> p (b e)"),
                          start=False, stop=True).then_inc(s.f_rank, 1)

            with pe.Fori(0, NG // 2, 1) as j:
                group(j * 2, 0)
                group(j * 2 + 1, 1)

        @block.vector
        def _(dve):
            prime(dve, *own["dve"])
            dve.memset(xfT[HD:HD + 1, :, :], 1.0).then_inc(s.f_const, 1)
            dve.tensor_scalar(region[:], v.rows[:, 0:E], float(REGION), None, ALU.mult)
            dve.wait_ge(s.ld_f, 5 * 16)
            for k in range(2):
                dve.tensor_scalar(w12[:, k], w12[:, k], v.fcol[:, k:k + 1], None, ALU.mult).then_inc(s.f_fold, 1)

            def group(i, half, j):
                send = (s.f_send0, s.f_send1)[half]
                store = (s.f_store0, s.f_store1)[half]
                dve.wait_ge(s.f_rn, done(i))
                dve.wait_ge(s.f_xT, prev(i))
                for b in range(G):
                    dve.tensor_scalar(xn[:, b, :], row(v.x1buf, i * G + b), frn[:, b:b + 1], None,
                                      ALU.mult).then_inc(s.f_xn, 1)
                dve.wait_ge(s.f_xT, done(i))
                dve.wait_ge(s.f_ab, prev(i, NH))
                dve.tensor_copy(xnT[:, 1, :], XB[0:HD, :]).then_inc(s.f_xTv, 1)
                dve.wait_ge(s.f_w3, prev(i, 2))
                for k in range(NH):
                    dve.wait_ge(s.f_silu, done(i, NH, k))
                    dve.tensor_tensor(u[:, k, :], act_a[:, k % 2, :], (B0, B1)[k % 2][:], ALU.mult).then_inc(s.f_u, 1)
                dve.wait_ge(s.f_hx, done(i))
                for k in range(2):
                    dve.wait_ge(s.f_w3, done(i, 2, k))
                    hh = v.hbuf[:, bass.ds(i * G + 2 * k, 2), :]
                    dve.tensor_tensor(hh, hh, (Y0, Y1)[k][:, 0:2 * D].rearrange("p (b d) -> p b d", b=2),
                                      ALU.add).then_inc(s.f_h, 1)
                for b in range(G):
                    wait_alone(dve, s.f_h, done(i, 2, b // 2))
                    dve.bn_stats(stat[:, b, :], row(v.hbuf, i * G + b)).then_inc(s.f_stat, 1)
                for b in range(G):
                    wait_alone(dve, s.f_stat, done(i, G, b))
                    dve.bn_aggr(mv[:, b, :], stat[:, b, :]).then_inc(s.f_mv, 1)
                dve.wait_ge(s.f_rs, done(i))
                dve.wait_ge(send, j * (16 * G * TOPK) + 16)
                dve.wait_ge(store, prev(j, 16))
                for b in range(G):
                    dve.tensor_scalar(xf[:, half, b, :], row(v.hbuf, i * G + b), mv[:, b, 0:1], rs[:, b:b + 1],
                                      ALU.subtract, ALU.mult).then_inc(s.f_xf, 1)
                dve.wait_ge(s.f_fT, done(i))
                dve.wait_ge(s.f_gate, prev(i))
                dve.tensor_copy(xfT[0:HD, 1, :], XB[0:HD, :]).then_inc(s.f_fTv, 1)
                dve.wait_ge(s.f_gate, done(i))
                dve.tensor_copy(sc[:], A0[:, 0:G * E].rearrange("p (b e) -> p b e", b=G)).then_inc(s.f_score, 1)
                dve.wait_ge(s.f_score, done(i))
                dve.tensor_copy(v.scores[:, bass.ds(i * G, G), :], sc[:]).then_inc(s.f_keep, 1)
                for b in range(G):
                    dve.max(top8[:, b, :], sc[:, b, 1:E]).then_inc(s.f_top, 1)
                for b in range(G):
                    wait_alone(dve, s.f_top, done(i, G, b))
                    dve.max_index(idx8[:, b, :], top8[:, b, :], sc[:, b, 1:E]).then_inc(s.f_idx, 1)
                dve.wait_ge(s.f_idx, done(i, G, G - 1))
                pick = v.picked[:, bass.ds(i * G, G), :]
                dve.tensor_scalar(pick, idx8[:, :, 0:TOPK], 1.0, None, ALU.add).then_inc(s.f_pick, 1)
                dve.tensor_copy(v.score3[:, bass.ds(i * G, G), :], top8[:, :, 0:TOPK]).then_inc(s.f_keep, 1)
                dve.wait_ge(s.f_pick, done(i))
                flat = hot[:].rearrange("p b k e -> p (b k) e")
                dve.tensor_tensor(flat,
                                  v.rows[:, 0:E].rearrange("p (o e) -> p o e", o=1).broadcast_to([P, G * TOPK, E]),
                                  pick.rearrange("p b (k u) -> p (b k) u", u=1).broadcast_to([P, G * TOPK, E]),
                                  ALU.is_equal).then_inc(s.f_hot, 1)
                dve.wait_ge(s.f_hot, done(i))
                dve.wait_ge(s.f_rank, prev(i))
                dve.tensor_tensor(mask[:], hot[:, :, 0, :], hot[:, :, 1, :], ALU.add).then_inc(s.f_m1, 1)
                dve.wait_ge(s.f_m1, done(i))
                dve.tensor_tensor(mask[:], mask[:], hot[:, :, 2, :], ALU.add).then_inc(s.f_mask, 1)
                dve.wait_ge(s.f_mask, done(i))
                for b in range(G):
                    if b == 0:
                        dve.tensor_copy(before[:, 0, :], v.chosen[:]).then_inc(s.f_run, 1)
                    else:
                        dve.tensor_tensor(before[:, b, :], before[:, b - 1, :], mask[:, b - 1, :],
                                          ALU.add).then_inc(s.f_run, 1)
                    dve.wait_ge(s.f_run, done(i, G, b))
                dve.tensor_tensor(v.chosen[:], before[:, G - 1, :], mask[:, G - 1, :], ALU.add).then_inc(s.f_keep, 1)
                dve.wait_ge(s.f_rank, done(i))
                dve.tensor_tensor(rank[:], B0[:, 0:G * E].rearrange("p (b e) -> p b e", b=G),
                                  region[:].rearrange("p (o e) -> p o e", o=1).broadcast_to([P, G, E]),
                                  ALU.add).then_inc(s.f_place, 1)
                dve.wait_ge(s.f_place, done(i))
                for k in range(TOPK):
                    dve.tensor_tensor(hot_s[:, :, k, :], hot[:, :, k, :], rank[:], ALU.mult).then_inc(s.f_hs, 1)
                dve.wait_ge(s.f_hs, done(i, TOPK, TOPK - 1))
                dve.tensor_reduce(slot_f[:].rearrange("p b k -> p (b k)"), hot_s[:].rearrange("p b k e -> p (b k) e"),
                                  AX.X, ALU.add).then_inc(s.f_slot, 1)
                dve.wait_ge(s.f_slot, done(i))
                dve.tensor_copy(v.place[:, bass.ds(i * G, G), :], slot_f[:]).then_inc(s.f_keep, 1)
                dve.tensor_copy(slot_i[:, half], slot_f[:]).then_inc(s.f_int, 1)
                dve.wait_ge(s.f_keep, done(i, 4, 3))

            with dve.Fori(0, NG // 2, 1) as j:
                group(j * 2, 0, j)
                group(j * 2 + 1, 1, j)


def experts(nc, sbuf, sems, prime, bank, v):
    v = named("Shared", v)
    with ExitStack() as ctx:
        e_of = sbuf(ctx, "e_of", [1, RT], I32)
        r_of = sbuf(ctx, "r_of", [1, RT], I32)
        count = sbuf(ctx, "count", [P, E])
        cmp32 = sbuf(ctx, "cmp32", [P, E, NT])
        tiles = sbuf(ctx, "tiles", [P, E])
        ends = sbuf(ctx, "ends", [P, E])
        onesE = sbuf(ctx, "onesE", [P, E])
        cmpT = sbuf(ctx, "cmpT", [1, RT, E])
        cnt = sbuf(ctx, "cnt", [1, 6, RT])
        pad_f = sbuf(ctx, "pad_f", [P, E])
        pad_i = sbuf(ctx, "pad_i", [P, E], I32)
        zero = sbuf(ctx, "zero", [P, D])
        xin = sbuf(ctx, "xin", [P, 4, D])
        xT = sbuf(ctx, "exT", [HD + 1, 2, 2 * P])
        h = sbuf(ctx, "h", [P, 2, FH])
        st = sbuf(ctx, "est", [P, 2, 6])
        mv = sbuf(ctx, "emv", [P, 2, 2])
        va = sbuf(ctx, "eva", [P, 2])
        rs = sbuf(ctx, "ers", [P, 2])
        hT = sbuf(ctx, "hT", [P, 2, FH])
        y = sbuf(ctx, "y", [P, 4, D])
        s = sems("t_cnt", "t_chain", "t_ok", "t_pad", "t_zero", "t_padded", "e_one",
                 "e_in0", "e_in1", "e_in2", "e_in3", "e_xT", "e_xTs", "e_h", "e_gelu", "e_st", "e_mv", "e_va",
                 "e_rs", "e_hT", "e_hTs", "e_y", "e_ys", "e_out0", "e_out1", "e_out2", "e_out3")
        e_in = (s.e_in0, s.e_in1, s.e_in2, s.e_in3)
        e_out = (s.e_out0, s.e_out1, s.e_out2, s.e_out3)
        own = dict(dve=(s.e_xTs, s.e_st, s.e_mv, s.e_hTs), act=(s.e_gelu, s.e_ys),
                              pe=(s.e_xT, s.e_h, s.e_hT, s.e_y), pool=(s.e_va, s.e_rs), sp=e_in + e_out)
        XT, HP, HT, YP = (bank[0], bank[1]), (bank[2], bank[3]), (bank[4], bank[5]), (bank[6], bank[7])
        block = ctx.enter_context(nc.Block())
        QS, QR = NT // 4, RT // 4
        assert NT % 4 == 0 and RT % 2 == 0


        @block.sync
        def _(sp):
            prime(sp, *own["sp"])

            with sp.Fori(0, QS, 1) as q:
                for k in range(4):
                    sp.wait_ge(s.e_xT, done(q * 4 + k) - 4)
                    sp.dma_start(xin[:, k, :], v.x_rows[bass.ds((q * 4 + k) * P, P), :]).then_inc(e_in[k], 16)
            sp.wait_ge(s.t_ok, 1)
            sp.wait_ge(s.t_padded, (E - 1) * 16)
            with sp.Fori(0, QR, 1) as q:
                for k in range(4):
                    row = sp.value_load(r_of[0:1, bass.ds(q * 4 + k, 1)], min_val=0, max_val=(E * REGION - P))
                    sp.wait_ge(s.e_xT, done(q * 4 + k + NT) - 4)
                    sp.dma_start(xin[:, k, :], v.x_rows[bass.ds(row, P), :]).then_inc(e_in[k], 16)
            for k in range(RT % 4):
                n = QR * 4 + k
                row = sp.value_load(r_of[0:1, n:n + 1], min_val=0, max_val=(E * REGION - P))
                sp.wait_ge(s.e_xT, done(NT + n) - 4)
                sp.dma_start(xin[:, k, :], v.x_rows[bass.ds(row, P), :]).then_inc(e_in[k], 16)
            for k in range(4):
                sp.wait_ge(e_out[k], dma_done(QS + QR - 1 + (1 if k < RT % 4 else 0)))

        @block.gpsimd
        def _(pool):
            prime(pool, *own["pool"])
            pool.memset(zero[:], 0.0).then_inc(s.t_zero, 1)
            pool.wait_ge(s.t_pad, 1)
            pool.wait_ge(s.t_zero, 1)
            for e in range(1, E):
                pool.indirect_dma_start(v.x_rows, bass.IndirectOffsetOnAxis(ap=pad_i[:, e:e + 1], axis=0),
                                        zero[:], None).then_inc(s.t_padded, 16)
            NN = NT + RT
            with pool.Fori(0, NN // 2, 1) as q:
                for k in range(2):
                    n = q * 2 + k
                    wait_alone(pool, s.e_mv, done(n))
                    pool.tensor_scalar(va[:, k:k + 1], mv[:, k, 1:2], 1e-5, None, ALU.add).then_inc(s.e_va, 1)
                    pool.wait_ge(s.e_va, done(n))
                    pool.wait_ge(s.e_ys, done(n) - 2)
                    pool.tensor_tensor(rs[:, k:k + 1], va[:, k:k + 1], v.neghalf[:, 0:1], ALU.pow).then_inc(s.e_rs, 1)

        def tile_loop(eng, step, dynamic):
            with eng.Fori(0, QS, 1) as q:
                for k in range(4):
                    step(q * 4 + k, k, q, 0)
            if dynamic:
                eng.wait_ge(s.t_ok, 1)
            with eng.Fori(0, QR, 1) as q:
                for k in range(4):
                    e = eng.value_load(e_of[0:1, bass.ds(q * 4 + k, 1)], min_val=0, max_val=E - 1) if dynamic else 0
                    step(q * 4 + k + NT, k, q + QS, e)
            for k in range(RT % 4):
                n = QR * 4 + k
                e = eng.value_load(e_of[0:1, n:n + 1], min_val=0, max_val=E - 1) if dynamic else 0
                step(n + NT, k, QS + QR, e)

        @block.tensor
        def _(pe):
            prime(pe, *own["pe"])
            pe.matmul(bank[7][:, 256:256 + E], v.ones, v.chosen[:], start=True, stop=True).then_inc(s.t_cnt, 1)
            pe.wait_ge(s.e_one, 1)
            pe.wait_ge(s.t_chain, 1)

            def step(n, k, turn, e):
                m = k % 2
                pe.wait_ge(e_in[k], dma_done(turn))
                pe.wait_ge(s.e_xTs, done(n) - 2)
                for c in range(2):
                    mm = pe.transpose(XT[m][0:HD, c * P:(c + 1) * P], xin[:, k, c * HD:(c + 1) * HD], v.ident)
                mm.then_inc(s.e_xT, 1)
                pe.wait_ge(s.e_xTs, done(n))
                pe.wait_ge(s.e_gelu, done(n) - 2)
                if isinstance(e, int):
                    w1 = [v.W1[:, e, 0, :], v.W1[0:HD, e, 1, :]]
                    w2 = [v.W2[:, e, c, :] for c in range(FK)]
                else:
                    w1 = [v.W1[:, bass.ds(e, 1), 0, :].rearrange("p o n -> p (o n)"),
                          v.W1[0:HD, bass.ds(e, 1), 1, :].rearrange("p o n -> p (o n)")]
                    w2 = [v.W2[:, bass.ds(e, 1), c, :].rearrange("p o n -> p (o n)") for c in range(FK)]
                pe.matmul(HP[m][:, 0:FH], xT[:, m, 0:P], w1[0], start=True, stop=False)
                pe.matmul(HP[m][:, 0:FH], xT[0:HD, m, P:2 * P], w1[1], start=False, stop=True).then_inc(s.e_h, 1)
                pe.wait_ge(s.e_gelu, done(n))
                pe.wait_ge(s.e_hTs, done(n) - 2)
                for c in range(FK):
                    mm = pe.transpose(HT[m][:, c * P:(c + 1) * P], h[:, m, c * P:(c + 1) * P], v.ident)
                mm.then_inc(s.e_hT, 1)
                pe.wait_ge(s.e_hTs, done(n))
                pe.wait_ge(s.e_ys, done(n) - 2)
                for c in range(FK):
                    mm = pe.matmul(YP[m][:, 0:D], hT[:, m, c * P:(c + 1) * P], w2[c], start=(c == 0), stop=(c == FK - 1))
                mm.then_inc(s.e_y, 1)

            tile_loop(pe, step, True)

        @block.scalar
        def _(act):
            prime(act, *own["act"])

            def step(n, k, turn, e):
                m = k % 2
                act.wait_ge(s.e_h, done(n))
                act.wait_ge(s.e_hT, done(n) - 2)
                act.wait_ge(s.e_st, done(n) - 2)
                act.activation(h[:, m, :], HP[m][:, 0:FH], ACT.Gelu).then_inc(s.e_gelu, 1)
                act.wait_ge(s.e_y, done(n))
                act.wait_ge(s.e_rs, done(n))
                act.wait_ge(e_out[k], prev(turn, 16))
                act.activation(y[:, k, :], YP[m][:, 0:D], ACT.Copy, scale=rs[:, m:m + 1]).then_inc(s.e_ys, 1)
                act.wait_ge(s.e_ys, done(n))
                act.dma_start(v.y_rows[bass.ds(n * P, P), :], y[:, k, :]).then_inc(e_out[k], 16)

            tile_loop(act, step, False)

        @block.vector
        def _(dve):
            prime(dve, *own["dve"])
            n_link = [0]

            def link(ins):
                n_link[0] += 1
                ins.then_inc(s.t_chain, 1)
                dve.wait_ge(s.t_chain, n_link[0])

            dve.memset(xT[HD:HD + 1, :, :], 1.0).then_inc(s.e_one, 1)
            dve.wait_ge(s.t_cnt, 1)
            link(dve.tensor_copy(count[:], bank[7][:, 256:256 + E]))
            link(dve.scalar_tensor_tensor(pad_f[:], v.rows[:, 0:E], float(REGION), count[:], ALU.mult, ALU.add))
            link(dve.tensor_scalar(pad_f[:], pad_f[:], v.lpos[:, NG:NG + 1], None, ALU.add))
            dve.tensor_copy(pad_i[:], pad_f[:]).then_inc(s.t_pad, 1)
            link(dve.tensor_scalar(cmp32[:, 0, :], v.rows[:, 0:NT], float(P), None, ALU.mult))
            link(dve.tensor_copy(cmp32[:, 1, :], cmp32[:, 0, :]))
            link(dve.tensor_tensor(cmp32[:, 2:E, :],
                                   count[:, 2:E].rearrange("p (e u) -> p e u", u=1).broadcast_to([P, E - 2, NT]),
                                   cmp32[:, 0:1, :].broadcast_to([P, E - 2, NT]), ALU.is_gt))
            link(dve.tensor_tensor(cmp32[:, 1, :], count[:, 1:2].broadcast_to([P, NT]), cmp32[:, 1, :], ALU.is_gt))
            link(dve.memset(tiles[:, 0:1], 0.0))
            link(dve.tensor_reduce(tiles[:, 1:E], cmp32[:, 1:E, :], AX.X, ALU.add))
            link(dve.memset(onesE[:], 1.0))
            link(dve.tensor_tensor_scan(ends[:], onesE[:], tiles[:], 0.0, ALU.mult, ALU.add))
            it = v.rows[0:1, 0:RT]
            link(dve.tensor_tensor(cmpT[:, :, 1:E], it.rearrange("p (i u) -> p i u", u=1).broadcast_to([1, RT, E - 1]),
                                   ends[0:1, 1:E].rearrange("p (u e) -> p u e", u=1).broadcast_to([1, RT, E - 1]),
                                   ALU.is_ge))
            link(dve.tensor_reduce(cnt[:, 0, :], cmpT[:, :, 1:E], AX.X, ALU.add))
            link(dve.tensor_tensor(cmpT[:, :, 1:E], cmpT[:, :, 1:E],
                                   tiles[0:1, 1:E].rearrange("p (u e) -> p u e", u=1).broadcast_to([1, RT, E - 1]),
                                   ALU.mult))
            link(dve.tensor_reduce(cnt[:, 1, :], cmpT[:, :, 1:E], AX.X, ALU.add))
            link(dve.tensor_scalar(cnt[:, 2, :], it, ends[0:1, E - 1:E], None, ALU.is_lt))
            link(dve.tensor_tensor(cnt[:, 3, :], it, cnt[:, 1, :], ALU.subtract))
            link(dve.tensor_tensor(cnt[:, 3, :], cnt[:, 3, :], cnt[:, 2, :], ALU.mult))
            link(dve.tensor_tensor(cnt[:, 4, :], cnt[:, 0, :], cnt[:, 2, :], ALU.mult))
            link(dve.tensor_scalar(cnt[:, 4, :], cnt[:, 4, :], 1.0, None, ALU.add))
            link(dve.tensor_copy(e_of[:], cnt[:, 4, :]))
            link(dve.tensor_scalar(cnt[:, 4, :], cnt[:, 4, :], float(REGION), None, ALU.mult))
            link(dve.scalar_tensor_tensor(cnt[:, 5, :], cnt[:, 3, :], float(P), cnt[:, 4, :], ALU.mult, ALU.add))
            link(dve.tensor_copy(r_of[:], cnt[:, 5, :]))
            link(dve.tensor_tensor(v.y_row[:], ends[:], tiles[:], ALU.subtract))
            link(dve.tensor_scalar(v.y_row[:], v.y_row[:], float(P), float(NT * P), ALU.mult, ALU.add))
            link(dve.scalar_tensor_tensor(v.y_row[:], v.rows[:, 0:E], -float(REGION), v.y_row[:], ALU.mult, ALU.add))
            dve.sem_inc(s.t_ok, 1)

            def step(n, k, turn, e):
                m = k % 2
                dve.wait_ge(s.e_xT, done(n))
                dve.wait_ge(s.e_h, done(n) - 2)
                dve.tensor_copy(xT[0:HD, m, :], XT[m][0:HD, 0:2 * P]).then_inc(s.e_xTs, 1)
                wait_alone(dve, s.e_gelu, done(n))
                dve.bn_stats(st[:, m, :], h[:, m, :]).then_inc(s.e_st, 1)
                wait_alone(dve, s.e_st, done(n))
                dve.wait_ge(s.e_va, done(n) - 2)
                dve.bn_aggr(mv[:, m, :], st[:, m, :]).then_inc(s.e_mv, 1)
                dve.wait_ge(s.e_hT, done(n))
                dve.wait_ge(s.e_y, done(n) - 2)
                dve.tensor_copy(hT[:, m, :], HT[m][:, 0:FH]).then_inc(s.e_hTs, 1)

            tile_loop(dve, step, False)


def combine(nc, sbuf, sems, prime, bank, v):
    v = named("Shared", v)
    NK = NT * TOPK
    with ExitStack() as ctx:
        w3 = sbuf(ctx, "w3k", [P, NT, TOPK])
        ex = sbuf(ctx, "ex", [P, NT, E])
        sm = sbuf(ctx, "sm", [P, NT])
        rsm = sbuf(ctx, "rsm", [P, NT])
        hot = sbuf(ctx, "chot", [P, NK, E])
        tmp = sbuf(ctx, "ctmp", [P, NK, E])
        comb = sbuf(ctx, "comb", [P, NT, E])
        slot = sbuf(ctx, "slot", [P, NT, TOPK])
        slot_i = sbuf(ctx, "cslot", [P, NT, TOPK], I32)
        ysh = sbuf(ctx, "ysh", [P, 2, D])
        yk = sbuf(ctx, "yk", [P, 2, TOPK, D])
        cT = sbuf(ctx, "cT", [E, NT * P])
        o = sbuf(ctx, "o", [P, 2, D])
        s = sems("c_chain", "c_exp_in", "c_exp", "c_slot", "c_comb", "c_sh0", "c_sh1", "c_g0", "c_g1", "c_T",
                 "c_Ts", "c_b", "c_a0", "c_a1", "c_a2", "c_a3", "c_o", "c_out0", "c_out1")
        c_sh, c_g, c_out = (s.c_sh0, s.c_sh1), (s.c_g0, s.c_g1), (s.c_out0, s.c_out1)
        block = ctx.enter_context(nc.Block())

        @block.scalar
        def _(act):
            act.wait_ge(s.c_exp_in, 1)
            act.activation(ex[:], ex[:], ACT.Exp).then_inc(s.c_exp, 1)
            act.activation(w3[:], w3[:], ACT.Exp).then_inc(s.c_exp, 1)
            for q in range(NT // 4):
                act.wait_ge(s.c_T, q + 1)
                act.activation(cT[:, q * 4 * P:(q + 1) * 4 * P], bank[q % 2][0:E, :], ACT.Copy).then_inc(s.c_Ts, 1)

        def store(sp, t):
            sp.wait_ge(s.c_o, t + 1)
            b, c = t % NB, t // NB
            sp.dma_start(v.out[b, c * P:(c + 1) * P, :], o[:, t % 2, :]).then_inc(c_out[t % 2], 16)

        @block.sync
        def _(sp):
            for t in range(NT):
                if t >= 2:
                    sp.wait_ge(s.c_a0, t - 1)
                sp.dma_start(ysh[:, t % 2, :], v.y_rows[t * P:(t + 1) * P, :]).then_inc(c_sh[t % 2], 16)
                if t >= 1:
                    store(sp, t - 1)
            store(sp, NT - 1)
            sp.wait_ge(s.c_out0, NT // 2 * 16)
            sp.wait_ge(s.c_out1, NT // 2 * 16)

        @block.gpsimd
        def _(pool):
            pool.wait_ge(s.c_slot, 1)
            for t in range(NT):
                if t >= 2:
                    pool.wait_ge(s.c_a3, t - 1)
                for k in range(TOPK):
                    pool.indirect_dma_start(yk[:, t % 2, k, :], None, v.y_rows,
                                            bass.IndirectOffsetOnAxis(ap=slot_i[:, t, k:k + 1], axis=0)).then_inc(
                                                c_g[t % 2], 16)

        @block.tensor
        def _(pe):
            pe.wait_ge(s.c_comb, 1)
            for q in range(NT // 4):
                if q >= 2:
                    pe.wait_ge(s.c_Ts, q - 1)
                for b in range(4):
                    mm = pe.transpose(bank[q % 2][0:E, b * P:(b + 1) * P], comb[:, q * 4 + b, :], v.ident)
                mm.then_inc(s.c_T, 1)
            for t in range(NT):
                pe.wait_ge(s.c_Ts, t // 4 + 1)
                if t >= 2:
                    pe.wait_ge(s.c_a0, t - 1)
                pe.matmul(bank[2 + t % 2][:, 0:D], cT[:, t * P:(t + 1) * P], v.B2[:], start=True,
                          stop=True).then_inc(s.c_b, 1)

        @block.vector
        def _(dve):
            n = [0]

            def link(ins):
                n[0] += 1
                ins.then_inc(s.c_chain, 1)
                dve.wait_ge(s.c_chain, n[0])

            link(dve.memset(v.scores[:, :, 0:1], -1e9))
            best = v.score3[:, :, 0:1]
            link(dve.tensor_tensor(ex[:], v.scores[:], best.broadcast_to([P, NT, E]), ALU.subtract))
            link(dve.tensor_tensor(w3[:], v.score3[:], best.broadcast_to([P, NT, TOPK]), ALU.subtract))
            dve.sem_inc(s.c_exp_in, 1)
            ek = v.picked[:].rearrange("p t (k u) -> p (t k) u", u=1).broadcast_to([P, NK, E])
            link(dve.tensor_tensor(hot[:], v.rows[:, 0:E].rearrange("p (o e) -> p o e", o=1).broadcast_to([P, NK, E]),
                                   ek, ALU.is_equal))
            link(dve.tensor_tensor(tmp[:], hot[:],
                                   v.y_row[:].rearrange("p (o e) -> p o e", o=1).broadcast_to([P, NK, E]), ALU.mult))
            link(dve.tensor_reduce(slot[:].rearrange("p t k -> p (t k)"), tmp[:], AX.X, ALU.add))
            link(dve.tensor_tensor(slot[:], slot[:], v.place[:], ALU.add))
            dve.tensor_copy(slot_i[:], slot[:]).then_inc(s.c_slot, 1)
            dve.wait_ge(s.c_exp, 2)
            link(dve.tensor_reduce(sm[:], ex[:], AX.X, ALU.add))
            link(dve.reciprocal(rsm[:], sm[:]))
            link(dve.tensor_tensor(w3[:], w3[:], rsm[:].rearrange("p (t u) -> p t u", u=1).broadcast_to([P, NT, TOPK]),
                                   ALU.mult))
            link(dve.tensor_tensor(tmp[:], hot[:],
                                   w3[:].rearrange("p t (k u) -> p (t k) u", u=1).broadcast_to([P, NK, E]), ALU.mult))
            t4 = tmp[:].rearrange("p (t k) e -> p t k e", k=TOPK)
            link(dve.tensor_tensor(comb[:], t4[:, :, 0, :], t4[:, :, 1, :], ALU.add))
            link(dve.tensor_tensor(comb[:], comb[:], t4[:, :, 2, :], ALU.add))
            link(dve.memset(comb[:, :, 0:1], 1.0))
            dve.sem_inc(s.c_comb, 1)
            for t in range(NT):
                m = t % 2
                hrow = v.hbuf[:, t, :]
                dve.wait_ge(c_sh[m], (t // 2 + 1) * 16)
                dve.wait_ge(s.c_b, t + 1)
                dve.tensor_tensor(ysh[:, m, :], ysh[:, m, :], bank[2 + m][:, 0:D], ALU.add).then_inc(s.c_chain, 1)
                n[0] += 1
                dve.wait_ge(s.c_chain, n[0])
                dve.tensor_tensor(hrow, hrow, ysh[:, m, :], ALU.add).then_inc(s.c_a0, 1)
                dve.wait_ge(s.c_a0, t + 1)
                dve.wait_ge(c_g[m], (t // 2 + 1) * 16 * TOPK)
                dve.scalar_tensor_tensor(hrow, yk[:, m, 0, :], w3[:, t, 0:1], hrow, ALU.mult, ALU.add).then_inc(s.c_a1, 1)
                dve.wait_ge(s.c_a1, t + 1)
                dve.scalar_tensor_tensor(hrow, yk[:, m, 1, :], w3[:, t, 1:2], hrow, ALU.mult, ALU.add).then_inc(s.c_a2, 1)
                dve.wait_ge(s.c_a2, t + 1)
                if t >= 2:
                    dve.wait_ge(c_out[m], t // 2 * 16)
                dve.scalar_tensor_tensor(o[:, m, :], yk[:, m, 2, :], w3[:, t, 2:3], hrow, ALU.mult,
                                         ALU.add).then_inc(s.c_o, 1)
                dve.wait_ge(s.c_o, t + 1)
                dve.sem_inc(s.c_a3, 1)


_OUTS = [((NB, L, D), "float32")]


def shape_constants():
    f = np.float32
    p = np.arange(L, dtype=f)[:, None]
    exps = (np.floor(np.arange(D, dtype=f) / f(2)) * f(2) / f(D))[None]
    den = np.power(10000.0, exps.astype(np.float64)).astype(f)
    ang = (p / den).astype(np.float64)
    pos = np.where(np.arange(D) % 2 == 0, np.sin(ang), np.cos(ang)).astype(f)
    inv = (f(1) / np.power(10000.0, (np.arange(0, DH, 2, dtype=f) / f(DH)).astype(np.float64)).astype(f))
    fr = (p * inv[None]).astype(f).astype(np.float64)
    cos = np.concatenate([np.cos(fr), np.cos(fr)], 1)
    sin = np.concatenate([np.sin(fr), -np.sin(fr)], 1)
    rope = np.stack([cos, sin]).astype(f)
    a = np.arange(P)
    mats = np.stack([np.eye(P), a[:, None] <= a[None], a[:, None] < a[None], np.ones((P, P))], 1).astype(f)
    rows = np.arange(256, dtype=f)[None]
    lpos = np.concatenate([np.arange(NG)[None] * P + a[:, None] + 1, a[:, None]], 1).astype(f)
    return dict(c_pos=pos, c_rope=rope, c_mats=mats, c_rows=rows, c_lpos=lpos)


_INS = ["x", "mask_BS_i2_0", "L0_tok_token_table", "L0_tok_segm_table", "L0_attn_ln_w", "L0_attn_w_comp",
        "L0_attn_w_qkv", "L0_attn_w_reso", "L0_attn_qn_w", "L0_attn_kn_w", "L0_attn_w_outgate",
        "L0_attn_head_decay", "L0_attn_temperature", "L0_attn_w_proj", "L0_attn_memn_w", "L0_attn_ffn_ln_w",
        "L0_attn_w1", "L0_attn_w2", "L0_attn_w3", "L0_ffn_gate_w", "L0_ffn_gate_b", "L0_ffn_fc1_w",
        "L0_ffn_fc1_b", "L0_ffn_ln_w", "L0_ffn_ln_b", "L0_ffn_fc2_w", "L0_ffn_fc2_b"]


def kernel(**inputs):
    import numpy as _np
    import concourse.bacc as _bacc
    from concourse import mybir as _mybir
    from concourse.bass_utils import run_bass_kernel_spmd as _run

    nc = _bacc.Bacc("TRN2", target_bir_lowering=False, num_devices=1)
    arrays, args = {}, []
    consts = shape_constants()
    for name in _INS + list(consts):
        a = _np.ascontiguousarray(inputs[name] if name in inputs else consts[name])
        arrays[f"in_{name}"] = a
        args.append(nc.dram_tensor(f"in_{name}", a.shape, _mybir.dt.from_np(a.dtype), kind="ExternalInput").ap())
    for i, (shape, dtype) in enumerate(_OUTS):
        dt = _mybir.dt.from_np(_np.dtype(dtype))
        args.append(nc.dram_tensor(f"out_{i}", shape, dt, kind="ExternalOutput").ap())
    program(nc, *args)
    r = _run(nc, [arrays], core_ids=[0])
    return r.results[0]["out_0"]
```

```python
from collections import namedtuple
from contextlib import ExitStack

import numpy as np

import concourse.bass as bass
from concourse import mybir

ALU = mybir.AluOpType
ACT = mybir.ActivationFunctionType
AX = mybir.AxisListType
F32 = mybir.dt.float32
F16 = mybir.dt.float16
I32 = mybir.dt.int32
U32 = mybir.dt.uint32

P = 128
NB, L, D = 4, 1024, 192
NT = NB * L // P
NG = L // P
G = NB
HD = D // 2
VOCAB, NSEG = 8000, 3
LAT, H, DH = 128, 12, 16
DV = DH + 1
HID = 512
E, FH = 16, 384
FK = FH // P
TOPK = 3
REGION = NB * L + P
SLOTS = TOPK * NB * L
RT = SLOTS // P + (E - 2)
PI = float(np.pi)
PRIME = 4
WS = 64.0
HS = 16.0


def done(i, n=1, k=0):
    return i * n + k + 1 + PRIME


def prev(i, n=1):
    return i * n + PRIME


def dma_done(i, n=1, k=0):
    return (i * n + k + 1) * 16 + PRIME


def named(kind, values):
    return namedtuple(kind, list(values))(*values.values())


def wait_alone(eng, sem, value):
    if not isinstance(value, int):
        value = eng.snap(eng.to_reg(value))
    eng.wait_ge(sem, PRIME)
    eng.wait_ge(sem, value)


def program(nc, x, seg, tok_table, seg_table, ln_w, w_comp, w_qkv, w_reso, qn_w, kn_w, w_outgate,
            head_decay, temperature, w_proj, memn_w, ffn_ln_w, w1, w2, w3, gate_w, gate_b, fc1_w,
            fc1_b, eln_w, eln_b, fc2_w, fc2_b, c_pos, c_rope, c_mats, c_rows, c_lpos, out):
    x_rows = nc.dram_tensor("x_rows", (E * REGION, 2 * D), F16).ap()
    y_rows = nc.dram_tensor("y_rows", ((NT + RT) * P, D), F32).ap()

    with ExitStack() as top:
        def sbuf(ctx, name, shape, dt=F32):
            return ctx.enter_context(nc.sbuf_tensor(name, shape, dt))

        in_use = []

        def sems(*names):
            made = named("Semaphores", {n: nc.alloc_semaphore(name=n) for n in names})
            in_use.extend(made)
            return made

        def release_sems():
            nc.clear_and_free_semaphores(in_use)
            nc.all_engine_barrier()
            in_use.clear()

        def prime(eng, *ss):
            for s in ss:
                eng.sem_inc(s, PRIME)

        bank = [top.enter_context(nc.psum_tensor(f"bank{k}", [P, 512], F32)) for k in range(8)]

        hbuf = sbuf(top, "hbuf", [P, NT, D])
        x1buf = sbuf(top, "x1buf", [P, NT, D])
        W1 = sbuf(top, "W1", [HD + 1, E, 2, 2, FH], F16)
        W2 = sbuf(top, "W2", [P, E, 2, FK, D], F16)
        B2 = sbuf(top, "B2", [E, D])
        mats = sbuf(top, "mats", [P, 4, P])
        ident16 = sbuf(top, "ident16", [P, P], F16)
        ident, causal, strict, ones = (mats[:, k, :] for k in range(4))
        rows = sbuf(top, "rows", [P, 256])
        lpos = sbuf(top, "lpos", [P, NG + 1])
        neghalf = sbuf(top, "neghalf", [P, 96])
        fcol = sbuf(top, "fcol", [HD, 2])
        picked = sbuf(top, "picked", [P, NT, TOPK])
        place = sbuf(top, "place", [P, NT, TOPK])
        score3 = sbuf(top, "score3", [P, NT, TOPK])
        scores = sbuf(top, "scores", [P, NT, E])
        chosen = sbuf(top, "chosen", [P, E])
        y_row = sbuf(top, "y_row", [P, E])

        with ExitStack() as att:
            latT = sbuf(att, "latT", [P, NT * P])
            gates = sbuf(att, "gates", [P, NT, H])
            scale = sbuf(att, "scale", [P, NG, 2 * H])
            rope = sbuf(att, "rope", [P, 2, 2, NG, DH])
            wqkv = sbuf(att, "wqkv", [P, 3 * D])
            wog = sbuf(att, "wog", [P, D])
            wproj = sbuf(att, "wproj", [HD, 2, D])
            with ExitStack() as emb:
                params = sbuf(emb, "params", [P, NT, 4 * H])
                wcomp = sbuf(emb, "wcomp", [HD, 2, LAT])
                wreso = sbuf(emb, "wreso", [P, 4 * H])
                pos = sbuf(emb, "pos", [P, NG, D])
                temp = sbuf(emb, "temp", [P, 1])
                tok_id = sbuf(emb, "tok_id", [P, NG, NB], I32)
                seg_hot = sbuf(emb, "seg_hot", [P, NG, NB, NSEG])
                segw = sbuf(emb, "segw", [NB * NSEG, NB, D])
                setup(nc, sbuf, sems, bank, locals())
                embed(nc, sbuf, sems, prime, bank, locals())
                write_gates(nc, sbuf, sems, locals())
            attend(nc, sbuf, sems, prime, bank, locals())
        release_sems()
        ffn(nc, sbuf, sems, prime, bank, locals())
        experts(nc, sbuf, sems, prime, bank, locals())
        combine(nc, sbuf, sems, prime, bank, locals())
        release_sems()


def halves(w):
    return w.rearrange("(k d) n -> d k n", k=2)


def setup(nc, sbuf, sems, bank, v):
    v = named("Shared", v)
    with ExitStack() as ctx:
        cols = sbuf(ctx, "cols", [HD, 2, 2])
        qkn = sbuf(ctx, "qkn", [P, 2, DH])
        cs = sbuf(ctx, "cs", [P, 2, NG, DH])
        ln_rows = sbuf(ctx, "ln_rows", [E * FK, 2, P])
        lnT = sbuf(ctx, "lnT", [P, 2, E * FK])
        lnw, lnb = (lnT[:, k, :].rearrange("p (e k) -> p e k", k=FK) for k in range(2))
        col_rows = sbuf(ctx, "col_rows", [2 * 3, HD])
        id_rows = sbuf(ctx, "id_rows", [NT, 2, P], I32)
        idf = sbuf(ctx, "idf", [NT, 2, P])
        idg = sbuf(ctx, "idg", [NT, P])
        lnb_diag = sbuf(ctx, "lnb_diag", [P, E, FK, E])
        b2 = sbuf(ctx, "b2", [E, D])
        RING = 2
        raw1 = sbuf(ctx, "raw1", [HD + 1, RING, 2, FH])
        raw2 = sbuf(ctx, "raw2", [P, RING, FK, D])
        w2c = sbuf(ctx, "w2c", [P, 2, FK, D])
        dec = sbuf(ctx, "dec", [P, 6, H])
        df = sbuf(ctx, "df", [P, NG, H])
        dfe = sbuf(ctx, "dfe", [P, NG, H])
        seg_id = sbuf(ctx, "seg_id", [P, NG, NB])
        s = sems("seg_clear", "ld_small", "ld_ids", "ld_ln", "ids_clean", "turned", "turned_ok", "ld_w", "ld_b2", "ld_const",
                 "ld_e0", "ld_e1", "b2_sum", "b2_ok", "raw2_read", "w2_scaled", "col_sum",
                 "centred", "w2_hi", "w2_lo", "w1_hi", "w1_lo", "diag_ok", "decay_in", "tanh_ok", "ln_ok",
                 "df_in", "df_ok", "chain")
        ld_e = (s.ld_e0, s.ld_e1)
        block = ctx.enter_context(nc.Block())

        @block.sync
        def _(sp):
            bc = lambda a, n: a.rearrange("(o n) -> o n", o=1).broadcast_to([P, n])
            for k, a in enumerate((v.x, v.seg)):
                sp.dma_start(id_rows[:, k, :], a.rearrange("b (c p) -> (b c) p", p=P)).then_inc(s.ld_ids, 16)
            sp.dma_start(v.mats[:], v.c_mats).then_inc(s.ld_const, 16)
            sp.dma_start(v.rows[:], v.c_rows.broadcast_to([P, 256])).then_inc(s.ld_const, 16)
            sp.dma_start(v.lpos[:], v.c_lpos).then_inc(s.ld_const, 16)
            sp.dma_start(v.pos[:], v.c_pos.rearrange("(c p) d -> p c d", p=P)).then_inc(s.ld_const, 16)
            for k in range(2):
                sp.dma_start(cs[:, k], v.c_rope[k].rearrange("(c p) d -> p c d", p=P)).then_inc(s.ld_const, 16)
            sp.dma_start(dec[:, 0, :], bc(v.head_decay, H)).then_inc(s.ld_small, 16)
            sp.dma_start(v.temp[:], bc(v.temperature, 1)).then_inc(s.ld_small, 16)
            for k, a in enumerate((v.qn_w, v.kn_w)):
                sp.dma_start(qkn[:, k, :], bc(a, DH)).then_inc(s.ld_small, 16)
            for k, a in enumerate((v.ln_w, v.memn_w, v.ffn_ln_w)):
                sp.dma_start(col_rows[2 * k:2 * k + 2, :], a.rearrange("(k d) -> k d", k=2)).then_inc(s.ld_small, 16)
            sp.dma_start(v.wcomp[:], halves(v.w_comp)).then_inc(s.ld_w, 16)
            sp.dma_start(v.wproj[:], halves(v.w_proj)).then_inc(s.ld_w, 16)
            sp.dma_start(v.wqkv[:], v.w_qkv).then_inc(s.ld_w, 16)
            sp.dma_start(v.wog[:], v.w_outgate).then_inc(s.ld_w, 16)
            sp.dma_start(v.wreso[:], v.w_reso).then_inc(s.ld_w, 16)
            sp.wait_ge(s.seg_clear, 1)
            for b in range(NB):
                sp.dma_start(v.segw[b * NSEG:(b + 1) * NSEG, b, :], v.seg_table).then_inc(s.ld_w, 16)
            for e in range(E):
                if e >= RING:
                    sp.wait_ge(s.w1_lo, e - RING + 1)
                    sp.wait_ge(s.w2_scaled, e - RING + 1)
                    sp.wait_ge(s.raw2_read, e - RING + 1)
                r = e % RING
                sp.dma_start(raw1[0:HD, r], halves(v.fc1_w[e])).then_inc(ld_e[r], 16)
                sp.dma_start(raw1[HD:HD + 1, r, 0, :], v.fc1_b[e:e + 1, :]).then_inc(ld_e[r], 16)
                sp.dma_start(raw2[:, r], v.fc2_w[e].rearrange("(k p) n -> p k n", p=P)).then_inc(ld_e[r], 16)
            sp.wait_ge(s.ld_w, 9 * 16)

        @block.scalar
        def _(act):
            for k, a in enumerate((v.eln_w, v.eln_b)):
                act.dma_start(ln_rows[:, k, :], a.rearrange("e (k p) -> (e k) p", p=P)).then_inc(s.ld_ln, 16)
            act.dma_start(b2[:], v.fc2_b).then_inc(s.ld_b2, 16)
            act.wait_ge(s.ld_small, 7 * 16)
            act.activation(dec[:, 1, :], dec[:, 0, :], ACT.Tanh, scale=0.5).then_inc(s.tanh_ok, 1)
            act.wait_ge(s.decay_in, 1)
            act.activation(dec[:, 3, :], dec[:, 2, :], ACT.Ln).then_inc(s.ln_ok, 1)
            act.wait_ge(s.df_in, 1)
            act.activation(df[:], df[:], ACT.Exp).then_inc(s.df_ok, 1)
            act.wait_ge(s.turned_ok, 1)
            for e in range(E):
                r = e % RING
                act.wait_ge(ld_e[r], (e // RING + 1) * 48)
                if e >= 2:
                    act.wait_ge(s.w2_lo, e - 1)
                for k in range(FK):
                    ins = act.activation(w2c[:, e % 2, k, :], raw2[:, r, k, :], ACT.Copy, scale=lnw[:, e, k:k + 1])
                ins.then_inc(s.w2_scaled, 1)
                act.activation(v.W1[:, e, 0, 0, :], raw1[:, r, 0, :], ACT.Copy, scale=WS)
                act.activation(v.W1[0:HD, e, 0, 1, :], raw1[0:HD, r, 1, :], ACT.Copy, scale=WS).then_inc(s.w1_hi, 1)
                act.wait_ge(s.centred, e + 1)
                act.activation(v.W2[:, e, 0], w2c[:, e % 2], ACT.Copy, scale=WS).then_inc(s.w2_hi, 1)

        @block.tensor
        def _(pe):
            pe.wait_ge(s.ld_const, 6 * 16)
            pe.wait_ge(s.ld_ln, 2 * 16)
            pe.wait_ge(s.ld_small, 7 * 16)
            n = E * FK
            for k in range(2):
                pe.transpose(bank[3][:, k * n:(k + 1) * n], ln_rows[:, k, :], v.ident[0:n, 0:n])
            pe.transpose(bank[3][0:HD, 2 * n:2 * n + 6], col_rows[:], v.ident[0:6, 0:6]).then_inc(s.turned, 1)
            pe.wait_ge(s.ids_clean, 1)
            for k in range(2):
                mm = pe.transpose(bank[4][:, k * NT:(k + 1) * NT], idf[:, k, :], v.ident[0:NT, 0:NT])
            mm.then_inc(s.turned, 1)
            pe.wait_ge(s.diag_ok, 1)
            for e in range(E):
                r = e % RING
                pe.wait_ge(ld_e[r], (e // RING + 1) * 48)
                for k in range(FK):
                    mm = pe.matmul(bank[0][0:E, 0:D], lnb_diag[:, e, k, :], raw2[:, r, k, :],
                                   start=(e == 0 and k == 0), stop=(e == E - 1 and k == FK - 1))
                mm.then_inc(s.raw2_read, 1)
                pe.wait_ge(s.w2_scaled, e + 1)
                if e >= 2:
                    pe.wait_ge(s.centred, e - 1)
                for k in range(FK):
                    mm = pe.matmul(bank[1 + e % 2][:, 0:D], v.ones, w2c[:, e % 2, k, :],
                                   start=(k == 0), stop=(k == FK - 1))
                mm.then_inc(s.col_sum, 1)
            pe.wait_ge(s.col_sum, E)
            pe.sem_inc(s.b2_sum, 1)

        @block.gpsimd
        def _(pool):
            pool.memset(v.segw[:], 0.0).then_inc(s.seg_clear, 1)
            pool.memset(v.neghalf[:], -0.5)
            pool.memset(v.chosen[:], 0.0)

        @block.vector
        def _(dve):
            n = [0]

            def link(ins):
                n[0] += 1
                ins.then_inc(s.chain, 1)
                dve.wait_ge(s.chain, n[0])

            dve.wait_ge(s.ld_const, 6 * 16)
            link(dve.tensor_copy(v.ident16[:], v.ident))
            dve.wait_ge(s.ld_ids, 2 * 16)
            for k, size in enumerate((VOCAB, NSEG)):
                link(dve.tensor_copy(idf[:, k], id_rows[:, k]))
                link(dve.tensor_scalar(idg[:], idf[:, k], 0.0, float(size), ALU.is_lt, ALU.mult))
                link(dve.tensor_tensor(idf[:, k], idf[:, k], idg[:], ALU.add))
                link(dve.tensor_scalar(idf[:, k], idf[:, k], 0.0, float(size - 1), ALU.max, ALU.min))
            dve.sem_inc(s.ids_clean, 1)
            dve.wait_ge(s.turned, 1)
            n2 = 2 * E * FK
            link(dve.tensor_copy(lnT[:].rearrange("p a n -> p (a n)"), bank[3][:, 0:n2]))
            link(dve.tensor_copy(cols[:].rearrange("d a k -> d (a k)"), bank[3][0:HD, n2:n2 + 4]))
            link(dve.tensor_copy(v.fcol[:], bank[3][0:HD, n2 + 4:n2 + 6]))
            dve.sem_inc(s.turned_ok, 1)
            eye = v.rows[:, 0:E]
            for e in range(E):
                for k in range(FK):
                    ins = dve.tensor_scalar(lnb_diag[:, e, k, :], eye, float(e), lnb[:, e, k:k + 1],
                                            ALU.is_equal, ALU.mult)
            ins.then_inc(s.diag_ok, 1)
            dve.wait_ge(s.turned, 2)

            def by_group(k):
                return bank[4][:, k * NT:(k + 1) * NT].rearrange("p (b c) -> p c b", b=NB)
            link(dve.tensor_copy(v.tok_id[:], by_group(0)))
            link(dve.tensor_copy(seg_id[:], by_group(1)))
            for k in range(NSEG):
                link(dve.tensor_scalar(v.seg_hot[:, :, :, k], seg_id[:], float(k), None, ALU.is_equal))
            dve.wait_ge(s.tanh_ok, 1)
            link(dve.tensor_scalar(dec[:, 2, :], dec[:, 1, :], 0.325, 0.625, ALU.mult, ALU.add))
            link(dve.tensor_scalar(dec[:, 2, :], dec[:, 2, :], 1e-5, 0.999, ALU.max, ALU.min))
            dve.tensor_scalar(dec[:, 4, :], dec[:, 2, :], -1.0, 1.0, ALU.mult, ALU.add).then_inc(s.decay_in, 1)
            dve.wait_ge(s.ln_ok, 1)
            logd = dec[:, 3:4, :].broadcast_to([P, NG, H])
            lp = v.lpos[:, 0:NG].rearrange("p (c o) -> p c o", o=1).broadcast_to([P, NG, H])
            dve.tensor_tensor(df[:], logd, lp, ALU.mult).then_inc(s.df_in, 1)
            dve.wait_ge(s.df_ok, 1)
            dve.tensor_copy(v.scale[:, :, 0:H], df[:])
            link(dve.tensor_scalar(dfe[:], df[:], 1e-8, None, ALU.add))
            link(dve.reciprocal(dfe[:], dfe[:]))
            dt_b = dec[:, 4:5, :].broadcast_to([P, NG, H])
            link(dve.tensor_tensor(v.scale[:, :, H:], dfe[:], dt_b, ALU.mult))
            hf = DH // 2
            for k in range(2):
                for c in range(2):
                    link(dve.tensor_tensor(v.rope[:, k, c], cs[:, k],
                                           qkn[:, c:c + 1, :].broadcast_to([P, NG, DH]), ALU.mult))
            dve.wait_ge(s.ld_w, 9 * 16)
            for k in range(2):
                dve.tensor_scalar(v.wcomp[:, k], v.wcomp[:, k], cols[:, 0, k:k + 1], None, ALU.mult)
                dve.tensor_scalar(v.wproj[:, k], v.wproj[:, k], cols[:, 1, k:k + 1], 0.5, ALU.mult, ALU.mult)
            for e in range(E):
                r, m = e % RING, e % 2
                dve.wait_ge(s.col_sum, e + 1)
                total = bank[1 + m][:, 0:D].rearrange("p (o n) -> p o n", o=1).broadcast_to([P, FK, D])
                dve.scalar_tensor_tensor(w2c[:, m], total, -1.0 / FH, w2c[:, m],
                                         ALU.mult, ALU.add).then_inc(s.centred, 1)
                dve.wait_ge(s.w1_hi, e + 1)
                dve.scalar_tensor_tensor(v.W1[:, e, 1, 0, :], raw1[:, r, 0, :], WS, v.W1[:, e, 0, 0, :],
                                         ALU.mult, ALU.subtract)
                dve.scalar_tensor_tensor(v.W1[0:HD, e, 1, 1, :], raw1[0:HD, r, 1, :], WS, v.W1[0:HD, e, 0, 1, :],
                                         ALU.mult, ALU.subtract).then_inc(s.w1_lo, 1)
                dve.wait_ge(s.w2_hi, e + 1)
                dve.scalar_tensor_tensor(v.W2[:, e, 1], w2c[:, m], WS, v.W2[:, e, 0],
                                         ALU.mult, ALU.subtract).then_inc(s.w2_lo, 1)
            dve.wait_ge(s.b2_sum, 1)
            dve.wait_ge(s.ld_b2, 16)
            dve.tensor_tensor(v.B2[:], bank[0][0:E, 0:D], b2[:], ALU.add).then_inc(s.b2_ok, 1)
            dve.wait_ge(s.w2_lo, E)
            dve.wait_ge(s.b2_ok, 1)


def embed(nc, sbuf, sems, prime, bank, v):
    v = named("Shared", v)
    with ExitStack() as ctx:
        tok = sbuf(ctx, "tok", [P, 2, G, D])
        NS = NB * NSEG
        hotS = sbuf(ctx, "hotS", [P, NS])
        hotT = sbuf(ctx, "hotT", [NS, P])
        stat = sbuf(ctx, "stat", [P, G, 6])
        mv = sbuf(ctx, "mv", [P, G, 2])
        va, rs, r2, m2, m2e, p2 = (sbuf(ctx, n, [P, G]) for n in ("va", "rs", "r2", "m2", "m2e", "p2"))
        xs = sbuf(ctx, "xs", [P, G, D])
        xT = sbuf(ctx, "xT", [HD, 2, G * P])
        latS = sbuf(ctx, "latS", [P, G * P])
        s = sems("tok0", "tok1", "seg_one", "seg_T", "seg_Ts", "seg_mm", "pos_add", "h_ok", "stats", "moments", "va_ok", "rs_ok",
                 "r2_ok", "m2_ok", "m2e_ok", "p2_ok", "x_ok", "xs_ok", "xT_mm", "xT_a", "xT_v", "lat_mm",
                 "lat_ok", "lat_kept", "par_mm", "par_ok")
        block = ctx.enter_context(nc.Block())
        own = dict(
            dve=(s.seg_one, s.pos_add, s.h_ok, s.stats, s.moments, s.x_ok, s.xT_v, s.par_ok),
            act=(s.seg_Ts, s.xs_ok, s.xT_a, s.lat_ok), pe=(s.seg_T, s.seg_mm, s.xT_mm, s.lat_mm, s.par_mm),
            pool=(s.va_ok, s.rs_ok, s.r2_ok, s.m2_ok, s.m2e_ok, s.p2_ok, s.lat_kept))

        @block.gpsimd
        def _(pool):
            prime(pool, *own["pool"])

            def gather(c, slot):
                for b in range(NB):
                    pool.indirect_dma_start(
                        tok[:, slot, b, :], None, v.tok_table,
                        bass.IndirectOffsetOnAxis(ap=v.tok_id[:, c, b:b + 1], axis=0)).then_inc(
                            (s.tok0, s.tok1)[slot], 16)

            def norm(i):
                var = mv[:, :, 1]
                wait_alone(pool, s.moments, done(i, G, G - 1))
                pool.wait_ge(s.xs_ok, prev(i, G))
                pool.tensor_scalar(va[:], var, 1e-5, None, ALU.add).then_inc(s.va_ok, 1)
                pool.wait_ge(s.va_ok, done(i))
                pool.tensor_tensor(rs[:], va[:], v.neghalf[:, 0:G], ALU.pow).then_inc(s.rs_ok, 1)
                pool.wait_ge(s.rs_ok, done(i))
                pool.tensor_tensor(r2[:], rs[:], rs[:], ALU.mult).then_inc(s.r2_ok, 1)
                pool.wait_ge(s.r2_ok, done(i))
                pool.tensor_tensor(m2[:], r2[:], var, ALU.mult).then_inc(s.m2_ok, 1)
                wait_alone(pool, s.m2_ok, done(i))
                pool.tensor_scalar(m2e[:], m2[:], 1e-6, None, ALU.add).then_inc(s.m2e_ok, 1)
                pool.wait_ge(s.m2e_ok, done(i))
                pool.tensor_tensor(p2[:], m2e[:], v.neghalf[:, 0:G], ALU.pow).then_inc(s.p2_ok, 1)

            def keep(i):
                pool.wait_ge(s.lat_ok, done(i))
                pool.tensor_copy(v.latT[:, bass.ds(i * (G * P), G * P)], latS[:]).then_inc(s.lat_kept, 1)

            gather(0, 0)
            gather(1, 1)
            for c in range(NG):
                norm(c)
                keep(c)
                if c + 2 < NG:
                    pool.wait_ge(s.h_ok, done(c, 2, 1))
                    gather(c + 2, c % 2)

        @block.vector
        def _(dve):
            prime(dve, *own["dve"])

            def group(i, slot, turn):
                dve.wait_ge(s.seg_T, prev(i))
                dve.tensor_copy(hotS[:], v.seg_hot[:, bass.ds(i, 1), :, :].rearrange("p o b k -> p (o b k)")
                                ).then_inc(s.seg_one, 1)
                dve.wait_ge((s.tok0, s.tok1)[slot], (turn + 1) * (NB * 16))
                t = tok[:, slot]
                dve.tensor_tensor(t, t, v.pos[:, bass.ds(i, 1), :].broadcast_to([P, G, D]),
                                  ALU.add).then_inc(s.pos_add, 1)
                dve.wait_ge(s.pos_add, done(i))
                dve.wait_ge(s.seg_mm, done(i))
                for k in range(2):
                    dve.tensor_tensor(v.hbuf[:, bass.ds(i * G + 2 * k, 2), :], t[:, 2 * k:2 * k + 2, :],
                                      bank[k][:, 0:2 * D].rearrange("p (b d) -> p b d", b=2),
                                      ALU.add).then_inc(s.h_ok, 1)
                wait_alone(dve, s.h_ok, done(i, 2, 1))
                h = [v.hbuf[:, bass.ds(i * G + b, 1), :].rearrange("p o d -> p (o d)") for b in range(G)]
                for b in range(G):
                    dve.bn_stats(stat[:, b, :], h[b]).then_inc(s.stats, 1)
                for b in range(G):
                    wait_alone(dve, s.stats, done(i, G, b))
                    dve.bn_aggr(mv[:, b, :], stat[:, b, :]).then_inc(s.moments, 1)
                dve.wait_ge(s.rs_ok, done(i))
                for b in range(G):
                    dve.tensor_scalar(v.x1buf[:, bass.ds(i * G + b, 1), :].rearrange("p o d -> p (o d)"), h[b],
                                      mv[:, b, 0:1], rs[:, b:b + 1], ALU.subtract, ALU.mult).then_inc(s.x_ok, 1)
                dve.wait_ge(s.xT_mm, done(i))
                dve.tensor_copy(xT[:, 1, :], bank[3][0:HD, :]).then_inc(s.xT_v, 1)
                dve.wait_ge(s.par_mm, done(i))
                dve.tensor_copy(v.params[:, bass.ds(i * G, G), :],
                                bank[5][:, 0:G * 4 * H].rearrange("p (b n) -> p b n", b=G)).then_inc(s.par_ok, 1)

            with dve.Fori(0, NG // 2, 1) as j:
                group(j * 2, 0, j)
                group(j * 2 + 1, 1, j)

        @block.scalar
        def _(act):
            prime(act, *own["act"])
            with act.Fori(0, NG, 1) as i:
                act.wait_ge(s.seg_T, done(i))
                act.wait_ge(s.seg_mm, prev(i))
                act.activation(hotT[:], bank[6][0:NS, 0:P], ACT.Copy).then_inc(s.seg_Ts, 1)
                act.wait_ge(s.p2_ok, done(i))
                act.wait_ge(s.xT_mm, prev(i))
                for b in range(G):
                    act.wait_ge(s.x_ok, done(i, G, b))
                    act.activation(xs[:, b, :], v.x1buf[:, bass.ds(i * G + b, 1), :].rearrange("p o d -> p (o d)"),
                                   ACT.Copy, scale=p2[:, b:b + 1]).then_inc(s.xs_ok, 1)
                act.wait_ge(s.xT_mm, done(i))
                act.activation(xT[:, 0, :], bank[2][0:HD, :], ACT.Copy).then_inc(s.xT_a, 1)
                act.wait_ge(s.lat_mm, done(i))
                act.wait_ge(s.lat_kept, prev(i))
                act.wait_ge(s.par_mm, prev(i))
                act.activation(latS[:], bank[4][:], ACT.Silu).then_inc(s.lat_ok, 1)

        @block.tensor
        def _(pe):
            prime(pe, *own["pe"])
            with pe.Fori(0, NG, 1) as i:
                pe.wait_ge(s.seg_one, done(i))
                pe.wait_ge(s.seg_Ts, prev(i))
                pe.transpose(bank[6][0:NS, 0:P], hotS[:], v.ident).then_inc(s.seg_T, 1)
                pe.wait_ge(s.seg_Ts, done(i))
                pe.wait_ge(s.h_ok, prev(i, 2))
                for k in range(2):
                    mm = pe.matmul(bank[k][:, 0:2 * D], hotT[:],
                                   v.segw[:, 2 * k:2 * k + 2, :].rearrange("s b d -> s (b d)"), start=True, stop=True)
                mm.then_inc(s.seg_mm, 1)
                pe.wait_ge(s.xT_a, prev(i))
                pe.wait_ge(s.xT_v, prev(i))
                for b in range(G):
                    pe.wait_ge(s.xs_ok, done(i, G, b))
                    for k in range(2):
                        mm = pe.transpose(bank[2 + k][0:HD, b * P:(b + 1) * P], xs[:, b, k * HD:(k + 1) * HD], v.ident)
                mm.then_inc(s.xT_mm, 1)
                pe.wait_ge(s.xT_a, done(i))
                pe.wait_ge(s.xT_v, done(i))
                pe.wait_ge(s.lat_ok, prev(i))
                for k in range(2):
                    mm = pe.matmul(bank[4][:], v.wcomp[:, k, :], xT[:, k, :], start=(k == 0), stop=(k == 1))
                mm.then_inc(s.lat_mm, 1)
                pe.wait_ge(s.lat_ok, done(i))
                pe.wait_ge(s.par_ok, prev(i))
                for b in range(G):
                    mm = pe.matmul(bank[5][:, b * 4 * H:(b + 1) * 4 * H], latS[:, b * P:(b + 1) * P], v.wreso[:],
                                   start=True, stop=True)
                mm.then_inc(s.par_mm, 1)


def write_gates(nc, sbuf, sems, v):
    v = named("Shared", v)
    n = NT * H
    with ExitStack() as ctx:
        th = sbuf(ctx, "th", [P, NT * H, 4])
        ph = sbuf(ctx, "ph", [P, n])
        amp = sbuf(ctx, "amp", [P, n])
        s = sems("g_tanh", "g_phase", "g_sin", "g_cos", "g_chain", "g_prod", "g_sig", "g_ok")
        block = ctx.enter_context(nc.Block())

        @block.scalar
        def _(act):
            act.activation(th[:].rearrange("p n k -> p (n k)"), v.params[:].rearrange("p t n -> p (t n)"),
                           ACT.Tanh, scale=0.5).then_inc(s.g_tanh, 1)
            act.wait_ge(s.g_phase, 1)
            act.activation(ph[:], ph[:], ACT.Sin, scale=PI / 4).then_inc(s.g_sin, 1)
            act.wait_ge(s.g_prod, 1)
            act.activation(amp[:], amp[:], ACT.Tanh, scale=v.temp[:, 0:1]).then_inc(s.g_sig, 1)

        @block.vector
        def _(dve):
            dve.wait_ge(s.g_tanh, 1)
            dve.tensor_tensor(ph[:], th[:, :, 1], th[:, :, 3], ALU.subtract).then_inc(s.g_phase, 1)
            dve.tensor_scalar(amp[:], th[:, :, 2], 1.0, None, ALU.add).then_inc(s.g_chain, 1)
            dve.wait_ge(s.g_chain, 1)
            dve.scalar_tensor_tensor(amp[:], th[:, :, 0], 1.0, amp[:], ALU.add, ALU.mult).then_inc(s.g_chain, 1)
            dve.wait_ge(s.g_sin, 1)
            dve.tensor_tensor(ph[:], ph[:], ph[:], ALU.mult).then_inc(s.g_cos, 1)
            dve.wait_ge(s.g_cos, 1)
            dve.tensor_scalar(ph[:], ph[:], -0.25, 0.125, ALU.mult, ALU.add).then_inc(s.g_cos, 1)
            dve.wait_ge(s.g_cos, 2)
            dve.wait_ge(s.g_chain, 2)
            dve.tensor_tensor(amp[:], amp[:], ph[:], ALU.mult).then_inc(s.g_prod, 1)
            dve.wait_ge(s.g_sig, 1)
            dve.tensor_scalar(amp[:], amp[:], 0.6, 0.5, ALU.mult, ALU.add).then_inc(s.g_chain, 1)
            dve.wait_ge(s.g_chain, 3)
            dve.tensor_scalar(v.gates[:].rearrange("p t h -> p (t h)"), amp[:], 0.05, 0.95,
                              ALU.max, ALU.min).then_inc(s.g_ok, 1)
            dve.wait_ge(s.g_ok, 1)


def attend(nc, sbuf, sems, prime, bank, v):
    v = named("Shared", v)
    NQ = 2 * H
    HB = H // 4
    hf = DH // 2
    with ExitStack() as ctx:
        latA = sbuf(ctx, "latA", [P, G * P])
        ssum = sbuf(ctx, "ssum", [P, NQ])
        ms = sbuf(ctx, "ms", [P, NQ])
        rn = sbuf(ctx, "rn", [P, NQ])
        qn = sbuf(ctx, "qn", [P, 2, H, DH])
        t1 = sbuf(ctx, "t1", [P, 2, H, DH])
        rot = sbuf(ctx, "rot", [P, NQ, DH])
        neg = sbuf(ctx, "neg", [P, NQ * DH])
        sq = neg
        fpad = sbuf(ctx, "fpad", [P, 2, NQ, 2 * DH])
        vaug = sbuf(ctx, "vaug", [P, 2, H, DV])
        og = sbuf(ctx, "og", [P, 2, D])
        qkT = sbuf(ctx, "qkT", [P, 2, HB * P])
        att = sbuf(ctx, "att", [P, 4, HB * P])
        state = sbuf(ctx, "state", [P, NB, HB * 4 * DV])
        stmp = sbuf(ctx, "stmp", [P, HB * 4 * DV])
        bd = sbuf(ctx, "bd", [P, HB, 4, DV])
        den = sbuf(ctx, "den", [P, H])
        rden = sbuf(ctx, "rden", [P, H])
        on = sbuf(ctx, "on", [P, D])
        osq = sbuf(ctx, "osq", [P, D])
        oss = sbuf(ctx, "oss", [P, 1])
        oms = sbuf(ctx, "oms", [P, 1])
        orn = sbuf(ctx, "orn", [P, 1])
        oT = sbuf(ctx, "oT", [HD, 2 * P])
        upd = sbuf(ctx, "upd", [P, D])
        s = sems("a_zero", "a_lat", "a_qk", "a_vo", "a_sq", "a_sum", "a_ms", "a_rn", "a_qn", "a_t1", "a_t2",
                 "a_rot", "a_neg", "a_exp", "a_f", "a_fp", "a_vaug", "a_tanh", "a_og", "a_T", "a_qT", "a_kT",
                 "a_s", "a_mask", "a_supd", "a_stmp", "a_state", "a_o", "a_den", "a_rden", "a_on", "a_osq",
                 "a_oms", "a_orn", "a_oT", "a_oTs", "a_proj", "a_upd", "a_x1")
        own = dict(
            dve=(s.a_lat, s.a_sum, s.a_qn, s.a_t1, s.a_t2, s.a_rot, s.a_neg, s.a_f, s.a_fp, s.a_vaug, s.a_og,
                 s.a_qT, s.a_mask, s.a_stmp, s.a_state, s.a_den, s.a_rden, s.a_on, s.a_oTs, s.a_upd),
            act=(s.a_sq, s.a_exp, s.a_tanh, s.a_kT, s.a_osq),
            pe=(s.a_qk, s.a_vo, s.a_T, s.a_s, s.a_supd, s.a_o, s.a_oT, s.a_proj),
            pool=(s.a_ms, s.a_rn, s.a_oms, s.a_orn, s.a_x1))
        QK, VO, TQ, TK, S0, S1, OB, RB = bank
        block = ctx.enter_context(nc.Block())

        @block.gpsimd
        def _(pool):
            prime(pool, *own["pool"])
            pool.memset(fpad[:], 0.0).then_inc(s.a_zero, 1)
            pool.memset(state[:], 0.0).then_inc(s.a_zero, 1)
            pool.memset(bd[:], 1.0).then_inc(s.a_zero, 1)
            pool.wait_ge(s.a_zero, 3)
            pool.affine_select(out=bd[:], in_=bd[:], compare_op=ALU.is_ge, fill=0.0, base=0,
                               pattern=[[0, HB], [-2 * DH, 4], [0, DV]], channel_multiplier=1).then_inc(s.a_zero, 1)
            pool.wait_ge(s.a_zero, 4)
            pool.affine_select(out=bd[:], in_=bd[:], compare_op=ALU.is_ge, fill=0.0, base=DH - 1,
                               pattern=[[0, HB], [2 * DH, 4], [0, DV]], channel_multiplier=-1).then_inc(s.a_zero, 1)

            def head_norm(i, b):
                wait_alone(pool, s.a_sum, done(i, NB, b))
                pool.tensor_scalar(ms[:], ssum[:], 1.0 / DH, 1e-6, ALU.mult, ALU.add).then_inc(s.a_ms, 1)
                pool.wait_ge(s.a_ms, done(i, NB, b))
                pool.wait_ge(s.a_qn, done(i, NB, b - 1))
                pool.tensor_tensor(rn[:], ms[:], v.neghalf[:, 0:NQ], ALU.pow).then_inc(s.a_rn, 1)

            with pool.Fori(0, NG, 1) as i:
                head_norm(i, 0)
                for b in range(NB):
                    if b + 1 < NB:
                        head_norm(i, b + 1)
                    wait_alone(pool, s.a_osq, done(i, NB, b))
                    pool.tensor_scalar(oms[:], oss[:], 1.0 / D, 1e-6, ALU.mult, ALU.add).then_inc(s.a_oms, 1)
                    pool.wait_ge(s.a_oms, done(i, NB, b))
                    pool.wait_ge(s.a_upd, done(i, NB, b - 1))
                    pool.tensor_tensor(orn[:], oms[:], v.neghalf[:, 0:1], ALU.pow).then_inc(s.a_orn, 1)
                    pool.wait_ge(s.a_upd, done(i, NB, b))
                    xr = v.x1buf[:, bass.ds(i * NB + b, 1), :].rearrange("p o d -> p (o d)")
                    pool.tensor_tensor(xr, xr, upd[:], ALU.add).then_inc(s.a_x1, 1)

        @block.scalar
        def _(act):
            prime(act, *own["act"])

            def front(i, b):
                act.wait_ge(s.a_qk, done(i, NB, b))
                act.wait_ge(s.a_f, done(i, NB, b - 1))
                act.activation(sq[:], QK[:, 0:2 * D], ACT.Square).then_inc(s.a_sq, 1)
                act.wait_ge(s.a_neg, done(i, NB, b))
                act.activation(neg[:], neg[:], ACT.Exp).then_inc(s.a_exp, 1)
                act.wait_ge(s.a_vaug, done(i, NB, b))
                act.wait_ge(s.a_upd, done(i, NB, b - 2))
                act.activation(og[:, b % 2], VO[:, D:2 * D], ACT.Tanh, scale=0.5).then_inc(s.a_tanh, 1)

            with act.Fori(0, NG, 1) as i:
                front(i, 0)
                for b in range(NB):
                    act.wait_ge(s.a_T, done(i, NB, b))
                    act.wait_ge(s.a_o, done(i, NB, b - 1))
                    act.activation(qkT[:, 1, :], TK[:, 0:HB * P], ACT.Copy).then_inc(s.a_kT, 1)
                    if b + 1 < NB:
                        front(i, b + 1)
                    act.wait_ge(s.a_on, done(i, NB, b))
                    act.wait_ge(s.a_oms, done(i, NB, b - 1))
                    act.activation(osq[:], on[:], ACT.Square, accum_out=oss[:]).then_inc(s.a_osq, 1)

        @block.tensor
        def _(pe):
            prime(pe, *own["pe"])

            def project(i, b):
                lat = latA[:, b * P:(b + 1) * P]
                pe.wait_ge(s.a_qn, done(i, NB, b - 1))
                pe.matmul(QK[:, 0:2 * D], lat, v.wqkv[:, 0:2 * D], start=True, stop=True).then_inc(s.a_qk, 1)
                pe.wait_ge(s.a_vaug, done(i, NB, b - 1))
                pe.wait_ge(s.a_og, done(i, NB, b - 1))
                pe.matmul(VO[:, 0:D], lat, v.wqkv[:, 2 * D:3 * D], start=True, stop=True)
                pe.matmul(VO[:, D:2 * D], lat, v.wog[:], start=True, stop=True).then_inc(s.a_vo, 1)

            def head_scores(i, b, half):
                pe.wait_ge(s.a_mask, done(i, 4 * NB, 4 * b + 2 * half - 1))
                for g in range(HB):
                    for jj in range(2):
                        j = 2 * half + jj
                        r = slice(32 * j, 32 * j + DH)
                        mm = pe.matmul((S0, S1)[jj][:, g * P:(g + 1) * P], qkT[r, 1, g * P:(g + 1) * P],
                                       qkT[r, 0, g * P:(g + 1) * P], start=True, stop=True)
                mm.then_inc(s.a_s, 1)

            def tail(i, b):
                pe.wait_ge(s.a_on, done(i, NB, b))
                pe.wait_ge(s.a_upd, done(i, NB, b - 1))
                for k in range(2):
                    mm = pe.transpose(RB[0:HD, k * P:(k + 1) * P], on[:, k * HD:(k + 1) * HD], v.ident)
                mm.then_inc(s.a_oT, 1)
                pe.wait_ge(s.a_oTs, done(i, NB, b))
                for k in range(2):
                    mm = pe.matmul(RB[:, 2 * P:2 * P + D], oT[:, k * P:(k + 1) * P], v.wproj[:, k, :],
                                   start=(k == 0), stop=(k == 1))
                mm.then_inc(s.a_proj, 1)

            with pe.Fori(0, NG, 1) as i:
                pe.wait_ge(s.a_lat, done(i))
                project(i, 0)
                for b in range(NB):
                    pe.wait_ge(s.a_fp, done(i, NB, b))
                    pe.wait_ge(s.a_qT, done(i, NB, b - 1))
                    pe.wait_ge(s.a_kT, done(i, NB, b - 1))
                    for k, t in enumerate((TQ, TK)):
                        for g in range(HB):
                            blk = fpad[:, b % 2, k * H + 4 * g:k * H + 4 * g + 4, :].rearrange("p h d -> p (h d)")
                            mm = pe.transpose(t[:, g * P:(g + 1) * P], blk, v.ident)
                    mm.then_inc(s.a_T, 1)
                    if b + 1 < NB:
                        project(i, b + 1)
                    pe.wait_ge(s.a_qT, done(i, NB, b))
                    pe.wait_ge(s.a_kT, done(i, NB, b))
                    head_scores(i, b, 0)
                    pe.wait_ge(s.a_vaug, done(i, NB, b))
                    pe.wait_ge(s.a_stmp, done(i, NB, b - 1))
                    pe.wait_ge(s.a_on, done(i, NB, b - 1))
                    for g in range(HB):
                        blk = fpad[:, b % 2, H + 4 * g:H + 4 * g + 4, :].rearrange("p h d -> p (h d)")
                        mm = pe.matmul(OB[:, 256 + g * 4 * DV:256 + (g + 1) * 4 * DV], blk,
                                       vaug[:, b % 2, 4 * g:4 * g + 4, :].rearrange("p h d -> p (h d)"),
                                       start=True, stop=True)
                    mm.then_inc(s.a_supd, 1)
                    head_scores(i, b, 1)
                    pe.wait_ge(s.a_state, done(i, NB, b - NB))
                    pe.wait_ge(s.a_stmp, done(i, NB, b))
                    for g in range(HB):
                        pe.matmul(OB[:, g * 4 * DV:(g + 1) * 4 * DV], qkT[:, 0, g * P:(g + 1) * P],
                                  state[:, b, g * 4 * DV:(g + 1) * 4 * DV],
                                  start=(g == 0), stop=False, skip_group_check=True)
                    pe.wait_ge(s.a_mask, done(i, 4 * NB, 4 * b + 3))
                    for h in range(H):
                        g, j = h // 4, h % 4
                        mm = pe.matmul(OB[:, h * DV:(h + 1) * DV], att[:, j, g * P:(g + 1) * P],
                                       vaug[:, b % 2, h, :], start=False, stop=(h == H - 1), skip_group_check=True)
                    mm.then_inc(s.a_o, 1)
                    tail(i, b)

        @block.vector
        def _(dve):
            prime(dve, *own["dve"])
            dve.wait_ge(s.a_zero, 5)
            dve.memset(vaug[:], 1.0)

            def front(i, b):
                dve.wait_ge(s.a_sq, done(i, NB, b))
                dve.wait_ge(s.a_ms, done(i, NB, b - 1))
                dve.tensor_reduce(ssum[:], sq[:].rearrange("p (h d) -> p h d", d=DH), AX.X, ALU.add).then_inc(s.a_sum, 1)
                dve.wait_ge(s.a_vo, done(i, NB, b))
                dve.wait_ge(s.a_o, done(i, NB, b - 2))
                dve.tensor_tensor(vaug[:, b % 2, :, 0:DH], VO[:, 0:D].rearrange("p (h d) -> p h d", d=DH),
                                  v.gates[:, bass.ds(i * NB + b, 1), :].rearrange("p o (h u) -> p (o h) u", u=1)
                                  .broadcast_to([P, H, DH]), ALU.mult).then_inc(s.a_vaug, 1)
                dve.wait_ge(s.a_rn, done(i, NB, b))
                qk = QK[:, 0:2 * D].rearrange("p (h d) -> p h d", d=DH)
                dve.tensor_tensor(qn[:].rearrange("p a h d -> p (a h) d"), qk,
                                  rn[:].rearrange("p (h u) -> p h u", u=1).broadcast_to([P, NQ, DH]),
                                  ALU.mult).then_inc(s.a_qn, 1)
                dve.wait_ge(s.a_qn, done(i, NB, b))

                def table(k):
                    return v.rope[:, k, :, bass.ds(i, 1), :].broadcast_to([P, 2, H, DH])
                dve.tensor_tensor(t1[:], qn[:], table(0), ALU.mult).then_inc(s.a_t1, 1)
                dve.tensor_tensor(qn[:], qn[:], table(1), ALU.mult).then_inc(s.a_t2, 1)
                dve.wait_ge(s.a_t1, done(i, NB, b))
                dve.wait_ge(s.a_t2, done(i, NB, b))
                a = t1[:].rearrange("p a h d -> p (a h) d")
                c = qn[:].rearrange("p a h d -> p (a h) d")
                dve.tensor_tensor(rot[:, :, 0:hf], a[:, :, 0:hf], c[:, :, hf:], ALU.add).then_inc(s.a_rot, 1)
                dve.tensor_tensor(rot[:, :, hf:], a[:, :, hf:], c[:, :, 0:hf], ALU.add).then_inc(s.a_rot, 1)
                dve.wait_ge(s.a_rot, done(i, 2 * NB, 2 * b + 1))
                rflat = rot[:].rearrange("p h d -> p (h d)")
                dve.tensor_scalar(neg[:], rflat, 0.0, None, ALU.min).then_inc(s.a_neg, 1)
                dve.wait_ge(s.a_exp, done(i, NB, b))
                dve.scalar_tensor_tensor(rflat, rflat, 0.0, neg[:], ALU.max, ALU.add).then_inc(s.a_f, 1)
                dve.wait_ge(s.a_f, done(i, NB, b))
                dve.wait_ge(s.a_supd, done(i, NB, b - 2))
                dve.tensor_tensor(fpad[:, b % 2, :, 0:DH], rot[:],
                                  v.scale[:, bass.ds(i, 1), :].rearrange("p o (h u) -> p (o h) u", u=1)
                                  .broadcast_to([P, NQ, DH]), ALU.mult).then_inc(s.a_fp, 1)
                dve.wait_ge(s.a_tanh, done(i, NB, b))
                dve.scalar_tensor_tensor(og[:, b % 2], og[:, b % 2], 1.0, VO[:, D:2 * D],
                                         ALU.add, ALU.mult).then_inc(s.a_og, 1)

            def mask(i, b, half):
                dve.wait_ge(s.a_s, done(i, 2 * NB, 2 * b + half))
                if half == 0:
                    dve.wait_ge(s.a_o, done(i, NB, b - 1))
                for jj in range(2):
                    dve.tensor_tensor(att[:, 2 * half + jj, :].rearrange("p (g n) -> p g n", g=HB),
                                      (S0, S1)[jj][:, 0:HB * P].rearrange("p (g n) -> p g n", g=HB),
                                      v.causal.rearrange("p (o n) -> p o n", o=1).broadcast_to([P, HB, P]),
                                      ALU.mult).then_inc(s.a_mask, 1)

            with dve.Fori(0, NG, 1) as i:
                dve.wait_ge(s.a_vo, prev(i, NB))
                dve.tensor_copy(latA[:], v.latT[:, bass.ds(i * (G * P), G * P)]).then_inc(s.a_lat, 1)
                front(i, 0)
                for b in range(NB):
                    dve.wait_ge(s.a_T, done(i, NB, b))
                    dve.wait_ge(s.a_o, done(i, NB, b - 1))
                    dve.tensor_copy(qkT[:, 0, :], TQ[:, 0:HB * P]).then_inc(s.a_qT, 1)
                    mask(i, b, 0)
                    dve.wait_ge(s.a_supd, done(i, NB, b))
                    dve.tensor_tensor(stmp[:], OB[:, 256:256 + HB * 4 * DV], bd[:].rearrange("p g j d -> p (g j d)"),
                                      ALU.mult).then_inc(s.a_stmp, 1)
                    mask(i, b, 1)
                    if b + 1 < NB:
                        front(i, b + 1)
                    dve.wait_ge(s.a_o, done(i, NB, b))
                    num = OB[:, 0:H * DV].rearrange("p (h d) -> p h d", d=DV)
                    dve.tensor_scalar(den[:], num[:, :, DH], 1e-5, None, ALU.max).then_inc(s.a_den, 1)
                    dve.tensor_tensor(state[:, b, :], state[:, b, :], stmp[:], ALU.add).then_inc(s.a_state, 1)
                    dve.wait_ge(s.a_den, done(i, NB, b))
                    dve.reciprocal(rden[:], den[:]).then_inc(s.a_rden, 1)
                    dve.wait_ge(s.a_rden, done(i, NB, b))
                    dve.wait_ge(s.a_oT, done(i, NB, b - 1))
                    dve.wait_ge(s.a_osq, done(i, NB, b - 1))
                    dve.tensor_tensor(on[:].rearrange("p (h d) -> p h d", d=DH), num[:, :, 0:DH],
                                      rden[:].rearrange("p (h u) -> p h u", u=1).broadcast_to([P, H, DH]),
                                      ALU.mult).then_inc(s.a_on, 1)
                    dve.wait_ge(s.a_oT, done(i, NB, b))
                    dve.wait_ge(s.a_proj, done(i, NB, b - 1))
                    dve.tensor_copy(oT[:], RB[0:HD, 0:2 * P]).then_inc(s.a_oTs, 1)
                    dve.wait_ge(s.a_proj, done(i, NB, b))
                    dve.wait_ge(s.a_orn, done(i, NB, b))
                    dve.wait_ge(s.a_x1, done(i, NB, b - 1))
                    dve.scalar_tensor_tensor(upd[:], RB[:, 2 * P:2 * P + D], orn[:, 0:1], og[:, b % 2],
                                             ALU.mult, ALU.mult).then_inc(s.a_upd, 1)


def ffn(nc, sbuf, sems, prime, bank, v):
    v = named("Shared", v)
    NH = HID // P
    with ExitStack() as ctx:
        fsq = sbuf(ctx, "fsq", [P, D])
        ss = sbuf(ctx, "ss", [P, G])
        fms = sbuf(ctx, "fms", [P, G])
        frn = sbuf(ctx, "frn", [P, G])
        xn = sbuf(ctx, "xn", [P, G, D])
        xnT = sbuf(ctx, "xnT", [HD, 2, G * P])
        act_a = sbuf(ctx, "act_a", [P, 2, G * P])
        u = sbuf(ctx, "u", [P, NH, G * P])
        stat = sbuf(ctx, "fstat", [P, G, 6])
        mv = sbuf(ctx, "fmv", [P, G, 2])
        va = sbuf(ctx, "fva", [P, G])
        rs = sbuf(ctx, "frs", [P, G])
        xf = sbuf(ctx, "xf", [P, 2, G, D])
        xp = sbuf(ctx, "xp", [P, 2, G, 2 * D], F16)
        xfT = sbuf(ctx, "xfT", [HD + 1, 2, G * P])
        top8 = sbuf(ctx, "top8", [P, G, 8])
        idx8 = sbuf(ctx, "idx8", [P, G, 8], U32)
        sc = sbuf(ctx, "sc", [P, G, E])
        hot = sbuf(ctx, "hot", [P, G, TOPK, E])
        hot_s = sbuf(ctx, "hot_s", [P, G, TOPK, E])
        mask = sbuf(ctx, "mask", [P, G, E])
        before = sbuf(ctx, "before", [P, G, E])
        region = sbuf(ctx, "region", [P, E])
        spare = sbuf(ctx, "spare", [2, E])
        rank = sbuf(ctx, "rank", [P, G, E])
        slot_f = sbuf(ctx, "slot_f", [P, G, TOPK])
        slot_i = sbuf(ctx, "slot_i", [P, 2, G, TOPK], I32)
        s = sems("ld_f", "f_fold", "f_const", "f_sq", "f_ms", "f_rn", "f_xn", "f_xT", "f_xTa", "f_xTv", "f_ab", "f_silu", "f_u",
                 "f_w3", "f_hx", "f_h", "f_stat", "f_mv", "f_va", "f_rs", "f_xf", "f_fT", "f_fTa", "f_fTv",
                 "f_gate", "f_score", "f_top", "f_idx", "f_pick", "f_hot", "f_m1", "f_mask", "f_run", "f_rank",
                 "f_place", "f_hs", "f_slot", "f_keep", "f_int", "f_hi", "f_lo", "f_store0", "f_store1", "f_send0", "f_send1")
        own = dict(
            dve=(s.f_xn, s.f_xTv, s.f_u, s.f_h, s.f_stat, s.f_mv, s.f_xf, s.f_fTv, s.f_score, s.f_top, s.f_idx,
                 s.f_pick, s.f_hot, s.f_m1, s.f_mask, s.f_run, s.f_place, s.f_hs, s.f_slot, s.f_keep, s.f_int, s.f_lo),
            act=(s.f_sq, s.f_xTa, s.f_silu, s.f_fTa, s.f_hi), pe=(s.f_xT, s.f_ab, s.f_w3, s.f_fT, s.f_gate, s.f_rank),
            pool=(s.f_ms, s.f_rn, s.f_hx, s.f_va, s.f_rs), sp=(s.f_store0, s.f_store1))
        XA, XB, A0, B0, A1, B1, Y0, Y1 = bank
        w12 = sbuf(ctx, "w12", [HD, 2, 2 * HID])
        w3s = sbuf(ctx, "w3s", [P, HID // P, D])
        gw = sbuf(ctx, "gw", [HD + 1, 2, E])
        block = ctx.enter_context(nc.Block())

        def row(t, k):
            return t[:, bass.ds(k, 1), :].rearrange("p o d -> p (o d)")

        @block.sync
        def _(sp):
            sp.dma_start(w12[:, :, 0:HID], halves(v.w1)).then_inc(s.ld_f, 16)
            sp.dma_start(w12[:, :, HID:], halves(v.w2)).then_inc(s.ld_f, 16)
            sp.dma_start(w3s[:], v.w3.rearrange("(k p) n -> p k n", p=P)).then_inc(s.ld_f, 16)
            sp.dma_start(gw[0:HD], halves(v.gate_w)).then_inc(s.ld_f, 16)
            sp.dma_start(gw[HD:HD + 1, 0, :], v.gate_b.rearrange("(o n) -> o n", o=1)).then_inc(s.ld_f, 16)
            prime(sp, *own["sp"])
            with sp.Fori(0, NG // 2, 1) as j:
                for half in range(2):
                    i = j * 2 + half
                    store = (s.f_store0, s.f_store1)[half]
                    sp.wait_ge(s.f_lo, done(i))
                    sp.dma_start(v.x_rows[bass.ds(i * (G * P), G * P), :].rearrange("(b p) d -> p b d", p=P),
                                 xp[:, half]).then_inc(store, 16)
            sp.wait_ge(s.f_store0, dma_done(NG // 2 - 1))
            sp.wait_ge(s.f_store1, dma_done(NG // 2 - 1))

        @block.gpsimd
        def _(pool):
            prime(pool, *own["pool"])
            NS = G * TOPK
            for k, send in enumerate((s.f_send0, s.f_send1)):
                pool.dma_start(spare[k:k + 1, :], v.c_rows[:, 0:E]).then_inc(send, 16)

            def send(i, half):
                wait_alone(pool, s.f_int, done(i))
                pool.wait_ge(s.f_lo, done(i))
                for b in range(G):
                    for k in range(TOPK):
                        pool.indirect_dma_start(
                            v.x_rows, bass.IndirectOffsetOnAxis(ap=slot_i[:, half, b, k:k + 1], axis=0),
                            xp[:, half, b, :], None).then_inc((s.f_send0, s.f_send1)[half], 16)

            with pool.Fori(0, NG // 2, 1) as j:
                for half in range(2):
                    i = j * 2 + half
                    wait_alone(pool, s.f_sq, done(i, G, G - 1))
                    pool.tensor_scalar(fms[:], ss[:], 1.0 / D, 1e-6, ALU.mult, ALU.add).then_inc(s.f_ms, 1)
                    pool.wait_ge(s.f_ms, done(i))
                    pool.wait_ge(s.f_xn, prev(i, G))
                    pool.tensor_tensor(frn[:], fms[:], v.neghalf[:, 0:G], ALU.pow).then_inc(s.f_rn, 1)
                    pool.wait_ge(s.f_xn, done(i, G, G - 1))
                    hx = v.hbuf[:, bass.ds(i * G, G), :]
                    pool.tensor_tensor(hx, hx, v.x1buf[:, bass.ds(i * G, G), :], ALU.add).then_inc(s.f_hx, 1)
                    wait_alone(pool, s.f_mv, done(i, G, G - 1))
                    pool.tensor_scalar(va[:], mv[:, :, 1], 1e-5, None, ALU.add).then_inc(s.f_va, 1)
                    pool.wait_ge(s.f_va, done(i))
                    pool.wait_ge(s.f_xf, prev(i, G))
                    pool.tensor_tensor(rs[:], va[:], v.neghalf[:, 0:G], ALU.pow).then_inc(s.f_rs, 1)
                    send(i, half)
            pool.wait_ge(s.f_send0, (NG // 2 * NS + 1) * 16)
            pool.wait_ge(s.f_send1, (NG // 2 * NS + 1) * 16)

        @block.scalar
        def _(act):
            prime(act, *own["act"])
            def group(i, half, j):
                act.wait_ge(s.f_ms, prev(i))
                for b in range(G):
                    act.wait_ge(s.f_sq, done(i, G, b - 1))
                    act.activation(fsq[:], row(v.x1buf, i * G + b), ACT.Square,
                                   accum_out=ss[:, b:b + 1]).then_inc(s.f_sq, 1)
                act.wait_ge(s.f_xT, done(i))
                act.wait_ge(s.f_ab, prev(i, NH))
                act.activation(xnT[:, 0, :], XA[0:HD, :], ACT.Copy).then_inc(s.f_xTa, 1)
                for k in range(NH):
                    act.wait_ge(s.f_ab, done(i, NH, k))
                    act.wait_ge(s.f_u, done(i, NH, k - 2))
                    act.activation(act_a[:, k % 2, :], (A0, A1)[k % 2][:], ACT.Silu).then_inc(s.f_silu, 1)
                act.wait_ge((s.f_send0, s.f_send1)[half], j * (16 * G * TOPK) + 16)
                act.wait_ge((s.f_store0, s.f_store1)[half], prev(j, 16))
                act.wait_ge(s.f_xf, done(i, G, G - 1))
                act.activation(xp[:, half, :, 0:D], xf[:, half], ACT.Copy).then_inc(s.f_hi, 1)
                act.wait_ge(s.f_fT, done(i))
                act.wait_ge(s.f_gate, prev(i))
                act.activation(xfT[0:HD, 0, :], XA[0:HD, :], ACT.Copy).then_inc(s.f_fTa, 1)

            with act.Fori(0, NG // 2, 1) as j:
                group(j * 2, 0, j)
                group(j * 2 + 1, 1, j)

        @block.tensor
        def _(pe):
            prime(pe, *own["pe"])
            pe.wait_ge(s.f_const, 1)
            pe.wait_ge(s.f_fold, 2)
            pe.wait_ge(s.ld_f, 5 * 16)

            def turn(src, i, ready, signal):
                for b in range(G):
                    pe.wait_ge(ready, done(i, G, b))
                    for k in range(2):
                        mm = pe.transpose((XA, XB)[k][0:HD, b * P:(b + 1) * P], src[:, b, k * HD:(k + 1) * HD], v.ident)
                mm.then_inc(signal, 1)

            def group(i, half):
                pe.wait_ge(s.f_fTa, prev(i))
                pe.wait_ge(s.f_fTv, prev(i))
                turn(xn, i, s.f_xn, s.f_xT)
                pe.wait_ge(s.f_xTa, done(i))
                pe.wait_ge(s.f_xTv, done(i))
                pe.wait_ge(s.f_score, prev(i))
                pe.wait_ge(s.f_place, prev(i))
                for k in range(NH):
                    pe.wait_ge(s.f_u, done(i, NH, k - 2))
                    for n, dst in enumerate(((A0, A1)[k % 2], (B0, B1)[k % 2])):
                        for c in range(2):
                            w = w12[:, c, n * HID + k * P:n * HID + (k + 1) * P]
                            mm = pe.matmul(dst[:], w, xnT[:, c, :], start=(c == 0), stop=(c == 1))
                    mm.then_inc(s.f_ab, 1)
                pe.wait_ge(s.f_h, prev(i, 2))
                pe.wait_ge(s.f_u, done(i, NH, NH - 1))
                for b in range(G):
                    for k in range(NH):
                        mm = pe.matmul((Y0, Y1)[b // 2][:, (b % 2) * D:(b % 2 + 1) * D], u[:, k, b * P:(b + 1) * P],
                                       w3s[:, k, :], start=(k == 0), stop=(k == NH - 1))
                    if b % 2:
                        mm.then_inc(s.f_w3, 1)
                turn(xf[:, half], i, s.f_xf, s.f_fT)
                pe.wait_ge(s.f_fTa, done(i))
                pe.wait_ge(s.f_fTv, done(i))
                for b in range(G):
                    pe.matmul(A0[:, b * E:(b + 1) * E], xfT[:, 0, b * P:(b + 1) * P], gw[:, 0, :],
                              start=True, stop=False)
                    mm = pe.matmul(A0[:, b * E:(b + 1) * E], xfT[0:HD, 1, b * P:(b + 1) * P], gw[0:HD, 1, :],
                                   start=False, stop=True)
                mm.then_inc(s.f_gate, 1)
                pe.wait_ge(s.f_run, done(i, G, G - 1))
                pe.matmul(B0[:, 0:G * E], v.ones, before[:].rearrange("p b e -> p (b e)"), start=True, stop=False)
                pe.matmul(B0[:, 0:G * E], v.strict, mask[:].rearrange("p b e -> p (b e)"),
                          start=False, stop=True).then_inc(s.f_rank, 1)

            with pe.Fori(0, NG // 2, 1) as j:
                group(j * 2, 0)
                group(j * 2 + 1, 1)

        @block.vector
        def _(dve):
            prime(dve, *own["dve"])
            dve.memset(xfT[HD:HD + 1, :, :], 1.0).then_inc(s.f_const, 1)
            dve.tensor_scalar(region[:], v.rows[:, 0:E], float(REGION), None, ALU.mult)
            dve.wait_ge(s.ld_f, 5 * 16)
            for k in range(2):
                dve.tensor_scalar(w12[:, k], w12[:, k], v.fcol[:, k:k + 1], None, ALU.mult).then_inc(s.f_fold, 1)

            def group(i, half, j):
                dve.wait_ge(s.f_rn, done(i))
                dve.wait_ge(s.f_xT, prev(i))
                for b in range(G):
                    dve.tensor_scalar(xn[:, b, :], row(v.x1buf, i * G + b), frn[:, b:b + 1], None,
                                      ALU.mult).then_inc(s.f_xn, 1)
                dve.wait_ge(s.f_xT, done(i))
                dve.wait_ge(s.f_ab, prev(i, NH))
                dve.tensor_copy(xnT[:, 1, :], XB[0:HD, :]).then_inc(s.f_xTv, 1)
                dve.wait_ge(s.f_w3, prev(i, 2))
                for k in range(NH):
                    dve.wait_ge(s.f_silu, done(i, NH, k))
                    dve.tensor_tensor(u[:, k, :], act_a[:, k % 2, :], (B0, B1)[k % 2][:], ALU.mult).then_inc(s.f_u, 1)
                dve.wait_ge(s.f_hx, done(i))
                for k in range(2):
                    dve.wait_ge(s.f_w3, done(i, 2, k))
                    hh = v.hbuf[:, bass.ds(i * G + 2 * k, 2), :]
                    dve.tensor_tensor(hh, hh, (Y0, Y1)[k][:, 0:2 * D].rearrange("p (b d) -> p b d", b=2),
                                      ALU.add).then_inc(s.f_h, 1)
                for b in range(G):
                    wait_alone(dve, s.f_h, done(i, 2, b // 2))
                    dve.bn_stats(stat[:, b, :], row(v.hbuf, i * G + b)).then_inc(s.f_stat, 1)
                for b in range(G):
                    wait_alone(dve, s.f_stat, done(i, G, b))
                    dve.bn_aggr(mv[:, b, :], stat[:, b, :]).then_inc(s.f_mv, 1)
                dve.wait_ge(s.f_rs, done(i))
                for b in range(G):
                    dve.tensor_scalar(xf[:, half, b, :], row(v.hbuf, i * G + b), mv[:, b, 0:1], rs[:, b:b + 1],
                                      ALU.subtract, ALU.mult).then_inc(s.f_xf, 1)
                dve.wait_ge(s.f_hi, done(i))
                dve.tensor_tensor(xp[:, half, :, D:], xf[:, half], xp[:, half, :, 0:D],
                                  ALU.subtract).then_inc(s.f_lo, 1)
                dve.wait_ge(s.f_fT, done(i))
                dve.wait_ge(s.f_gate, prev(i))
                dve.tensor_copy(xfT[0:HD, 1, :], XB[0:HD, :]).then_inc(s.f_fTv, 1)
                dve.wait_ge(s.f_gate, done(i))
                dve.tensor_copy(sc[:], A0[:, 0:G * E].rearrange("p (b e) -> p b e", b=G)).then_inc(s.f_score, 1)
                dve.wait_ge(s.f_score, done(i))
                dve.tensor_copy(v.scores[:, bass.ds(i * G, G), :], sc[:]).then_inc(s.f_keep, 1)
                for b in range(G):
                    dve.max(top8[:, b, :], sc[:, b, 1:E]).then_inc(s.f_top, 1)
                for b in range(G):
                    wait_alone(dve, s.f_top, done(i, G, b))
                    dve.max_index(idx8[:, b, :], top8[:, b, :], sc[:, b, 1:E]).then_inc(s.f_idx, 1)
                dve.wait_ge(s.f_idx, done(i, G, G - 1))
                pick = v.picked[:, bass.ds(i * G, G), :]
                dve.tensor_scalar(pick, idx8[:, :, 0:TOPK], 1.0, None, ALU.add).then_inc(s.f_pick, 1)
                dve.tensor_copy(v.score3[:, bass.ds(i * G, G), :], top8[:, :, 0:TOPK]).then_inc(s.f_keep, 1)
                dve.wait_ge(s.f_pick, done(i))
                flat = hot[:].rearrange("p b k e -> p (b k) e")
                dve.tensor_tensor(flat,
                                  v.rows[:, 0:E].rearrange("p (o e) -> p o e", o=1).broadcast_to([P, G * TOPK, E]),
                                  pick.rearrange("p b (k u) -> p (b k) u", u=1).broadcast_to([P, G * TOPK, E]),
                                  ALU.is_equal).then_inc(s.f_hot, 1)
                dve.wait_ge(s.f_hot, done(i))
                dve.wait_ge(s.f_rank, prev(i))
                dve.tensor_tensor(mask[:], hot[:, :, 0, :], hot[:, :, 1, :], ALU.add).then_inc(s.f_m1, 1)
                dve.wait_ge(s.f_m1, done(i))
                dve.tensor_tensor(mask[:], mask[:], hot[:, :, 2, :], ALU.add).then_inc(s.f_mask, 1)
                dve.wait_ge(s.f_mask, done(i))
                for b in range(G):
                    if b == 0:
                        dve.tensor_copy(before[:, 0, :], v.chosen[:]).then_inc(s.f_run, 1)
                    else:
                        dve.tensor_tensor(before[:, b, :], before[:, b - 1, :], mask[:, b - 1, :],
                                          ALU.add).then_inc(s.f_run, 1)
                    dve.wait_ge(s.f_run, done(i, G, b))
                dve.tensor_tensor(v.chosen[:], before[:, G - 1, :], mask[:, G - 1, :], ALU.add).then_inc(s.f_keep, 1)
                dve.wait_ge(s.f_rank, done(i))
                dve.tensor_tensor(rank[:], B0[:, 0:G * E].rearrange("p (b e) -> p b e", b=G),
                                  region[:].rearrange("p (o e) -> p o e", o=1).broadcast_to([P, G, E]),
                                  ALU.add).then_inc(s.f_place, 1)
                dve.wait_ge(s.f_place, done(i))
                for k in range(TOPK):
                    dve.tensor_tensor(hot_s[:, :, k, :], hot[:, :, k, :], rank[:], ALU.mult).then_inc(s.f_hs, 1)
                dve.wait_ge(s.f_hs, done(i, TOPK, TOPK - 1))
                dve.tensor_reduce(slot_f[:].rearrange("p b k -> p (b k)"), hot_s[:].rearrange("p b k e -> p (b k) e"),
                                  AX.X, ALU.add).then_inc(s.f_slot, 1)
                dve.wait_ge(s.f_slot, done(i))
                dve.tensor_copy(v.place[:, bass.ds(i * G, G), :], slot_f[:]).then_inc(s.f_keep, 1)
                dve.tensor_copy(slot_i[:, half], slot_f[:]).then_inc(s.f_int, 1)
                dve.wait_ge(s.f_keep, done(i, 4, 3))

            with dve.Fori(0, NG // 2, 1) as j:
                group(j * 2, 0, j)
                group(j * 2 + 1, 1, j)


def experts(nc, sbuf, sems, prime, bank, v):
    v = named("Shared", v)
    with ExitStack() as ctx:
        TILES = NT + RT
        e_of = sbuf(ctx, "e_of", [1, TILES], I32)
        r_of = sbuf(ctx, "r_of", [1, TILES], I32)
        count = sbuf(ctx, "count", [P, E])
        cmp32 = sbuf(ctx, "cmp32", [P, E, NT])
        tiles = sbuf(ctx, "tiles", [P, E])
        ends = sbuf(ctx, "ends", [P, E])
        onesE = sbuf(ctx, "onesE", [P, E])
        cmpT = sbuf(ctx, "cmpT", [1, RT, E])
        cnt = sbuf(ctx, "cnt", [1, 6, RT])
        pad_f = sbuf(ctx, "pad_f", [P, E])
        pad_i = sbuf(ctx, "pad_i", [P, E], I32)
        zero = sbuf(ctx, "zero", [P, 2 * D], F16)
        xin = sbuf(ctx, "xin", [P, 4, 2 * D], F16)
        xT = sbuf(ctx, "exT", [HD + 1, 2, 4, P], F16)
        h = sbuf(ctx, "h", [P, 2, FH])
        hp = sbuf(ctx, "hp", [P, 2, 2, FH], F16)
        hT = sbuf(ctx, "hT", [P, 2, 2, FH], F16)
        st = sbuf(ctx, "est", [P, 2, 6])
        mv = sbuf(ctx, "emv", [P, 4, 2])
        va = sbuf(ctx, "eva", [P, 4])
        rs = sbuf(ctx, "ers", [P, 4])
        y = sbuf(ctx, "y", [P, 4, D])
        s = sems("t_cnt", "t_chain", "t_ok", "t_pad", "t_zero", "t_padded", "e_one",
                 "e_in0", "e_in1", "e_in2", "e_in3", "e_xT", "e_xTs", "e_h", "e_gelu", "e_hi", "e_lo", "e_st",
                 "e_mv", "e_va", "e_rs", "e_hT", "e_hTa", "e_hTv", "e_y", "e_ys", "e_out0", "e_out1", "e_out2",
                 "e_out3")
        e_in = (s.e_in0, s.e_in1, s.e_in2, s.e_in3)
        e_out = (s.e_out0, s.e_out1, s.e_out2, s.e_out3)
        own = dict(dve=(s.e_lo, s.e_st, s.e_mv, s.e_hTv), act=(s.e_xTs, s.e_gelu, s.e_hi, s.e_hTa, s.e_ys),
                   pe=(s.e_xT, s.e_h, s.e_hT, s.e_y), pool=(s.e_va, s.e_rs), sp=e_in + e_out)
        XT, HP, HTA, HTV, YP = bank[0], (bank[1], bank[2]), bank[3], bank[4], (bank[5], bank[6])
        half_bank = lambda a, n: a[:, 0:n // 2].bitcast(F16)
        block = ctx.enter_context(nc.Block())

        def at(n):
            return slice(n, n + 1) if isinstance(n, int) else bass.ds(n, 1)

        def pipeline(eng, step, last):
            def run(q, k):
                def tile(behind):
                    m = k - behind
                    if isinstance(q, int) and not 0 <= q * 4 + m < TILES:
                        return None
                    return q * 4 + m, m % 4, q + m // 4
                step(tile)
            first = (last + 3) // 4
            for n in range(first * 4):
                run(n // 4, n % 4)
            with eng.Fori(first, TILES // 4, 1) as q:
                for k in range(4):
                    run(q, k)
            for n in range(TILES // 4 * 4, TILES + last):
                run(n // 4, n % 4)

        @block.sync
        def _(sp):
            prime(sp, *own["sp"])
            sp.wait_ge(s.t_ok, 1)
            sp.wait_ge(s.t_padded, (E - 1) * 16)

            def step(tile):
                if tile(0):
                    n, k, turn = tile(0)
                    row = sp.value_load(r_of[0:1, at(n)], min_val=0, max_val=(E * REGION - P))
                    sp.wait_ge(s.e_xT, done(n) - 4)
                    sp.dma_start(xin[:, k, :], v.x_rows[bass.ds(row, P), :]).then_inc(e_in[k], 16)
                if tile(8):
                    n, k, turn = tile(8)
                    sp.wait_ge(s.e_ys, done(n))
                    sp.dma_start(v.y_rows[bass.ds(n * P, P), :], y[:, k, :]).then_inc(e_out[k], 16)

            pipeline(sp, step, 8)
            for k in range(4):
                sp.wait_ge(e_out[k], dma_done((TILES - 1 - k) // 4))

        @block.gpsimd
        def _(pool):
            prime(pool, *own["pool"])
            pool.memset(zero[:], 0.0).then_inc(s.t_zero, 1)
            pool.wait_ge(s.t_pad, 1)
            pool.wait_ge(s.t_zero, 1)
            for e in range(1, E):
                pool.indirect_dma_start(v.x_rows, bass.IndirectOffsetOnAxis(ap=pad_i[:, e:e + 1], axis=0),
                                        zero[:], None).then_inc(s.t_padded, 16)

            def step(tile):
                n, k, turn = tile(0)
                scale2 = (WS * HS) ** 2
                wait_alone(pool, s.e_mv, done(n))
                pool.tensor_scalar(va[:, k:k + 1], mv[:, k, 1:2], scale2, 1e-5 * scale2,
                                   ALU.mult, ALU.add).then_inc(s.e_va, 1)
                pool.wait_ge(s.e_va, done(n))
                pool.wait_ge(s.e_ys, done(n) - 4)
                pool.tensor_tensor(rs[:, k:k + 1], va[:, k:k + 1], v.neghalf[:, 0:1], ALU.pow).then_inc(s.e_rs, 1)

            pipeline(pool, step, 0)

        @block.tensor
        def _(pe):
            prime(pe, *own["pe"])
            pe.matmul(bank[7][:, 256:256 + E], v.ones, v.chosen[:], start=True, stop=True).then_inc(s.t_cnt, 1)
            pe.wait_ge(s.e_one, 1)
            pe.wait_ge(s.t_ok, 1)
            pairs = ((0, 0), (0, 1), (1, 0))

            def expert(n):
                return pe.value_load(e_of[0:1, at(n)], min_val=0, max_val=E - 1)

            def step(tile):
                if tile(0):
                    n, k, turn = tile(0)
                    pe.wait_ge(e_in[k], dma_done(turn))
                    pe.wait_ge(s.e_xTs, done(n) - 1)
                    xt = half_bank(XT, 4 * P)
                    for c in range(4):
                        mm = pe.transpose(xt[0:HD, c * P:(c + 1) * P], xin[:, k, c * HD:(c + 1) * HD], v.ident16[:])
                    mm.then_inc(s.e_xT, 1)
                if tile(1):
                    n, k, turn = tile(1)
                    m = k % 2
                    w = v.W1[:, bass.ds(expert(n), 1)].rearrange("p o a c n -> p (o a) c n")
                    pe.wait_ge(s.e_xTs, done(n))
                    pe.wait_ge(s.e_gelu, done(n) - 2)
                    for j, (a, b) in enumerate(pairs):
                        for c in range(2):
                            rows = HD + 1 if (a, c) == (0, 0) else HD
                            mm = pe.matmul(HP[m][:, 0:FH], xT[0:rows, m, 2 * a + c, :], w[0:rows, b, c, :],
                                           start=(j == 0 and c == 0), stop=(j == 2 and c == 1))
                    mm.then_inc(s.e_h, 1)
                if tile(3):
                    n, k, turn = tile(3)
                    m = k % 2
                    w = v.W2[:, bass.ds(expert(n), 1)].rearrange("p o a c n -> p (o a) c n")
                    pe.wait_ge(s.e_hTa, done(n))
                    pe.wait_ge(s.e_hTv, done(n))
                    pe.wait_ge(s.e_ys, done(n) - 2)
                    for j, (a, b) in enumerate(pairs):
                        for c in range(FK):
                            mm = pe.matmul(YP[m][:, 0:D], hT[:, m, a, c * P:(c + 1) * P], w[:, b, c, :],
                                           start=(j == 0 and c == 0), stop=(j == 2 and c == FK - 1))
                    mm.then_inc(s.e_y, 1)
                if tile(2):
                    n, k, turn = tile(2)
                    m = k % 2
                    pe.wait_ge(s.e_lo, done(n))
                    pe.wait_ge(s.e_hTa, done(n) - 1)
                    pe.wait_ge(s.e_hTv, done(n) - 1)
                    for a, dst in enumerate((HTA, HTV)):
                        for c in range(FK):
                            mm = pe.transpose(half_bank(dst, FH)[:, c * P:(c + 1) * P],
                                              hp[:, m, a, c * P:(c + 1) * P], v.ident16[:])
                    mm.then_inc(s.e_hT, 1)

            pipeline(pe, step, 3)

        @block.scalar
        def _(act):
            prime(act, *own["act"])

            def step(tile):
                if tile(0):
                    n, k, turn = tile(0)
                    act.wait_ge(s.e_xT, done(n))
                    act.wait_ge(s.e_h, done(n) - 2)
                    act.activation(xT[0:HD, k % 2], half_bank(XT, 4 * P)[0:HD, :].rearrange("p (c t) -> p c t", c=4),
                                   ACT.Copy).then_inc(s.e_xTs, 1)
                if tile(1):
                    n, k, turn = tile(1)
                    m = k % 2
                    act.wait_ge(s.e_h, done(n))
                    act.wait_ge(s.e_lo, done(n) - 2)
                    act.wait_ge(s.e_st, done(n) - 2)
                    act.activation(h[:, m, :], HP[m][:, 0:FH], ACT.Gelu, scale=1.0 / WS).then_inc(s.e_gelu, 1)
                    act.wait_ge(s.e_gelu, done(n))
                    act.wait_ge(s.e_hT, done(n) - 2)
                    act.activation(hp[:, m, 0, :], h[:, m, :], ACT.Copy, scale=HS).then_inc(s.e_hi, 1)
                if tile(3):
                    n, k, turn = tile(3)
                    act.wait_ge(s.e_y, done(n))
                    act.wait_ge(s.e_rs, done(n))
                    act.wait_ge(e_out[k], prev(turn, 16))
                    act.activation(y[:, k, :], YP[k % 2][:, 0:D], ACT.Copy, scale=rs[:, k:k + 1]).then_inc(s.e_ys, 1)
                if tile(2):
                    n, k, turn = tile(2)
                    act.wait_ge(s.e_hT, done(n))
                    act.wait_ge(s.e_y, done(n) - 2)
                    act.activation(hT[:, k % 2, 0, :], half_bank(HTA, FH), ACT.Copy).then_inc(s.e_hTa, 1)

            pipeline(act, step, 3)

        @block.vector
        def _(dve):
            prime(dve, *own["dve"])
            n_link = [0]

            def link(ins):
                n_link[0] += 1
                ins.then_inc(s.t_chain, 1)
                dve.wait_ge(s.t_chain, n_link[0])

            dve.memset(xT[HD:HD + 1, :, :], 1.0).then_inc(s.e_one, 1)
            dve.wait_ge(s.t_cnt, 1)
            link(dve.tensor_copy(count[:], bank[7][:, 256:256 + E]))
            link(dve.scalar_tensor_tensor(pad_f[:], v.rows[:, 0:E], float(REGION), count[:], ALU.mult, ALU.add))
            link(dve.tensor_scalar(pad_f[:], pad_f[:], v.lpos[:, NG:NG + 1], None, ALU.add))
            dve.tensor_copy(pad_i[:], pad_f[:]).then_inc(s.t_pad, 1)
            link(dve.tensor_scalar(cmp32[:, 0, :], v.rows[:, 0:NT], float(P), None, ALU.mult))
            link(dve.tensor_copy(cmp32[:, 1, :], cmp32[:, 0, :]))
            link(dve.tensor_tensor(cmp32[:, 2:E, :],
                                   count[:, 2:E].rearrange("p (e u) -> p e u", u=1).broadcast_to([P, E - 2, NT]),
                                   cmp32[:, 0:1, :].broadcast_to([P, E - 2, NT]), ALU.is_gt))
            link(dve.tensor_tensor(cmp32[:, 1, :], count[:, 1:2].broadcast_to([P, NT]), cmp32[:, 1, :], ALU.is_gt))
            link(dve.memset(tiles[:, 0:1], 0.0))
            link(dve.tensor_reduce(tiles[:, 1:E], cmp32[:, 1:E, :], AX.X, ALU.add))
            link(dve.memset(onesE[:], 1.0))
            link(dve.tensor_tensor_scan(ends[:], onesE[:], tiles[:], 0.0, ALU.mult, ALU.add))
            it = v.rows[0:1, 0:RT]
            link(dve.tensor_tensor(cmpT[:, :, 1:E], it.rearrange("p (i u) -> p i u", u=1).broadcast_to([1, RT, E - 1]),
                                   ends[0:1, 1:E].rearrange("p (u e) -> p u e", u=1).broadcast_to([1, RT, E - 1]),
                                   ALU.is_ge))
            link(dve.tensor_reduce(cnt[:, 0, :], cmpT[:, :, 1:E], AX.X, ALU.add))
            link(dve.tensor_tensor(cmpT[:, :, 1:E], cmpT[:, :, 1:E],
                                   tiles[0:1, 1:E].rearrange("p (u e) -> p u e", u=1).broadcast_to([1, RT, E - 1]),
                                   ALU.mult))
            link(dve.tensor_reduce(cnt[:, 1, :], cmpT[:, :, 1:E], AX.X, ALU.add))
            link(dve.tensor_scalar(cnt[:, 2, :], it, ends[0:1, E - 1:E], None, ALU.is_lt))
            link(dve.tensor_tensor(cnt[:, 3, :], it, cnt[:, 1, :], ALU.subtract))
            link(dve.tensor_tensor(cnt[:, 3, :], cnt[:, 3, :], cnt[:, 2, :], ALU.mult))
            link(dve.tensor_tensor(cnt[:, 4, :], cnt[:, 0, :], cnt[:, 2, :], ALU.mult))
            link(dve.tensor_scalar(cnt[:, 4, :], cnt[:, 4, :], 1.0, None, ALU.add))
            link(dve.tensor_copy(e_of[:, NT:], cnt[:, 4, :]))
            link(dve.tensor_scalar(cnt[:, 4, :], cnt[:, 4, :], float(REGION), None, ALU.mult))
            link(dve.scalar_tensor_tensor(cnt[:, 5, :], cnt[:, 3, :], float(P), cnt[:, 4, :], ALU.mult, ALU.add))
            link(dve.tensor_copy(r_of[:, NT:], cnt[:, 5, :]))
            link(dve.tensor_scalar(e_of[:, 0:NT], v.rows[0:1, 0:NT], 0.0, None, ALU.mult))
            link(dve.tensor_scalar(r_of[:, 0:NT], v.rows[0:1, 0:NT], float(P), None, ALU.mult))
            link(dve.tensor_tensor(v.y_row[:], ends[:], tiles[:], ALU.subtract))
            link(dve.tensor_scalar(v.y_row[:], v.y_row[:], float(P), float(NT * P), ALU.mult, ALU.add))
            link(dve.scalar_tensor_tensor(v.y_row[:], v.rows[:, 0:E], -float(REGION), v.y_row[:], ALU.mult, ALU.add))
            dve.sem_inc(s.t_ok, 1)

            def step(tile):
                if tile(1):
                    n, k, turn = tile(1)
                    m = k % 2
                    wait_alone(dve, s.e_gelu, done(n))
                    dve.bn_stats(st[:, m, :], h[:, m, :]).then_inc(s.e_st, 1)
                    dve.wait_ge(s.e_hi, done(n))
                    dve.scalar_tensor_tensor(hp[:, m, 1, :], h[:, m, :], HS, hp[:, m, 0, :],
                                             ALU.mult, ALU.subtract).then_inc(s.e_lo, 1)
                    wait_alone(dve, s.e_st, done(n))
                    dve.wait_ge(s.e_va, done(n) - 4)
                    dve.bn_aggr(mv[:, k, :], st[:, m, :]).then_inc(s.e_mv, 1)
                if tile(2):
                    n, k, turn = tile(2)
                    dve.wait_ge(s.e_hT, done(n))
                    dve.wait_ge(s.e_y, done(n) - 2)
                    dve.tensor_copy(hT[:, k % 2, 1, :], half_bank(HTV, FH)).then_inc(s.e_hTv, 1)

            pipeline(dve, step, 2)


def combine(nc, sbuf, sems, prime, bank, v):
    v = named("Shared", v)
    NK = NT * TOPK
    with ExitStack() as ctx:
        w3 = sbuf(ctx, "w3k", [P, NT, TOPK])
        ex = sbuf(ctx, "ex", [P, NT, E])
        sm = sbuf(ctx, "sm", [P, NT])
        rsm = sbuf(ctx, "rsm", [P, NT])
        hot = sbuf(ctx, "chot", [P, NK, E])
        tmp = sbuf(ctx, "ctmp", [P, NK, E])
        comb = sbuf(ctx, "comb", [P, NT, E])
        slot = sbuf(ctx, "slot", [P, NT, TOPK])
        slot_i = sbuf(ctx, "cslot", [P, NT, TOPK], I32)
        ysh = sbuf(ctx, "ysh", [P, 2, D])
        yk = sbuf(ctx, "yk", [P, 2, TOPK, D])
        cT = sbuf(ctx, "cT", [E, NT * P])
        o = sbuf(ctx, "o", [P, 2, D])
        s = sems("c_chain", "c_exp_in", "c_exp", "c_slot", "c_comb", "c_sh0", "c_sh1", "c_g0", "c_g1", "c_T",
                 "c_Ts", "c_b", "c_a0", "c_a1", "c_a2", "c_a3", "c_o", "c_out0", "c_out1")
        c_sh, c_g, c_out = (s.c_sh0, s.c_sh1), (s.c_g0, s.c_g1), (s.c_out0, s.c_out1)
        block = ctx.enter_context(nc.Block())

        @block.scalar
        def _(act):
            act.wait_ge(s.c_exp_in, 1)
            act.activation(ex[:], ex[:], ACT.Exp).then_inc(s.c_exp, 1)
            act.activation(w3[:], w3[:], ACT.Exp).then_inc(s.c_exp, 1)
            for q in range(NT // 4):
                act.wait_ge(s.c_T, q + 1)
                act.activation(cT[:, q * 4 * P:(q + 1) * 4 * P], bank[q % 2][0:E, :], ACT.Copy).then_inc(s.c_Ts, 1)

        def store(sp, t):
            sp.wait_ge(s.c_o, t + 1)
            b, c = t % NB, t // NB
            sp.dma_start(v.out[b, c * P:(c + 1) * P, :], o[:, t % 2, :]).then_inc(c_out[t % 2], 16)

        @block.sync
        def _(sp):
            for t in range(NT):
                if t >= 2:
                    sp.wait_ge(s.c_a0, t - 1)
                sp.dma_start(ysh[:, t % 2, :], v.y_rows[t * P:(t + 1) * P, :]).then_inc(c_sh[t % 2], 16)
                if t >= 1:
                    store(sp, t - 1)
            store(sp, NT - 1)
            sp.wait_ge(s.c_out0, NT // 2 * 16)
            sp.wait_ge(s.c_out1, NT // 2 * 16)

        @block.gpsimd
        def _(pool):
            pool.wait_ge(s.c_slot, 1)
            for t in range(NT):
                if t >= 2:
                    pool.wait_ge(s.c_a3, t - 1)
                for k in range(TOPK):
                    pool.indirect_dma_start(yk[:, t % 2, k, :], None, v.y_rows,
                                            bass.IndirectOffsetOnAxis(ap=slot_i[:, t, k:k + 1], axis=0)).then_inc(
                                                c_g[t % 2], 16)

        @block.tensor
        def _(pe):
            pe.wait_ge(s.c_comb, 1)
            for q in range(NT // 4):
                if q >= 2:
                    pe.wait_ge(s.c_Ts, q - 1)
                for b in range(4):
                    mm = pe.transpose(bank[q % 2][0:E, b * P:(b + 1) * P], comb[:, q * 4 + b, :], v.ident)
                mm.then_inc(s.c_T, 1)
            for t in range(NT):
                pe.wait_ge(s.c_Ts, t // 4 + 1)
                if t >= 2:
                    pe.wait_ge(s.c_a0, t - 1)
                pe.matmul(bank[2 + t % 2][:, 0:D], cT[:, t * P:(t + 1) * P], v.B2[:], start=True,
                          stop=True).then_inc(s.c_b, 1)

        @block.vector
        def _(dve):
            n = [0]

            def link(ins):
                n[0] += 1
                ins.then_inc(s.c_chain, 1)
                dve.wait_ge(s.c_chain, n[0])

            link(dve.memset(v.scores[:, :, 0:1], -1e9))
            best = v.score3[:, :, 0:1]
            link(dve.tensor_tensor(ex[:], v.scores[:], best.broadcast_to([P, NT, E]), ALU.subtract))
            link(dve.tensor_tensor(w3[:], v.score3[:], best.broadcast_to([P, NT, TOPK]), ALU.subtract))
            dve.sem_inc(s.c_exp_in, 1)
            ek = v.picked[:].rearrange("p t (k u) -> p (t k) u", u=1).broadcast_to([P, NK, E])
            link(dve.tensor_tensor(hot[:], v.rows[:, 0:E].rearrange("p (o e) -> p o e", o=1).broadcast_to([P, NK, E]),
                                   ek, ALU.is_equal))
            link(dve.tensor_tensor(tmp[:], hot[:],
                                   v.y_row[:].rearrange("p (o e) -> p o e", o=1).broadcast_to([P, NK, E]), ALU.mult))
            link(dve.tensor_reduce(slot[:].rearrange("p t k -> p (t k)"), tmp[:], AX.X, ALU.add))
            link(dve.tensor_tensor(slot[:], slot[:], v.place[:], ALU.add))
            dve.tensor_copy(slot_i[:], slot[:]).then_inc(s.c_slot, 1)
            dve.wait_ge(s.c_exp, 2)
            link(dve.tensor_reduce(sm[:], ex[:], AX.X, ALU.add))
            link(dve.reciprocal(rsm[:], sm[:]))
            link(dve.tensor_tensor(w3[:], w3[:], rsm[:].rearrange("p (t u) -> p t u", u=1).broadcast_to([P, NT, TOPK]),
                                   ALU.mult))
            link(dve.tensor_tensor(tmp[:], hot[:],
                                   w3[:].rearrange("p t (k u) -> p (t k) u", u=1).broadcast_to([P, NK, E]), ALU.mult))
            t4 = tmp[:].rearrange("p (t k) e -> p t k e", k=TOPK)
            link(dve.tensor_tensor(comb[:], t4[:, :, 0, :], t4[:, :, 1, :], ALU.add))
            link(dve.tensor_tensor(comb[:], comb[:], t4[:, :, 2, :], ALU.add))
            link(dve.memset(comb[:, :, 0:1], 1.0))
            dve.sem_inc(s.c_comb, 1)
            for t in range(NT):
                m = t % 2
                hrow = v.hbuf[:, t, :]
                dve.wait_ge(c_sh[m], (t // 2 + 1) * 16)
                dve.wait_ge(s.c_b, t + 1)
                dve.tensor_tensor(ysh[:, m, :], ysh[:, m, :], bank[2 + m][:, 0:D], ALU.add).then_inc(s.c_chain, 1)
                n[0] += 1
                dve.wait_ge(s.c_chain, n[0])
                dve.tensor_tensor(hrow, hrow, ysh[:, m, :], ALU.add).then_inc(s.c_a0, 1)
                dve.wait_ge(s.c_a0, t + 1)
                dve.wait_ge(c_g[m], (t // 2 + 1) * 16 * TOPK)
                dve.scalar_tensor_tensor(hrow, yk[:, m, 0, :], w3[:, t, 0:1], hrow, ALU.mult, ALU.add).then_inc(s.c_a1, 1)
                dve.wait_ge(s.c_a1, t + 1)
                dve.scalar_tensor_tensor(hrow, yk[:, m, 1, :], w3[:, t, 1:2], hrow, ALU.mult, ALU.add).then_inc(s.c_a2, 1)
                dve.wait_ge(s.c_a2, t + 1)
                if t >= 2:
                    dve.wait_ge(c_out[m], t // 2 * 16)
                dve.scalar_tensor_tensor(o[:, m, :], yk[:, m, 2, :], w3[:, t, 2:3], hrow, ALU.mult,
                                         ALU.add).then_inc(s.c_o, 1)
                dve.wait_ge(s.c_o, t + 1)
                dve.sem_inc(s.c_a3, 1)


_OUTS = [((NB, L, D), "float32")]


def shape_constants():
    f = np.float32
    p = np.arange(L, dtype=f)[:, None]
    exps = (np.floor(np.arange(D, dtype=f) / f(2)) * f(2) / f(D))[None]
    den = np.power(10000.0, exps.astype(np.float64)).astype(f)
    ang = (p / den).astype(np.float64)
    pos = np.where(np.arange(D) % 2 == 0, np.sin(ang), np.cos(ang)).astype(f)
    inv = (f(1) / np.power(10000.0, (np.arange(0, DH, 2, dtype=f) / f(DH)).astype(np.float64)).astype(f))
    fr = (p * inv[None]).astype(f).astype(np.float64)
    cos = np.concatenate([np.cos(fr), np.cos(fr)], 1)
    sin = np.concatenate([np.sin(fr), -np.sin(fr)], 1)
    rope = np.stack([cos, sin]).astype(f)
    a = np.arange(P)
    mats = np.stack([np.eye(P), a[:, None] <= a[None], a[:, None] < a[None], np.ones((P, P))], 1).astype(f)
    rows = np.arange(256, dtype=f)[None]
    lpos = np.concatenate([np.arange(NG)[None] * P + a[:, None] + 1, a[:, None]], 1).astype(f)
    return dict(c_pos=pos, c_rope=rope, c_mats=mats, c_rows=rows, c_lpos=lpos)


_INS = ["x", "mask_BS_i2_0", "L0_tok_token_table", "L0_tok_segm_table", "L0_attn_ln_w", "L0_attn_w_comp",
        "L0_attn_w_qkv", "L0_attn_w_reso", "L0_attn_qn_w", "L0_attn_kn_w", "L0_attn_w_outgate",
        "L0_attn_head_decay", "L0_attn_temperature", "L0_attn_w_proj", "L0_attn_memn_w", "L0_attn_ffn_ln_w",
        "L0_attn_w1", "L0_attn_w2", "L0_attn_w3", "L0_ffn_gate_w", "L0_ffn_gate_b", "L0_ffn_fc1_w",
        "L0_ffn_fc1_b", "L0_ffn_ln_w", "L0_ffn_ln_b", "L0_ffn_fc2_w", "L0_ffn_fc2_b"]


def kernel(**inputs):
    import numpy as _np
    import concourse.bacc as _bacc
    from concourse import mybir as _mybir
    from concourse.bass_utils import run_bass_kernel_spmd as _run

    nc = _bacc.Bacc("TRN2", target_bir_lowering=False, num_devices=1)
    arrays, args = {}, []
    consts = shape_constants()
    for name in _INS + list(consts):
        a = _np.ascontiguousarray(inputs[name] if name in inputs else consts[name])
        arrays[f"in_{name}"] = a
        args.append(nc.dram_tensor(f"in_{name}", a.shape, _mybir.dt.from_np(a.dtype), kind="ExternalInput").ap())
    for i, (shape, dtype) in enumerate(_OUTS):
        dt = _mybir.dt.from_np(_np.dtype(dtype))
        args.append(nc.dram_tensor(f"out_{i}", shape, dt, kind="ExternalOutput").ap())
    program(nc, *args)
    r = _run(nc, [arrays], core_ids=[0])
    return r.results[0]["out_0"]
```

```python
from collections import namedtuple
from contextlib import ExitStack

import numpy as np

import concourse.bass as bass
from concourse import mybir

ALU = mybir.AluOpType
ACT = mybir.ActivationFunctionType
AX = mybir.AxisListType
F32 = mybir.dt.float32
F16 = mybir.dt.float16
I32 = mybir.dt.int32
U32 = mybir.dt.uint32

P = 128
NB, L, D = 4, 1024, 192
NT = NB * L // P
NG = L // P
G = NB
HD = D // 2
VOCAB, NSEG = 8000, 3
LAT, H, DH = 128, 12, 16
DV = DH + 1
HID = 512
E, FH = 16, 384
FK = FH // P
TOPK = 3
REGION = NB * L + P
SLOTS = TOPK * NB * L
RT = SLOTS // P + (E - 2)
SHARED_FIRST = 8
GATHER_FROM = (SHARED_FIRST + RT + 3) // 4 * 4 + 4
PI = float(np.pi)
PRIME = 4
WS = 64.0
HS = 16.0


def done(i, n=1, k=0):
    return i * n + k + 1 + PRIME


def prev(i, n=1):
    return i * n + PRIME


def dma_done(i, n=1, k=0):
    return (i * n + k + 1) * 16 + PRIME


def named(kind, values):
    return namedtuple(kind, list(values))(*values.values())


def wait_alone(eng, sem, value):
    if not isinstance(value, int):
        value = eng.snap(eng.to_reg(value))
    eng.wait_ge(sem, PRIME)
    eng.wait_ge(sem, value)


def run_steps(eng, step, tiles, last, width=4, turn_start=None, pauses=(), loop_end=None):
    def run(q, k):
        if turn_start and k == 0:
            turn_start(q)

        def tile(behind):
            m = k - behind
            if isinstance(q, int) and not 0 <= q * width + m < tiles:
                return None
            return q * width + m, m % width, q + m // width
        tile.slot = k
        step(tile)
    first = (last + width - 1) // width
    for n in range(first * width):
        run(n // width, n % width)
    loop_end = loop_end or tiles // width
    edges = [first] + [turn for turn, _ in pauses] + [loop_end]
    for n, (start, end) in enumerate(zip(edges, edges[1:])):
        if n:
            pauses[n - 1][1]()
        if end > start:
            with eng.Fori(start, end, 1) as q:
                for k in range(width):
                    run(q, k)
    for n in range(loop_end * width, tiles + last):
        run(n // width, n % width)


def row(t, k):
    return t[:, bass.ds(k, 1), :].rearrange("p o d -> p (o d)")


def half_bank(a, n):
    return a[:, 0:n // 2].bitcast(F16)


PAIRS = ((0, 0), (0, 1), (1, 0))


def program(nc, x, seg, tok_table, seg_table, ln_w, w_comp, w_qkv, w_reso, qn_w, kn_w, w_outgate,
            head_decay, temperature, w_proj, memn_w, ffn_ln_w, w1, w2, w3, gate_w, gate_b, fc1_w,
            fc1_b, eln_w, eln_b, fc2_w, fc2_b, c_pos, c_rope, c_mats, c_rows, c_lpos, out):
    x_rows = nc.dram_tensor("x_rows", (E * REGION, 2 * D), F16).ap()
    y_rows = nc.dram_tensor("y_rows", (RT * P, D), F32).ap()
    y_shared = nc.dram_tensor("y_shared", (NT * P, D), F32).ap()

    with ExitStack() as top:
        def sbuf(ctx, name, shape, dt=F32):
            return ctx.enter_context(nc.sbuf_tensor(name, shape, dt))

        in_use = []

        def sems(*names):
            made = named("Semaphores", {n: nc.alloc_semaphore(name=n) for n in names})
            in_use.extend(made)
            return made

        def release_sems():
            nc.clear_and_free_semaphores(in_use)
            nc.all_engine_barrier()
            in_use.clear()

        def prime(eng, *ss):
            for s in ss:
                eng.sem_inc(s, PRIME)

        bank = [top.enter_context(nc.psum_tensor(f"bank{k}", [P, 512], F32)) for k in range(8)]

        hbuf = sbuf(top, "hbuf", [P, NT, D])
        x1buf = sbuf(top, "x1buf", [P, NT, D])
        B2 = sbuf(top, "B2", [E, D])
        mats = sbuf(top, "mats", [P, 4, P])
        ident16 = sbuf(top, "ident16", [P, P], F16)
        ident, causal, strict, ones = (mats[:, k, :] for k in range(4))
        rows = sbuf(top, "rows", [P, 256])
        lpos = sbuf(top, "lpos", [P, NG + 1])
        neghalf = sbuf(top, "neghalf", [P, 2 * H])
        fcol = sbuf(top, "fcol", [HD, 2])
        picked = sbuf(top, "picked", [P, NT, TOPK])
        place = sbuf(top, "place", [P, NT, TOPK])
        score3 = sbuf(top, "score3", [P, NT, TOPK])
        scores = sbuf(top, "scores", [P, NT, E])
        chosen = sbuf(top, "chosen", [P, E])
        y_row = sbuf(top, "y_row", [P, E])

        slot_i = sbuf(top, "slots", [P, NT, TOPK], I32)
        weights = top.enter_context(ExitStack())
        W1 = sbuf(weights, "W1", [HD + 1, E, 2, 2, FH], F16)
        W2 = sbuf(weights, "W2", [P, E, 2, FK, D], F16)

        with ExitStack() as att:
            latT = sbuf(att, "latT", [P, 2, NT * P], F16)
            gates = sbuf(att, "gates", [P, NT, H])
            scale = sbuf(att, "scale", [P, NG, 2 * H])
            rope = sbuf(att, "rope", [P, 2, 2, NG, DH])
            wlat = sbuf(att, "wlat", [P, 2, 4 * D], F16)
            wproj = sbuf(att, "wproj", [HD, 2, 2, D], F16)
            with ExitStack() as emb:
                params = sbuf(emb, "params", [P, NT, 4 * H])
                wcomp = sbuf(emb, "wcomp", [HD, 2, LAT])
                wreso = sbuf(emb, "wreso", [P, 4 * H])
                pos = sbuf(emb, "pos", [P, NG, D])
                temp = sbuf(emb, "temp", [P, 1])
                tok_id = sbuf(emb, "tok_id", [P, NG, NB], I32)
                seg_hot = sbuf(emb, "seg_hot", [P, NG, NB, NSEG])
                segw = sbuf(emb, "segw", [NB * NSEG, NB, D])
                setup(nc, sbuf, sems, bank, locals())
                embed(nc, sbuf, sems, prime, bank, locals())
                write_gates(nc, sbuf, sems, locals())
            attend(nc, sbuf, sems, prime, bank, locals())
        release_sems()
        ffn(nc, sbuf, sems, prime, bank, locals())
        IN_X1 = NT // TOPK
        routed_x1 = x1buf[:, 0:IN_X1 * TOPK, :].rearrange("p (t k) d -> p t k d", k=TOPK)
        gathered = sems("gathered0", "gathered1", "gathered2", "gathered3", "gathered4", "gathered5",
                        "gathered6", "gathered7")

        def routed(t):
            return routed_x1[:, t] if t < IN_X1 else later[0][:, t - IN_X1]

        def gather(pool, t, k):
            pool.indirect_dma_start(routed(t)[:, k, :], None, y_rows,
                                    bass.IndirectOffsetOnAxis(ap=slot_i[:, t, k:k + 1], axis=0)
                                    ).then_inc(gathered[t // 4], 16)

        later = []
        gathers = [(t, k) for t in range(NT) for k in range(TOPK)]
        EARLY = IN_X1 * TOPK
        experts(nc, sbuf, sems, prime, bank, locals())
        weights.close()
        later.append(sbuf(top, "routed_later", [P, NT - IN_X1, TOPK, D]))
        combine(nc, sbuf, sems, prime, bank, locals())
        release_sems()


def halves(w):
    return w.rearrange("(k d) n -> d k n", k=2)


def setup(nc, sbuf, sems, bank, v):
    v = named("Shared", v)
    with ExitStack() as ctx:
        cols = sbuf(ctx, "cols", [HD, 2, 2])
        qkn = sbuf(ctx, "qkn", [P, 2, DH])
        cs = sbuf(ctx, "cs", [P, 2, NG, DH])
        ln_rows = sbuf(ctx, "ln_rows", [E * FK, 2, P])
        lnT = sbuf(ctx, "lnT", [P, 2, E * FK])
        lnw, lnb = (lnT[:, k, :].rearrange("p (e k) -> p e k", k=FK) for k in range(2))
        col_rows = sbuf(ctx, "col_rows", [2 * 3, HD])
        id_rows = sbuf(ctx, "id_rows", [NT, 2, P], I32)
        idf = sbuf(ctx, "idf", [NT, 2, P])
        idg = sbuf(ctx, "idg", [NT, P])
        lnb_diag = sbuf(ctx, "lnb_diag", [P, E, FK, E])
        b2 = sbuf(ctx, "b2", [E, D])
        wqkv = sbuf(ctx, "wqkv", [P, 4 * D])
        wpr = sbuf(ctx, "wpr", [HD, 2, D])
        RING = 4
        n1, n2 = RING * 2 * FH, RING * FK * D
        stage = v.hbuf[:].rearrange("p t d -> p (t d)")
        raw1 = stage[0:HD + 1, 0:n1].rearrange("p (r c n) -> p r c n", r=RING, c=2)
        raw2 = stage[:, n1:n1 + n2].rearrange("p (r c n) -> p r c n", r=RING, c=FK)
        w2c = v.x1buf[:, 0:RING * FK, :].rearrange("p (m k) d -> p m k d", m=RING)
        dec = sbuf(ctx, "dec", [P, 6, H])
        df = sbuf(ctx, "df", [P, NG, H])
        dfe = sbuf(ctx, "dfe", [P, NG, H])
        seg_id = sbuf(ctx, "seg_id", [P, NG, NB])
        s = sems("seg_clear", "ld_small", "ld_ids", "ld_ln", "ids_clean", "turned", "turned_ok", "ld_w", "ld_b2", "ld_const",
                 "ld_e0", "ld_e1", "ld_e2", "ld_e3", "b2_sum", "b2_ok", "raw2_read", "w2_scaled", "col_sum",
                 "centred", "w2_hi", "w2_lo", "w1_hi", "w1_lo", "diag_ok", "rope_ok", "decay_in", "tanh_ok", "ln_ok",
                 "df_in", "df_ok", "chain")
        ld_e = (s.ld_e0, s.ld_e1, s.ld_e2, s.ld_e3)
        block = ctx.enter_context(nc.Block())

        @block.sync
        def _(sp):
            bc = lambda a, n: a.rearrange("(o n) -> o n", o=1).broadcast_to([P, n])
            for k, a in enumerate((v.x, v.seg)):
                sp.dma_start(id_rows[:, k, :], a.rearrange("b (c p) -> (b c) p", p=P)).then_inc(s.ld_ids, 16)
            sp.dma_start(v.mats[:], v.c_mats).then_inc(s.ld_const, 16)
            sp.dma_start(v.rows[:], v.c_rows.broadcast_to([P, 256])).then_inc(s.ld_const, 16)
            sp.dma_start(v.lpos[:], v.c_lpos).then_inc(s.ld_const, 16)
            sp.dma_start(v.pos[:], v.c_pos.rearrange("(c p) d -> p c d", p=P)).then_inc(s.ld_const, 16)
            for k in range(2):
                sp.dma_start(cs[:, k], v.c_rope[k].rearrange("(c p) d -> p c d", p=P)).then_inc(s.ld_const, 16)
            sp.dma_start(dec[:, 0, :], bc(v.head_decay, H)).then_inc(s.ld_small, 16)
            sp.dma_start(v.temp[:], bc(v.temperature, 1)).then_inc(s.ld_small, 16)
            for k, a in enumerate((v.qn_w, v.kn_w)):
                sp.dma_start(qkn[:, k, :], bc(a, DH)).then_inc(s.ld_small, 16)
            for k, a in enumerate((v.ln_w, v.memn_w, v.ffn_ln_w)):
                sp.dma_start(col_rows[2 * k:2 * k + 2, :], a.rearrange("(k d) -> k d", k=2)).then_inc(s.ld_small, 16)
            sp.dma_start(v.wcomp[:], halves(v.w_comp)).then_inc(s.ld_w, 16)
            sp.dma_start(wpr[:], halves(v.w_proj)).then_inc(s.ld_w, 16)
            sp.dma_start(wqkv[:, 0:3 * D], v.w_qkv).then_inc(s.ld_w, 16)
            sp.dma_start(wqkv[:, 3 * D:], v.w_outgate).then_inc(s.ld_w, 16)
            sp.dma_start(v.wreso[:], v.w_reso).then_inc(s.ld_w, 16)
            sp.wait_ge(s.seg_clear, 1)
            for b in range(NB):
                sp.dma_start(v.segw[b * NSEG:(b + 1) * NSEG, b, :], v.seg_table).then_inc(s.ld_w, 16)
            for e in range(E):
                if e >= RING:
                    sp.wait_ge(s.w1_lo, e - RING + 1)
                    sp.wait_ge(s.w2_scaled, e - RING + 1)
                    sp.wait_ge(s.raw2_read, e - RING + 1)
                r = e % RING
                sp.dma_start(raw1[0:HD, r], halves(v.fc1_w[e])).then_inc(ld_e[r], 16)
                sp.dma_start(raw1[HD:HD + 1, r, 0, :], v.fc1_b[e:e + 1, :]).then_inc(ld_e[r], 16)
                sp.dma_start(raw2[:, r], v.fc2_w[e].rearrange("(k p) n -> p k n", p=P)).then_inc(ld_e[r], 16)
            sp.wait_ge(s.ld_w, 9 * 16)

        @block.scalar
        def _(act):
            for k, a in enumerate((v.eln_w, v.eln_b)):
                act.dma_start(ln_rows[:, k, :], a.rearrange("e (k p) -> (e k) p", p=P)).then_inc(s.ld_ln, 16)
            act.dma_start(b2[:], v.fc2_b).then_inc(s.ld_b2, 16)
            act.wait_ge(s.ld_small, 7 * 16)
            act.activation(dec[:, 1, :], dec[:, 0, :], ACT.Tanh, scale=0.5).then_inc(s.tanh_ok, 1)
            act.wait_ge(s.decay_in, 1)
            act.activation(dec[:, 3, :], dec[:, 2, :], ACT.Ln).then_inc(s.ln_ok, 1)
            act.wait_ge(s.df_in, 1)
            act.activation(df[:], df[:], ACT.Exp).then_inc(s.df_ok, 1)
            def upper_half2(e):
                act.wait_ge(s.centred, e + 1)
                act.activation(v.W2[:, e, 0], w2c[:, e % RING], ACT.Copy, scale=WS).then_inc(s.w2_hi, 1)

            act.wait_ge(s.turned_ok, 1)
            for e in range(E):
                r = e % RING
                act.wait_ge(ld_e[r], (e // RING + 1) * 48)
                if e >= RING:
                    act.wait_ge(s.w2_lo, e - RING + 1)
                for k in range(FK):
                    ins = act.activation(w2c[:, r, k, :], raw2[:, r, k, :], ACT.Copy, scale=lnw[:, e, k:k + 1])
                ins.then_inc(s.w2_scaled, 1)
                act.activation(v.W1[:, e, 0, 0, :], raw1[:, r, 0, :], ACT.Copy, scale=WS)
                act.activation(v.W1[0:HD, e, 0, 1, :], raw1[0:HD, r, 1, :], ACT.Copy, scale=WS).then_inc(s.w1_hi, 1)
                if e:
                    upper_half2(e - 1)
            upper_half2(E - 1)

        @block.tensor
        def _(pe):
            pe.wait_ge(s.ld_const, 6 * 16)
            pe.wait_ge(s.ld_ln, 2 * 16)
            pe.wait_ge(s.ld_small, 7 * 16)
            n = E * FK
            for k in range(2):
                pe.transpose(bank[3][:, k * n:(k + 1) * n], ln_rows[:, k, :], v.ident[0:n, 0:n])
            pe.transpose(bank[3][0:HD, 2 * n:2 * n + 6], col_rows[:], v.ident[0:6, 0:6]).then_inc(s.turned, 1)
            pe.wait_ge(s.ids_clean, 1)
            for k in range(2):
                mm = pe.transpose(bank[4][:, k * NT:(k + 1) * NT], idf[:, k, :], v.ident[0:NT, 0:NT])
            mm.then_inc(s.turned, 1)
            for e in range(E):
                r = e % RING
                pe.wait_ge(s.diag_ok, e + 1)
                pe.wait_ge(ld_e[r], (e // RING + 1) * 48)
                for k in range(FK):
                    mm = pe.matmul(bank[0][0:E, 0:D], lnb_diag[:, e, k, :], raw2[:, r, k, :],
                                   start=(e == 0 and k == 0), stop=(e == E - 1 and k == FK - 1))
                mm.then_inc(s.raw2_read, 1)
                pe.wait_ge(s.w2_scaled, e + 1)
                if e >= 2:
                    pe.wait_ge(s.centred, e - 1)
                for k in range(FK):
                    mm = pe.matmul(bank[1 + e % 2][:, 0:D], v.ones, w2c[:, r, k, :],
                                   start=(k == 0), stop=(k == FK - 1))
                mm.then_inc(s.col_sum, 1)
            pe.wait_ge(s.col_sum, E)
            pe.sem_inc(s.b2_sum, 1)

        @block.gpsimd
        def _(pool):
            pool.memset(v.segw[:], 0.0).then_inc(s.seg_clear, 1)
            pool.memset(v.neghalf[:], -0.5)
            pool.memset(v.chosen[:], 0.0)
            pool.wait_ge(s.ld_const, 6 * 16)
            pool.wait_ge(s.turned_ok, 1)
            eye = v.rows[:, 0:E]
            for e in range(E):
                for k in range(FK):
                    ins = pool.tensor_scalar(lnb_diag[:, e, k, :], eye, float(e), lnb[:, e, k:k + 1],
                                             ALU.is_equal, ALU.mult)
                ins.then_inc(s.diag_ok, 1)
            pool.wait_ge(s.ld_small, 7 * 16)
            for k in range(2):
                for c in range(2):
                    pool.tensor_tensor(v.rope[:, k, c], cs[:, k],
                                       qkn[:, c:c + 1, :].broadcast_to([P, NG, DH]),
                                       ALU.mult).then_inc(s.rope_ok, 1)
            pool.wait_ge(s.rope_ok, 4)

        @block.vector
        def _(dve):
            n = [0]

            def link(ins):
                n[0] += 1
                ins.then_inc(s.chain, 1)
                dve.wait_ge(s.chain, n[0])

            dve.wait_ge(s.ld_const, 6 * 16)
            link(dve.tensor_copy(v.ident16[:], v.ident))
            dve.wait_ge(s.ld_ids, 2 * 16)
            for k, size in enumerate((VOCAB, NSEG)):
                link(dve.tensor_copy(idf[:, k], id_rows[:, k]))
                link(dve.tensor_scalar(idg[:], idf[:, k], 0.0, float(size), ALU.is_lt, ALU.mult))
                link(dve.tensor_tensor(idf[:, k], idf[:, k], idg[:], ALU.add))
                link(dve.tensor_scalar(idf[:, k], idf[:, k], 0.0, float(size - 1), ALU.max, ALU.min))
            dve.sem_inc(s.ids_clean, 1)
            dve.wait_ge(s.turned, 1)
            n2 = 2 * E * FK
            link(dve.tensor_copy(lnT[:].rearrange("p a n -> p (a n)"), bank[3][:, 0:n2]))
            link(dve.tensor_copy(cols[:].rearrange("d a k -> d (a k)"), bank[3][0:HD, n2:n2 + 4]))
            link(dve.tensor_scalar(v.fcol[:], bank[3][0:HD, n2 + 4:n2 + 6], WS, None, ALU.mult))
            dve.sem_inc(s.turned_ok, 1)
            dve.wait_ge(s.turned, 2)

            def by_group(k):
                return bank[4][:, k * NT:(k + 1) * NT].rearrange("p (b c) -> p c b", b=NB)
            link(dve.tensor_copy(v.tok_id[:], by_group(0)))
            link(dve.tensor_copy(seg_id[:], by_group(1)))
            for k in range(NSEG):
                link(dve.tensor_scalar(v.seg_hot[:, :, :, k], seg_id[:], float(k), None, ALU.is_equal))
            dve.wait_ge(s.tanh_ok, 1)
            link(dve.tensor_scalar(dec[:, 2, :], dec[:, 1, :], 0.325, 0.625, ALU.mult, ALU.add))
            link(dve.tensor_scalar(dec[:, 2, :], dec[:, 2, :], 1e-5, 0.999, ALU.max, ALU.min))
            dve.tensor_scalar(dec[:, 4, :], dec[:, 2, :], -1.0, 1.0, ALU.mult, ALU.add).then_inc(s.decay_in, 1)
            dve.wait_ge(s.ln_ok, 1)
            logd = dec[:, 3:4, :].broadcast_to([P, NG, H])
            lp = v.lpos[:, 0:NG].rearrange("p (c o) -> p c o", o=1).broadcast_to([P, NG, H])
            dve.tensor_tensor(df[:], logd, lp, ALU.mult).then_inc(s.df_in, 1)
            dve.wait_ge(s.df_ok, 1)
            dve.tensor_copy(v.scale[:, :, 0:H], df[:])
            link(dve.tensor_scalar(dfe[:], df[:], 1e-8, None, ALU.add))
            link(dve.reciprocal(dfe[:], dfe[:]))
            dt_b = dec[:, 4:5, :].broadcast_to([P, NG, H])
            link(dve.tensor_tensor(v.scale[:, :, H:], dfe[:], dt_b, ALU.mult))
            dve.wait_ge(s.ld_w, 9 * 16)
            for k in range(2):
                dve.tensor_scalar(v.wcomp[:, k], v.wcomp[:, k], cols[:, 0, k:k + 1], None, ALU.mult)
                link(dve.tensor_scalar(wpr[:, k], wpr[:, k], cols[:, 1, k:k + 1], 0.5 * WS, ALU.mult, ALU.mult))
            for hi, lo, w, scale in ((v.wproj[:, 0], v.wproj[:, 1], wpr[:], 1.0),
                                     (v.wlat[:, 0], v.wlat[:, 1], wqkv[:], WS)):
                link(dve.tensor_scalar(hi, w, scale, None, ALU.mult))
                link(dve.scalar_tensor_tensor(lo, w, scale, hi, ALU.mult, ALU.subtract))
            def lower_half2(e):
                dve.wait_ge(s.w2_hi, e + 1)
                dve.scalar_tensor_tensor(v.W2[:, e, 1], w2c[:, e % RING], WS, v.W2[:, e, 0],
                                         ALU.mult, ALU.subtract).then_inc(s.w2_lo, 1)

            for e in range(E):
                r, m = e % RING, e % 2
                dve.wait_ge(s.col_sum, e + 1)
                total = bank[1 + m][:, 0:D].rearrange("p (o n) -> p o n", o=1).broadcast_to([P, FK, D])
                dve.scalar_tensor_tensor(w2c[:, r], total, -1.0 / FH, w2c[:, r],
                                         ALU.mult, ALU.add).then_inc(s.centred, 1)
                if e:
                    lower_half2(e - 1)
                dve.wait_ge(s.w1_hi, e + 1)
                dve.scalar_tensor_tensor(v.W1[:, e, 1, 0, :], raw1[:, r, 0, :], WS, v.W1[:, e, 0, 0, :],
                                         ALU.mult, ALU.subtract)
                dve.scalar_tensor_tensor(v.W1[0:HD, e, 1, 1, :], raw1[0:HD, r, 1, :], WS, v.W1[0:HD, e, 0, 1, :],
                                         ALU.mult, ALU.subtract).then_inc(s.w1_lo, 1)
            lower_half2(E - 1)
            dve.wait_ge(s.b2_sum, 1)
            dve.wait_ge(s.ld_b2, 16)
            dve.tensor_tensor(v.B2[:], bank[0][0:E, 0:D], b2[:], ALU.add).then_inc(s.b2_ok, 1)
            dve.wait_ge(s.w2_lo, E)
            dve.wait_ge(s.b2_ok, 1)


def embed(nc, sbuf, sems, prime, bank, v):
    v = named("Shared", v)
    with ExitStack() as ctx:
        tok = sbuf(ctx, "tok", [P, 2, G, D])
        NS = NB * NSEG
        hotS = sbuf(ctx, "hotS", [P, NS])
        hotT = sbuf(ctx, "hotT", [NS, P])
        stat = sbuf(ctx, "stat", [P, G, 6])
        mv = sbuf(ctx, "mv", [P, G, 2])
        va, rs, r2, m2, m2e, p2 = (sbuf(ctx, n, [P, G]) for n in ("va", "rs", "r2", "m2", "m2e", "p2"))
        xs = sbuf(ctx, "xs", [P, G, D])
        xT = sbuf(ctx, "xT", [HD, 2, G * P])
        latS = sbuf(ctx, "latS", [P, G * P])
        s = sems("tok0", "tok1", "seg_one", "seg_T", "seg_Ts", "seg_mm", "pos_add", "h_ok", "stats", "moments", "va_ok", "rs_ok",
                 "r2_ok", "m2_ok", "m2e_ok", "p2_ok", "x_ok", "xs_ok", "xT_mm", "xT_a", "xT_v", "lat_mm",
                 "lat_ok", "lat_hi", "lat_kept", "par_mm", "par_ok")
        block = ctx.enter_context(nc.Block())
        own = dict(
            dve=(s.seg_one, s.pos_add, s.h_ok, s.stats, s.moments, s.x_ok, s.xT_v, s.lat_kept, s.par_ok),
            act=(s.seg_Ts, s.xs_ok, s.xT_a, s.lat_ok, s.lat_hi), pe=(s.seg_T, s.seg_mm, s.xT_mm, s.lat_mm, s.par_mm),
            pool=(s.va_ok, s.rs_ok, s.r2_ok, s.m2_ok, s.m2e_ok, s.p2_ok))

        @block.gpsimd
        def _(pool):
            prime(pool, *own["pool"])

            def gather(c, slot):
                for b in range(NB):
                    pool.indirect_dma_start(
                        tok[:, slot, b, :], None, v.tok_table,
                        bass.IndirectOffsetOnAxis(ap=v.tok_id[:, c, b:b + 1], axis=0)).then_inc(
                            (s.tok0, s.tok1)[slot], 16)

            def norm(i):
                var = mv[:, :, 1]
                wait_alone(pool, s.moments, done(i, G, G - 1))
                pool.wait_ge(s.xs_ok, prev(i, G))
                pool.tensor_scalar(va[:], var, 1e-5, None, ALU.add).then_inc(s.va_ok, 1)
                pool.wait_ge(s.va_ok, done(i))
                pool.tensor_tensor(rs[:], va[:], v.neghalf[:, 0:G], ALU.pow).then_inc(s.rs_ok, 1)
                pool.wait_ge(s.rs_ok, done(i))
                pool.tensor_tensor(r2[:], rs[:], rs[:], ALU.mult).then_inc(s.r2_ok, 1)
                pool.wait_ge(s.r2_ok, done(i))
                pool.tensor_tensor(m2[:], r2[:], var, ALU.mult).then_inc(s.m2_ok, 1)
                wait_alone(pool, s.m2_ok, done(i))
                pool.tensor_scalar(m2e[:], m2[:], 1e-6, None, ALU.add).then_inc(s.m2e_ok, 1)
                pool.wait_ge(s.m2e_ok, done(i))
                pool.tensor_tensor(p2[:], m2e[:], v.neghalf[:, 0:G], ALU.pow).then_inc(s.p2_ok, 1)

            gather(0, 0)
            gather(1, 1)
            for c in range(NG):
                norm(c)
                if c + 2 < NG:
                    pool.wait_ge(s.h_ok, done(c, 2, 1))
                    gather(c + 2, c % 2)

        def pipeline(eng, step):
            run_steps(eng, step, NG, 2, width=2)

        @block.vector
        def _(dve):
            prime(dve, *own["dve"])

            def step(tile):
                if tile(0):
                    i, slot, turn = tile(0)
                    t = tok[:, slot]
                    dve.wait_ge(s.seg_T, prev(i))
                    dve.tensor_copy(hotS[:], v.seg_hot[:, bass.ds(i, 1), :, :].rearrange("p o b k -> p (o b k)")
                                    ).then_inc(s.seg_one, 1)
                    dve.wait_ge((s.tok0, s.tok1)[slot], (turn + 1) * (NB * 16))
                    dve.tensor_tensor(t, t, v.pos[:, bass.ds(i, 1), :].broadcast_to([P, G, D]),
                                      ALU.add).then_inc(s.pos_add, 1)
                if tile(2):
                    i = tile(2)[0]
                    dve.wait_ge(s.xT_mm, done(i))
                    dve.wait_ge(s.lat_mm, prev(i))
                    dve.tensor_copy(xT[:, 1, :], bank[3][0:HD, :]).then_inc(s.xT_v, 1)
                if tile(1):
                    i = tile(1)[0]
                    dve.wait_ge(s.rs_ok, done(i))
                    for b in range(G):
                        dve.tensor_scalar(row(v.x1buf, i * G + b), row(v.hbuf, i * G + b), mv[:, b, 0:1], rs[:, b:b + 1],
                                          ALU.subtract, ALU.mult).then_inc(s.x_ok, 1)
                if tile(0):
                    i, slot, turn = tile(0)
                    t = tok[:, slot]
                    dve.wait_ge(s.pos_add, done(i))
                    dve.wait_ge(s.seg_mm, done(i))
                    for k in range(2):
                        dve.tensor_tensor(v.hbuf[:, bass.ds(i * G + 2 * k, 2), :], t[:, 2 * k:2 * k + 2, :],
                                          bank[k][:, 0:2 * D].rearrange("p (b d) -> p b d", b=2),
                                          ALU.add).then_inc(s.h_ok, 1)
                    wait_alone(dve, s.h_ok, done(i, 2, 1))
                    for b in range(G):
                        dve.bn_stats(stat[:, b, :], row(v.hbuf, i * G + b)).then_inc(s.stats, 1)
                    wait_alone(dve, s.m2_ok, prev(i))
                    wait_alone(dve, s.x_ok, prev(i, G))
                    for b in range(G):
                        wait_alone(dve, s.stats, done(i, G, b))
                        dve.bn_aggr(mv[:, b, :], stat[:, b, :]).then_inc(s.moments, 1)
                if tile(2):
                    i = tile(2)[0]
                    dve.wait_ge(s.lat_hi, done(i))
                    group_cols = bass.ds(i * (G * P), G * P)
                    dve.tensor_tensor(v.latT[:, 1, group_cols], latS[:], v.latT[:, 0, group_cols],
                                      ALU.subtract).then_inc(s.lat_kept, 1)
                    dve.wait_ge(s.par_mm, done(i))
                    dve.tensor_copy(v.params[:, bass.ds(i * G, G), :],
                                    bank[5][:, 0:G * 4 * H].rearrange("p (b n) -> p b n", b=G)).then_inc(s.par_ok, 1)

            pipeline(dve, step)

        @block.scalar
        def _(act):
            prime(act, *own["act"])

            def step(tile):
                if tile(2):
                    i = tile(2)[0]
                    act.wait_ge(s.xT_mm, done(i))
                    act.wait_ge(s.lat_mm, prev(i))
                    act.activation(xT[:, 0, :], bank[2][0:HD, :], ACT.Copy).then_inc(s.xT_a, 1)
                if tile(0):
                    i = tile(0)[0]
                    act.wait_ge(s.seg_T, done(i))
                    act.wait_ge(s.seg_mm, prev(i))
                    act.activation(hotT[:], bank[6][0:NS, 0:P], ACT.Copy).then_inc(s.seg_Ts, 1)
                if tile(1):
                    i = tile(1)[0]
                    for b in range(G):
                        wait_alone(act, s.p2_ok, done(i))
                        act.wait_ge(s.xT_mm, prev(i))
                        act.wait_ge(s.x_ok, done(i, G, b))
                        act.activation(xs[:, b, :], row(v.x1buf, i * G + b), ACT.Copy,
                                       scale=p2[:, b:b + 1]).then_inc(s.xs_ok, 1)
                if tile(2):
                    i = tile(2)[0]
                    act.wait_ge(s.lat_mm, done(i))
                    act.wait_ge(s.lat_kept, prev(i))
                    act.wait_ge(s.par_mm, prev(i))
                    act.activation(latS[:], bank[4][:], ACT.Silu).then_inc(s.lat_ok, 1)
                    wait_alone(act, s.lat_ok, done(i))
                    act.activation(v.latT[:, 0, bass.ds(i * (G * P), G * P)], latS[:], ACT.Copy).then_inc(s.lat_hi, 1)

            pipeline(act, step)

        @block.tensor
        def _(pe):
            prime(pe, *own["pe"])

            def step(tile):
                if tile(2):
                    i = tile(2)[0]
                    pe.wait_ge(s.xT_a, prev(i))
                    pe.wait_ge(s.xT_v, prev(i))
                    for b in range(G):
                        pe.wait_ge(s.xs_ok, done(i, G, b))
                        for k in range(2):
                            mm = pe.transpose(bank[2 + k][0:HD, b * P:(b + 1) * P], xs[:, b, k * HD:(k + 1) * HD],
                                              v.ident)
                    mm.then_inc(s.xT_mm, 1)
                if tile(0):
                    i = tile(0)[0]
                    pe.wait_ge(s.seg_one, done(i))
                    pe.wait_ge(s.seg_Ts, prev(i))
                    pe.transpose(bank[6][0:NS, 0:P], hotS[:], v.ident).then_inc(s.seg_T, 1)
                    pe.wait_ge(s.seg_Ts, done(i))
                    pe.wait_ge(s.h_ok, prev(i, 2))
                    for k in range(2):
                        mm = pe.matmul(bank[k][:, 0:2 * D], hotT[:],
                                       v.segw[:, 2 * k:2 * k + 2, :].rearrange("s b d -> s (b d)"),
                                       start=True, stop=True)
                    mm.then_inc(s.seg_mm, 1)
                if tile(2):
                    i = tile(2)[0]
                    pe.wait_ge(s.xT_a, done(i))
                    pe.wait_ge(s.xT_v, done(i))
                    pe.wait_ge(s.lat_ok, prev(i))
                    for k in range(2):
                        mm = pe.matmul(bank[4][:], v.wcomp[:, k, :], xT[:, k, :], start=(k == 0), stop=(k == 1))
                    mm.then_inc(s.lat_mm, 1)
                    pe.wait_ge(s.lat_ok, done(i))
                    pe.wait_ge(s.par_ok, prev(i))
                    for b in range(G):
                        mm = pe.matmul(bank[5][:, b * 4 * H:(b + 1) * 4 * H], latS[:, b * P:(b + 1) * P], v.wreso[:],
                                       start=True, stop=True)
                    mm.then_inc(s.par_mm, 1)

            pipeline(pe, step)


def write_gates(nc, sbuf, sems, v):
    v = named("Shared", v)
    n = NT * H
    with ExitStack() as ctx:
        th = sbuf(ctx, "th", [P, NT * H, 4])
        ph = sbuf(ctx, "ph", [P, n])
        amp = sbuf(ctx, "amp", [P, n])
        s = sems("g_tanh", "g_phase", "g_sin", "g_cos", "g_chain", "g_prod", "g_sig", "g_ok")
        block = ctx.enter_context(nc.Block())

        @block.scalar
        def _(act):
            act.activation(th[:].rearrange("p n k -> p (n k)"), v.params[:].rearrange("p t n -> p (t n)"),
                           ACT.Tanh, scale=0.5).then_inc(s.g_tanh, 1)
            act.wait_ge(s.g_phase, 1)
            act.activation(ph[:], ph[:], ACT.Sin, scale=PI / 4).then_inc(s.g_sin, 1)
            act.wait_ge(s.g_prod, 1)
            act.activation(amp[:], amp[:], ACT.Tanh, scale=v.temp[:, 0:1]).then_inc(s.g_sig, 1)

        @block.vector
        def _(dve):
            dve.wait_ge(s.g_tanh, 1)
            dve.tensor_tensor(ph[:], th[:, :, 1], th[:, :, 3], ALU.subtract).then_inc(s.g_phase, 1)
            dve.tensor_scalar(amp[:], th[:, :, 2], 1.0, None, ALU.add).then_inc(s.g_chain, 1)
            dve.wait_ge(s.g_chain, 1)
            dve.scalar_tensor_tensor(amp[:], th[:, :, 0], 1.0, amp[:], ALU.add, ALU.mult).then_inc(s.g_chain, 1)
            dve.wait_ge(s.g_sin, 1)
            dve.tensor_tensor(ph[:], ph[:], ph[:], ALU.mult).then_inc(s.g_cos, 1)
            dve.wait_ge(s.g_cos, 1)
            dve.tensor_scalar(ph[:], ph[:], -0.25, 0.125, ALU.mult, ALU.add).then_inc(s.g_cos, 1)
            dve.wait_ge(s.g_cos, 2)
            dve.wait_ge(s.g_chain, 2)
            dve.tensor_tensor(amp[:], amp[:], ph[:], ALU.mult).then_inc(s.g_prod, 1)
            dve.wait_ge(s.g_sig, 1)
            dve.tensor_scalar(amp[:], amp[:], 0.6 / WS, 0.5 / WS, ALU.mult, ALU.add).then_inc(s.g_chain, 1)
            dve.wait_ge(s.g_chain, 3)
            dve.tensor_scalar(v.gates[:].rearrange("p t h -> p (t h)"), amp[:], 0.05 / WS, 0.95 / WS,
                              ALU.max, ALU.min).then_inc(s.g_ok, 1)
            dve.wait_ge(s.g_ok, 1)


def attend(nc, sbuf, sems, prime, bank, v):
    v = named("Shared", v)
    NQ = 2 * H
    HB = H // 4
    hf = DH // 2
    with ExitStack() as ctx:
        ssum = sbuf(ctx, "ssum", [P, NQ])
        ms = sbuf(ctx, "ms", [P, NQ])
        rn = sbuf(ctx, "rn", [P, NQ])
        qn = sbuf(ctx, "qn", [P, 2, H, DH])
        t1 = sbuf(ctx, "t1", [P, 2, H, DH])
        rot = sbuf(ctx, "rot", [P, NQ, DH])
        neg = sbuf(ctx, "neg", [P, NQ * DH])
        sq = neg
        fpad = sbuf(ctx, "fpad", [P, 2, NQ, 2 * DH])
        vaug = sbuf(ctx, "vaug", [P, NB, H, 2 * DH])
        og = sbuf(ctx, "og", [P, NB, D])
        qkT = sbuf(ctx, "qkT", [P, 2, HB * P])
        att = sbuf(ctx, "att", [P, 4, HB * P])
        state = sbuf(ctx, "state", [P, NB, HB * 4, 2 * DH])
        outT = sbuf(ctx, "outT", [P, HB * P])
        stmp = sbuf(ctx, "stmp", [P, HB * 4 * DV])
        bd = sbuf(ctx, "bd", [P, HB, 4, DV])
        den = sbuf(ctx, "den", [P, H])
        rden = sbuf(ctx, "rden", [P, H])
        on = sbuf(ctx, "on", [P, D])
        osq = sbuf(ctx, "osq", [P, D], F16)
        oss = sbuf(ctx, "oss", [P, 1])
        oms = sbuf(ctx, "oms", [P, 1])
        orn = sbuf(ctx, "orn", [P, 1])
        op = sbuf(ctx, "op", [P, 2, D], F16)
        oT = sbuf(ctx, "oT", [HD, 4, P], F16)
        upd = sbuf(ctx, "upd", [P, D])
        s = sems("a_zero", "a_past", "a_outs", "a_outT", "a_qk", "a_vo", "a_sq", "a_sum", "a_ms", "a_rn", "a_qn", "a_t1", "a_t2",
                 "a_rot", "a_neg", "a_exp", "a_f", "a_fp", "a_vaug", "a_tanh", "a_og", "a_T", "a_qT", "a_kT",
                 "a_s", "a_mask", "a_supd", "a_stmp", "a_state", "a_o", "a_den", "a_rden", "a_on", "a_osq",
                 "a_oms", "a_orn", "a_ohi", "a_olo", "a_oT", "a_oTs", "a_proj", "a_upd", "a_x1")
        own = dict(
            dve=(s.a_sum, s.a_olo, s.a_qn, s.a_t1, s.a_t2, s.a_rot, s.a_neg, s.a_f, s.a_fp, s.a_vaug, s.a_og,
                 s.a_qT, s.a_mask, s.a_stmp, s.a_state, s.a_den, s.a_rden, s.a_on, s.a_oTs, s.a_upd),
            act=(s.a_outs, s.a_sq, s.a_exp, s.a_tanh, s.a_kT, s.a_osq, s.a_ohi),
            pe=(s.a_past, s.a_outT, s.a_qk, s.a_vo, s.a_T, s.a_s, s.a_supd, s.a_o, s.a_oT, s.a_proj),
            pool=(s.a_ms, s.a_rn, s.a_oms, s.a_orn, s.a_x1))
        QK, VO, TQ, TK, S0, S1, OB, RB = bank

        def pipeline(eng, step):
            run_steps(eng, step, NT, 4)
        block = ctx.enter_context(nc.Block())

        @block.gpsimd
        def _(pool):
            prime(pool, *own["pool"])
            pool.memset(fpad[:], 0.0).then_inc(s.a_zero, 1)
            pool.memset(state[:], 0.0).then_inc(s.a_zero, 1)
            pool.memset(bd[:], 1.0).then_inc(s.a_zero, 1)
            pool.wait_ge(s.a_zero, 3)
            pool.affine_select(out=bd[:], in_=bd[:], compare_op=ALU.is_ge, fill=0.0, base=0,
                               pattern=[[0, HB], [-2 * DH, 4], [0, DV]], channel_multiplier=1).then_inc(s.a_zero, 1)
            pool.wait_ge(s.a_zero, 4)
            pool.affine_select(out=bd[:], in_=bd[:], compare_op=ALU.is_ge, fill=0.0, base=DH - 1,
                               pattern=[[0, HB], [2 * DH, 4], [0, DV]], channel_multiplier=-1).then_inc(s.a_zero, 1)

            def step(tile):
                if tile(4):
                    n, b, i = tile(4)
                    pool.wait_ge(s.a_upd, done(n))
                    xr = row(v.x1buf, n)
                    pool.tensor_tensor(xr, xr, upd[:], ALU.add).then_inc(s.a_x1, 1)
                if tile(3):
                    n, b, i = tile(3)
                    wait_alone(pool, s.a_osq, done(n))
                    pool.tensor_scalar(oms[:], oss[:], 1.0 / D, 1e-6, ALU.mult, ALU.add).then_inc(s.a_oms, 1)
                    pool.wait_ge(s.a_oms, done(n))
                    pool.wait_ge(s.a_ohi, done(n) - 1)
                    pool.tensor_tensor(orn[:], oms[:], v.neghalf[:, 0:1], ALU.pow).then_inc(s.a_orn, 1)
                if tile(0):
                    n, b, i = tile(0)
                    wait_alone(pool, s.a_sum, done(n))
                    pool.tensor_scalar(ms[:], ssum[:], 1.0 / DH, 1e-6 * WS * WS, ALU.mult, ALU.add).then_inc(s.a_ms, 1)
                    pool.wait_ge(s.a_ms, done(n))
                    pool.wait_ge(s.a_qn, done(n) - 1)
                    pool.tensor_tensor(rn[:], ms[:], v.neghalf[:, 0:NQ], ALU.pow).then_inc(s.a_rn, 1)

            pipeline(pool, step)

        @block.scalar
        def _(act):
            prime(act, *own["act"])

            def step(tile):
                if tile(2):
                    n, b, i = tile(2)
                    act.wait_ge(s.a_T, done(n))
                    act.wait_ge(s.a_o, done(n) - 1)
                    act.activation(qkT[:, 1, :], TK[:, 0:HB * P], ACT.Copy).then_inc(s.a_kT, 1)
                if tile(3):
                    n, b, i = tile(3)
                    act.wait_ge(s.a_on, done(n))
                    act.wait_ge(s.a_oms, done(n) - 1)
                    act.activation(osq[:], on[:], ACT.Square, accum_out=oss[:]).then_inc(s.a_osq, 1)
                    act.wait_ge(s.a_orn, done(n))
                    act.wait_ge(s.a_oT, done(n) - 1)
                    act.activation(op[:, 0, :], on[:], ACT.Copy, scale=orn[:, 0:1]).then_inc(s.a_ohi, 1)
                if tile(1):
                    n, b, i = tile(1)
                    act.wait_ge(s.a_neg, done(n))
                    act.activation(neg[:], neg[:], ACT.Exp).then_inc(s.a_exp, 1)
                if tile(0):
                    n, b, i = tile(0)
                    act.wait_ge(s.a_qk, done(n))
                    act.wait_ge(s.a_f, done(n) - 1)
                    act.activation(sq[:], QK[:, 0:2 * D], ACT.Square).then_inc(s.a_sq, 1)
                    act.wait_ge(s.a_vaug, done(n))
                    act.wait_ge(s.a_upd, done(n) - NB)
                    act.activation(og[:, b], VO[:, D:2 * D], ACT.Tanh, scale=0.5 / WS).then_inc(s.a_tanh, 1)
                if tile(2):
                    n, b, i = tile(2)
                    act.wait_ge(s.a_o, done(n))
                    act.wait_ge(s.a_outT, done(n) - 1)
                    act.activation(outT[:], OB[:, 0:HB * P], ACT.Copy).then_inc(s.a_outs, 1)

            pipeline(act, step)

        @block.tensor
        def _(pe):
            prime(pe, *own["pe"])

            def project(n):
                pe.wait_ge(s.a_qn, done(n) - 1)
                pe.wait_ge(s.a_vaug, done(n) - 1)
                pe.wait_ge(s.a_og, done(n) - 1)
                for k, (dst, signal) in enumerate(((QK, s.a_qk), (VO, s.a_vo))):
                    for j, (a, c) in enumerate(PAIRS):
                        mm = pe.matmul(dst[:, 0:2 * D], v.latT[:, a, bass.ds(n * P, P)],
                                       v.wlat[:, c, k * 2 * D:(k + 1) * 2 * D], start=(j == 0), stop=(j == 2))
                    mm.then_inc(signal, 1)

            def head_scores(n, half):
                pe.wait_ge(s.a_mask, done(n, 4, 2 * half - 1))
                for g in range(HB):
                    for jj in range(2):
                        j = 2 * half + jj
                        r = slice(32 * j, 32 * j + DH)
                        mm = pe.matmul((S0, S1)[jj][:, g * P:(g + 1) * P], qkT[r, 1, g * P:(g + 1) * P],
                                       qkT[r, 0, g * P:(g + 1) * P], start=True, stop=True)
                mm.then_inc(s.a_s, 1)

            def step(tile):
                if tile(2):
                    n, b, i = tile(2)
                    pe.wait_ge(s.a_fp, done(n))
                    pe.wait_ge(s.a_qT, done(n) - 1)
                    pe.wait_ge(s.a_kT, done(n) - 1)
                    for k, t in enumerate((TQ, TK)):
                        for g in range(HB):
                            blk = fpad[:, b % 2, k * H + 4 * g:k * H + 4 * g + 4, :].rearrange("p h d -> p (h d)")
                            mm = pe.transpose(t[:, g * P:(g + 1) * P], blk, v.ident)
                    mm.then_inc(s.a_T, 1)
                    pe.wait_ge(s.a_vaug, done(n))
                    pe.wait_ge(s.a_outs, done(n) - 1)
                    for g in range(HB):
                        blk = fpad[:, b % 2, H + 4 * g:H + 4 * g + 4, :].rearrange("p h d -> p (h d)")
                        mm = pe.matmul(OB[:, g * 4 * DV:(g + 1) * 4 * DV], blk,
                                       vaug[:, b, 4 * g:4 * g + 4, 0:DV], start=True, stop=True)
                    mm.then_inc(s.a_supd, 1)
                    pe.wait_ge(s.a_qT, done(n))
                    pe.wait_ge(s.a_kT, done(n))
                    pe.wait_ge(s.a_on, done(n) - 1)
                    head_scores(n, 0)
                    pe.wait_ge(s.a_state, done(n) - NB)
                    pe.wait_ge(s.a_stmp, done(n))
                    for g in range(HB):
                        mm = pe.matmul(OB[:, g * P:(g + 1) * P],
                                       state[:, b, 4 * g:4 * g + 4, :].rearrange("p h d -> p (h d)"),
                                       qkT[:, 0, g * P:(g + 1) * P], start=(g == 0), stop=False,
                                       skip_group_check=True)
                    mm.then_inc(s.a_past, 1)
                    head_scores(n, 1)
                if tile(0):
                    project(tile(0)[0])
                if tile(3):
                    n, b, i = tile(3)
                    pe.wait_ge(s.a_olo, done(n))
                    pe.wait_ge(s.a_upd, done(n) - 1)
                    for k in range(4):
                        mm = pe.transpose(half_bank(RB, 4 * P)[0:HD, k * P:(k + 1) * P],
                                          op[:, k // 2, (k % 2) * HD:(k % 2 + 1) * HD], v.ident16[:])
                    mm.then_inc(s.a_oT, 1)
                if tile(2):
                    n, b, i = tile(2)
                    for half in range(2):
                        pe.wait_ge(s.a_mask, done(n, 4, 2 * half + 1))
                        for g in range(HB):
                            for j in (2 * half, 2 * half + 1):
                                mm = pe.matmul(OB[32 * j:32 * j + 32, g * P:(g + 1) * P], vaug[:, b, 4 * g + j, :],
                                               att[:, j, g * P:(g + 1) * P], start=False,
                                               stop=(g == HB - 1 and j == 3), skip_group_check=True,
                                               tile_position=(0, 32 * j))
                    mm.then_inc(s.a_o, 1)
                if tile(3):
                    n, b, i = tile(3)
                    pe.wait_ge(s.a_oTs, done(n))
                    for j, (a, c) in enumerate(PAIRS):
                        for k in range(2):
                            mm = pe.matmul(RB[:, 2 * P:2 * P + D], oT[:, 2 * a + k, :], v.wproj[:, c, k, :],
                                           start=(j == 0 and k == 0), stop=(j == 2 and k == 1))
                    mm.then_inc(s.a_proj, 1)
                if tile(2):
                    n, b, i = tile(2)
                    pe.wait_ge(s.a_outs, done(n))
                    for g in range(HB):
                        mm = pe.transpose(S0[:, g * P:(g + 1) * P], outT[:, g * P:(g + 1) * P], v.ident)
                    mm.then_inc(s.a_outT, 1)

            pipeline(pe, step)

        @block.vector
        def _(dve):
            prime(dve, *own["dve"])
            dve.wait_ge(s.a_zero, 5)
            dve.memset(vaug[:], 0.0).then_inc(s.a_zero, 1)
            dve.wait_ge(s.a_zero, 6)
            dve.memset(vaug[:, :, :, DH:DV], 1.0).then_inc(s.a_zero, 1)
            dve.wait_ge(s.a_zero, 7)

            def mask(n, half):
                dve.wait_ge(s.a_s, done(n, 2, half))
                if half == 0:
                    dve.wait_ge(s.a_o, done(n) - 1)
                for jj in range(2):
                    dve.tensor_tensor(att[:, 2 * half + jj, :].rearrange("p (g n) -> p g n", g=HB),
                                      (S0, S1)[jj][:, 0:HB * P].rearrange("p (g n) -> p g n", g=HB),
                                      v.causal.rearrange("p (o n) -> p o n", o=1).broadcast_to([P, HB, P]),
                                      ALU.mult).then_inc(s.a_mask, 1)

            def step(tile):
                if tile(2):
                    n, b, i = tile(2)
                    dve.wait_ge(s.a_T, done(n))
                    dve.wait_ge(s.a_o, done(n) - 1)
                    dve.tensor_copy(qkT[:, 0, :], TQ[:, 0:HB * P]).then_inc(s.a_qT, 1)
                if tile(3):
                    n, b, i = tile(3)
                    dve.wait_ge(s.a_past, done(n))
                    kept = state[:, b, :, 0:DV]
                    dve.tensor_tensor(kept, kept, stmp[:].rearrange("p (h d) -> p h d", d=DV),
                                      ALU.add).then_inc(s.a_state, 1)
                if tile(2):
                    n, b, i = tile(2)
                    dve.wait_ge(s.a_supd, done(n))
                    dve.wait_ge(s.a_state, done(n) - 1)
                    dve.tensor_tensor(stmp[:], OB[:, 0:HB * 4 * DV], bd[:].rearrange("p g j d -> p (g j d)"),
                                      ALU.mult).then_inc(s.a_stmp, 1)
                if tile(4):
                    n, b, i = tile(4)
                    dve.wait_ge(s.a_proj, done(n))
                    dve.wait_ge(s.a_x1, done(n) - 1)
                    dve.wait_ge(s.a_og, done(n))
                    dve.scalar_tensor_tensor(upd[:], RB[:, 2 * P:2 * P + D], 1.0 / (WS * WS), og[:, b],
                                             ALU.mult, ALU.mult).then_inc(s.a_upd, 1)
                if tile(1):
                    n, b, i = tile(1)
                    dve.wait_ge(s.a_rn, done(n))
                    qk = QK[:, 0:2 * D].rearrange("p (h d) -> p h d", d=DH)
                    dve.tensor_tensor(qn[:].rearrange("p a h d -> p (a h) d"), qk,
                                      rn[:].rearrange("p (h u) -> p h u", u=1).broadcast_to([P, NQ, DH]),
                                      ALU.mult).then_inc(s.a_qn, 1)
                if tile(2):
                    n, b, i = tile(2)
                    mask(n, 0)
                if tile(1):
                    n, b, i = tile(1)
                    dve.wait_ge(s.a_qn, done(n))

                    def table(k):
                        return v.rope[:, k, :, bass.ds(i, 1), :].broadcast_to([P, 2, H, DH])
                    dve.tensor_tensor(t1[:], qn[:], table(0), ALU.mult).then_inc(s.a_t1, 1)
                    dve.tensor_tensor(qn[:], qn[:], table(1), ALU.mult).then_inc(s.a_t2, 1)
                    dve.wait_ge(s.a_t1, done(n))
                    dve.wait_ge(s.a_t2, done(n))
                    a = t1[:].rearrange("p a h d -> p (a h) d")
                    c = qn[:].rearrange("p a h d -> p (a h) d")
                    dve.tensor_tensor(rot[:, :, 0:hf], a[:, :, 0:hf], c[:, :, hf:], ALU.add).then_inc(s.a_rot, 1)
                    dve.tensor_tensor(rot[:, :, hf:], a[:, :, hf:], c[:, :, 0:hf], ALU.add).then_inc(s.a_rot, 1)
                    dve.wait_ge(s.a_rot, done(n, 2, 1))
                    rflat = rot[:].rearrange("p h d -> p (h d)")
                    dve.tensor_scalar(neg[:], rflat, 0.0, None, ALU.min).then_inc(s.a_neg, 1)
                if tile(3):
                    n, b, i = tile(3)
                    dve.wait_ge(s.a_ohi, done(n))
                    dve.scalar_tensor_tensor(op[:, 1, :], on[:], orn[:, 0:1], op[:, 0, :],
                                             ALU.mult, ALU.subtract).then_inc(s.a_olo, 1)
                if tile(2):
                    mask(tile(2)[0], 1)
                if tile(1):
                    n, b, i = tile(1)
                    rflat = rot[:].rearrange("p h d -> p (h d)")
                    dve.wait_ge(s.a_exp, done(n))
                    dve.scalar_tensor_tensor(rflat, rflat, 0.0, neg[:], ALU.max, ALU.add).then_inc(s.a_f, 1)
                    dve.wait_ge(s.a_f, done(n))
                    dve.wait_ge(s.a_supd, done(n) - 2)
                    dve.tensor_tensor(fpad[:, b % 2, :, 0:DH], rot[:],
                                      v.scale[:, bass.ds(i, 1), :].rearrange("p o (h u) -> p (o h) u", u=1)
                                      .broadcast_to([P, NQ, DH]), ALU.mult).then_inc(s.a_fp, 1)
                if tile(0):
                    n, b, i = tile(0)
                    dve.wait_ge(s.a_sq, done(n))
                    dve.wait_ge(s.a_ms, done(n) - 1)
                    dve.tensor_reduce(ssum[:], sq[:].rearrange("p (h d) -> p h d", d=DH),
                                      AX.X, ALU.add).then_inc(s.a_sum, 1)
                    dve.wait_ge(s.a_vo, done(n))
                    dve.wait_ge(s.a_o, done(n) - NB)
                    dve.tensor_tensor(vaug[:, b, :, 0:DH], VO[:, 0:D].rearrange("p (h d) -> p h d", d=DH),
                                      v.gates[:, bass.ds(n, 1), :].rearrange("p o (h u) -> p (o h) u", u=1)
                                      .broadcast_to([P, H, DH]), ALU.mult).then_inc(s.a_vaug, 1)
                if tile(3):
                    n, b, i = tile(3)
                    dve.wait_ge(s.a_oT, done(n))
                    dve.wait_ge(s.a_proj, done(n) - 1)
                    dve.tensor_copy(oT[:].rearrange("p c n -> p (c n)"), half_bank(RB, 4 * P)[0:HD, :]).then_inc(s.a_oTs, 1)
                if tile(0):
                    n, b, i = tile(0)
                    dve.wait_ge(s.a_tanh, done(n))
                    dve.scalar_tensor_tensor(og[:, b], og[:, b], 1.0, VO[:, D:2 * D],
                                             ALU.add, ALU.mult).then_inc(s.a_og, 1)
                if tile(2):
                    n, b, i = tile(2)
                    dve.wait_ge(s.a_outT, done(n))
                    num = S0[:, 0:HB * P].rearrange("p (h d) -> p h d", d=2 * DH)
                    dve.tensor_scalar(den[:], num[:, :, DH], 1e-5, None, ALU.max).then_inc(s.a_den, 1)
                    dve.wait_ge(s.a_den, done(n))
                    dve.reciprocal(rden[:], den[:]).then_inc(s.a_rden, 1)
                    dve.wait_ge(s.a_rden, done(n))
                    dve.wait_ge(s.a_olo, done(n) - 1)
                    dve.tensor_tensor(on[:].rearrange("p (h d) -> p h d", d=DH), num[:, :, 0:DH],
                                      rden[:].rearrange("p (h u) -> p h u", u=1).broadcast_to([P, H, DH]),
                                      ALU.mult).then_inc(s.a_on, 1)

            pipeline(dve, step)


def ffn(nc, sbuf, sems, prime, bank, v):
    v = named("Shared", v)
    NH = HID // P
    with ExitStack() as ctx:
        fsq = sbuf(ctx, "fsq", [P, D])
        ss = sbuf(ctx, "ss", [P, G])
        fms = sbuf(ctx, "fms", [P, G])
        frn = sbuf(ctx, "frn", [P, G])
        xn = sbuf(ctx, "xn", [P, 2, G, D], F16)
        xnT = sbuf(ctx, "xnT", [HD, 2, 2, G * P], F16)
        act_a = sbuf(ctx, "act_a", [P, 2, G * P])
        u = sbuf(ctx, "u", [P, 2, G * P])
        up = sbuf(ctx, "up", [P, 2, NH, G * P], F16)
        stat = sbuf(ctx, "fstat", [P, G, 6])
        mv = sbuf(ctx, "fmv", [P, G, 2])
        va = sbuf(ctx, "fva", [P, G])
        rs = sbuf(ctx, "frs", [P, G])
        xf = sbuf(ctx, "xf", [P, G, D])
        xp = sbuf(ctx, "xp", [P, 2, G, 2 * D], F16)
        xfT = sbuf(ctx, "xfT", [HD + 1, 2, 2, G * P], F16)
        top8 = sbuf(ctx, "top8", [P, G, 8])
        idx8 = sbuf(ctx, "idx8", [P, G, 8], U32)
        sc = sbuf(ctx, "sc", [P, G, E])
        hot = sbuf(ctx, "hot", [P, G, TOPK, E])
        hot_s = sbuf(ctx, "hot_s", [P, G, TOPK, E])
        mask = sbuf(ctx, "mask", [P, G, E])
        before = sbuf(ctx, "before", [P, G, E])
        region = sbuf(ctx, "region", [P, E])
        spare = sbuf(ctx, "spare", [2, E])
        rank = sbuf(ctx, "rank", [P, G, E])
        slot_f = sbuf(ctx, "slot_f", [P, G, TOPK])
        slot_i = sbuf(ctx, "slot_i", [P, 2, G, TOPK], I32)
        raw12 = sbuf(ctx, "raw12", [HD, 2, 2 * HID])
        raw3 = sbuf(ctx, "raw3", [P, NH, D])
        rawg = sbuf(ctx, "rawg", [HD + 1, 2, E])
        w12 = sbuf(ctx, "w12", [HD, 2, 2, 2 * HID], F16)
        w3s = sbuf(ctx, "w3s", [P, 2, NH, D], F16)
        gw = sbuf(ctx, "gw", [HD + 1, 2, 2, E], F16)
        s = sems("ld_w12", "ld_f", "f_w12_hi", "f_w12_lo", "f_w3_hi", "f_w3_lo", "f_const", "f_sq", "f_ms", "f_rn", "f_xh", "f_xl", "f_xT", "f_xTs", "f_ab",
                 "f_silu", "f_u", "f_uh", "f_ul", "f_w3", "f_hx", "f_h", "f_stat", "f_mv", "f_va", "f_rs", "f_xf",
                 "f_hi", "f_lo", "f_fT", "f_fTs", "f_gate", "f_score", "f_top", "f_idx", "f_pick", "f_hot", "f_m1",
                 "f_mask", "f_run", "f_rank", "f_place", "f_hs", "f_slot", "f_keep", "f_int", "f_store0",
                 "f_store1", "f_send0", "f_send1")
        f_send, f_store = (s.f_send0, s.f_send1), (s.f_store0, s.f_store1)
        own = dict(
            dve=(s.f_xl, s.f_u, s.f_ul, s.f_h, s.f_stat, s.f_mv, s.f_xf, s.f_lo, s.f_score, s.f_top, s.f_idx,
                 s.f_pick, s.f_hot, s.f_m1, s.f_mask, s.f_run, s.f_place, s.f_hs, s.f_slot, s.f_keep, s.f_int),
            act=(s.f_sq, s.f_xh, s.f_xTs, s.f_silu, s.f_uh, s.f_hi, s.f_fTs),
            pe=(s.f_xT, s.f_ab, s.f_w3, s.f_fT, s.f_gate, s.f_rank),
            pool=(s.f_ms, s.f_rn, s.f_hx, s.f_va, s.f_rs), sp=f_store)
        XA, XB, A0, B0, A1, B1, Y0, Y1 = bank
        SC, RK = Y0[:, 2 * D:2 * D + G * E], Y1[:, 2 * D:2 * D + G * E]
        block = ctx.enter_context(nc.Block())

        def pipeline(eng, step, last=2):
            run_steps(eng, step, NG, last, width=2)

        def first_group(i):
            return isinstance(i, int) and i == 0

        @block.sync
        def _(sp):
            sp.dma_start(raw12[:, :, 0:HID], halves(v.w1)).then_inc(s.ld_w12, 16)
            sp.dma_start(raw12[:, :, HID:], halves(v.w2)).then_inc(s.ld_w12, 16)
            sp.dma_start(raw3[:], v.w3.rearrange("(k p) n -> p k n", p=P)).then_inc(s.ld_f, 16)
            sp.dma_start(rawg[0:HD], halves(v.gate_w)).then_inc(s.ld_f, 16)
            sp.dma_start(rawg[HD:HD + 1, 0, :], v.gate_b.rearrange("(o n) -> o n", o=1)).then_inc(s.ld_f, 16)
            prime(sp, *own["sp"])
            with sp.Fori(0, NG // 2, 1) as j:
                for half in range(2):
                    i = j * 2 + half
                    sp.wait_ge(s.f_lo, done(i))
                    sp.dma_start(v.x_rows[bass.ds(i * (G * P), G * P), :].rearrange("(b p) d -> p b d", p=P),
                                 xp[:, half]).then_inc(f_store[half], 16)
            for store in f_store:
                sp.wait_ge(store, dma_done(NG // 2 - 1))

        @block.gpsimd
        def _(pool):
            prime(pool, *own["pool"])
            NS = G * TOPK
            for k, send in enumerate(f_send):
                pool.dma_start(spare[k:k + 1, :], v.c_rows[:, 0:E]).then_inc(send, 16)

            def step(tile):
                if tile(0):
                    i, half, j = tile(0)
                    wait_alone(pool, s.f_sq, done(i, G, G - 1))
                    pool.tensor_scalar(fms[:], ss[:], 1.0 / D, 1e-6, ALU.mult, ALU.add).then_inc(s.f_ms, 1)
                    pool.wait_ge(s.f_ms, done(i))
                    pool.wait_ge(s.f_xl, prev(i, G))
                    pool.tensor_tensor(frn[:], fms[:], v.neghalf[:, 0:G], ALU.pow).then_inc(s.f_rn, 1)
                if tile(2):
                    i, half, j = tile(2)
                    wait_alone(pool, s.f_mv, done(i, G, G - 1))
                    pool.tensor_scalar(va[:], mv[:, :, 1], 1e-5, None, ALU.add).then_inc(s.f_va, 1)
                    pool.wait_ge(s.f_va, done(i))
                    pool.wait_ge(s.f_xf, prev(i, G))
                    pool.tensor_tensor(rs[:], va[:], v.neghalf[:, 0:G], ALU.pow).then_inc(s.f_rs, 1)
                if tile(1):
                    i, half, j = tile(1)
                    pool.wait_ge(s.f_xl, done(i, G, G - 1))
                    hx = v.hbuf[:, bass.ds(i * G, G), :]
                    pool.tensor_tensor(hx, hx, v.x1buf[:, bass.ds(i * G, G), :], ALU.add).then_inc(s.f_hx, 1)
                if tile(3):
                    i, half, j = tile(3)
                    wait_alone(pool, s.f_int, done(i))
                    pool.wait_ge(s.f_lo, done(i))
                    for b in range(G):
                        for k in range(TOPK):
                            pool.indirect_dma_start(
                                v.x_rows, bass.IndirectOffsetOnAxis(ap=slot_i[:, half, b, k:k + 1], axis=0),
                                xp[:, half, b, :], None).then_inc(f_send[half], 16)

            pipeline(pool, step, 3)
            for send in f_send:
                pool.wait_ge(send, (NG // 2 * NS + 1) * 16)

        @block.scalar
        def _(act):
            prime(act, *own["act"])

            def fold_w12():
                act.wait_ge(s.ld_w12, 2 * 16)
                for k in range(2):
                    act.activation(w12[:, 0, k, :], raw12[:, k, :], ACT.Copy,
                                   scale=v.fcol[:, k:k + 1]).then_inc(s.f_w12_hi, 1)

            def fold_w3():
                act.wait_ge(s.ld_f, 3 * 16)
                act.activation(w3s[:, 0], raw3[:], ACT.Copy, scale=WS)
                act.activation(gw[:, 0, 0, :], rawg[:, 0, :], ACT.Copy, scale=WS)
                act.activation(gw[0:HD, 0, 1, :], rawg[0:HD, 1, :], ACT.Copy, scale=WS).then_inc(s.f_w3_hi, 1)

            def squares(i):
                for b in range(G):
                    act.wait_ge(s.f_ms, prev(i))
                    act.wait_ge(s.f_sq, done(i, G, b - 1))
                    act.activation(fsq[:], row(v.x1buf, i * G + b), ACT.Square,
                                   accum_out=ss[:, b:b + 1]).then_inc(s.f_sq, 1)

            def scaled(i):
                for b in range(G):
                    wait_alone(act, s.f_rn, done(i))
                    act.wait_ge(s.f_xT, prev(i))
                    act.activation(xn[:, 0, b, :], row(v.x1buf, i * G + b), ACT.Copy,
                                   scale=frn[:, b:b + 1]).then_inc(s.f_xh, 1)

            def hidden(i, k):
                act.wait_ge(s.f_ab, done(i, NH, k))
                act.wait_ge(s.f_u, done(i, NH, k - 2))
                act.activation(act_a[:, k % 2, :], (A0, A1)[k % 2][:], ACT.Silu, scale=1.0 / WS).then_inc(s.f_silu, 1)

            def hidden_hi(i, k):
                act.wait_ge(s.f_u, done(i, NH, k))
                act.wait_ge(s.f_w3, prev(i, 2))
                act.activation(up[:, 0, k, :], u[:, k % 2, :], ACT.Copy).then_inc(s.f_uh, 1)

            def step(tile):
                if tile(0):
                    squares(tile(0)[0])
                if tile(1):
                    hidden(tile(1)[0], 0)
                    hidden(tile(1)[0], 1)
                    hidden_hi(tile(1)[0], 0)
                if tile(2):
                    i, half, j = tile(2)
                    act.wait_ge(f_send[half], j * (16 * G * TOPK) + 16)
                    act.wait_ge(f_store[half], prev(j, 16))
                    act.wait_ge(s.f_xf, done(i, G, G - 1))
                    act.activation(xp[:, half, :, 0:D], xf[:], ACT.Copy).then_inc(s.f_hi, 1)
                if tile(0):
                    scaled(tile(0)[0])
                    if first_group(tile(0)[0]):
                        fold_w12()
                if tile(1):
                    hidden_hi(tile(1)[0], 1)
                    hidden(tile(1)[0], 2)
                if tile(2):
                    i, half, j = tile(2)
                    act.wait_ge(s.f_fT, done(i))
                    act.wait_ge(s.f_gate, prev(i))
                    for a, src in enumerate((XA, XB)):
                        ins = act.activation(xfT[0:HD, a].rearrange("d c n -> d (c n)"),
                                             half_bank(src, 8 * P)[0:HD, :], ACT.Copy)
                    ins.then_inc(s.f_fTs, 1)
                if tile(1):
                    i = tile(1)[0]
                    hidden_hi(i, 2)
                    hidden(i, 3)
                    hidden_hi(i, 3)
                if tile(0):
                    i = tile(0)[0]
                    act.wait_ge(s.f_xT, done(i))
                    act.wait_ge(s.f_ab, prev(i, NH))
                    for a, src in enumerate((XA, XB)):
                        ins = act.activation(xnT[:, a].rearrange("d c n -> d (c n)"), half_bank(src, 8 * P)[0:HD, :],
                                             ACT.Copy)
                    ins.then_inc(s.f_xTs, 1)
                    if first_group(i):
                        fold_w3()

            pipeline(act, step)

        @block.tensor
        def _(pe):
            prime(pe, *own["pe"])
            pe.wait_ge(s.f_const, 1)

            def turn(src, signal):
                for a, dst in enumerate((XA, XB)):
                    for b in range(G):
                        for k in range(2):
                            mm = pe.transpose(half_bank(dst, 8 * P)[0:HD, (k * G + b) * P:(k * G + b + 1) * P],
                                              src(a, b, k), v.ident16[:])
                mm.then_inc(signal, 1)

            def hidden(i, k):
                pe.wait_ge(s.f_u, done(i, NH, k - 2))
                for n, dst in enumerate(((A0, A1)[k % 2], (B0, B1)[k % 2])):
                    cols = slice(n * HID + k * P, n * HID + (k + 1) * P)
                    for m, (a, c) in enumerate(PAIRS):
                        for q in range(2):
                            mm = pe.matmul(dst[:], w12[:, a, q, cols], xnT[:, c, q, :],
                                           start=(m == 0 and q == 0), stop=(m == 2 and q == 1))
                mm.then_inc(s.f_ab, 1)

            def step(tile):
                if tile(1):
                    i, half, j = tile(1)
                    pe.wait_ge(s.f_xTs, done(i))
                    if first_group(i):
                        pe.wait_ge(s.f_w12_hi, 2)
                        pe.wait_ge(s.f_w12_lo, 2)
                    hidden(i, 0)
                    hidden(i, 1)
                    hidden(i, 2)
                if tile(2):
                    i, half, j = tile(2)
                    pe.wait_ge(s.f_xTs, done(i) + (1 if tile(1) else 0))
                    pe.wait_ge(s.f_lo, done(i))
                    turn(lambda a, b, k: xp[:, half, b, a * D + k * HD:a * D + (k + 1) * HD], s.f_fT)
                if tile(1):
                    hidden(tile(1)[0], 3)
                if tile(2):
                    i, half, j = tile(2)
                    pe.wait_ge(s.f_fTs, done(i))
                    pe.wait_ge(s.f_h, done(i, 2, 1))
                    for b in range(G):
                        for m, (a, c) in enumerate(PAIRS):
                            for q in range(2):
                                n = HD + 1 if (a, q) == (0, 0) else HD
                                mm = pe.matmul(SC[:, b * E:(b + 1) * E], xfT[0:n, a, q, b * P:(b + 1) * P],
                                               gw[0:n, c, q, :], start=(m == 0 and q == 0), stop=(m == 2 and q == 1))
                    mm.then_inc(s.f_gate, 1)
                if tile(0):
                    i, half, j = tile(0)
                    pe.wait_ge(s.f_xl, done(i, G, G - 1))
                    pe.wait_ge(s.f_xh, done(i, G, G - 1))
                    pe.wait_ge(s.f_fTs, done(i) - 2)
                    turn(lambda a, b, k: xn[:, a, b, k * HD:(k + 1) * HD], s.f_xT)
                if tile(1):
                    i, half, j = tile(1)
                    if first_group(i):
                        pe.wait_ge(s.f_w3_hi, 1)
                        pe.wait_ge(s.f_w3_lo, 1)
                    pe.wait_ge(s.f_score, done(i) - 1)
                    pe.wait_ge(s.f_h, prev(i, 2))
                    for b in range(G):
                        for k in range(NH):
                            if b == 0:
                                pe.wait_ge(s.f_uh, done(i, NH, k))
                                pe.wait_ge(s.f_ul, done(i, NH, k))
                            for m, (a, c) in enumerate(PAIRS):
                                mm = pe.matmul((Y0, Y1)[b // 2][:, (b % 2) * D:(b % 2 + 1) * D],
                                               up[:, a, k, b * P:(b + 1) * P], w3s[:, c, k, :],
                                               start=(m == 0 and k == 0), stop=(m == 2 and k == NH - 1))
                        if b % 2:
                            mm.then_inc(s.f_w3, 1)
                if tile(2):
                    i, half, j = tile(2)
                    pe.wait_ge(s.f_run, done(i, G, G - 1))
                    pe.matmul(RK, v.ones, before[:].rearrange("p b e -> p (b e)"), start=True, stop=False)
                    pe.matmul(RK, v.strict, mask[:].rearrange("p b e -> p (b e)"),
                              start=False, stop=True).then_inc(s.f_rank, 1)

            pipeline(pe, step)

        @block.vector
        def _(dve):
            prime(dve, *own["dve"])
            dve.memset(xfT[HD:HD + 1, 0, 0, :], 1.0).then_inc(s.f_const, 1)
            dve.tensor_scalar(region[:], v.rows[:, 0:E], float(REGION), None, ALU.mult)

            def fold_w12():
                dve.wait_ge(s.ld_w12, 2 * 16)
                for k in range(2):
                    dve.wait_ge(s.f_w12_hi, k + 1)
                    dve.scalar_tensor_tensor(w12[:, 1, k, :], raw12[:, k, :], v.fcol[:, k:k + 1], w12[:, 0, k, :],
                                             ALU.mult, ALU.subtract).then_inc(s.f_w12_lo, 1)

            def fold_w3():
                dve.wait_ge(s.ld_f, 3 * 16)
                dve.wait_ge(s.f_w3_hi, 1)
                dve.scalar_tensor_tensor(w3s[:, 1], raw3[:], WS, w3s[:, 0], ALU.mult, ALU.subtract)
                dve.scalar_tensor_tensor(gw[:, 1, 0, :], rawg[:, 0, :], WS, gw[:, 0, 0, :], ALU.mult, ALU.subtract)
                dve.scalar_tensor_tensor(gw[0:HD, 1, 1, :], rawg[0:HD, 1, :], WS, gw[0:HD, 0, 1, :],
                                         ALU.mult, ALU.subtract).then_inc(s.f_w3_lo, 1)

            def scaled_lo(i):
                dve.wait_ge(s.f_rn, done(i))
                for b in range(G):
                    dve.wait_ge(s.f_xh, done(i, G, b))
                    dve.scalar_tensor_tensor(xn[:, 1, b, :], row(v.x1buf, i * G + b), frn[:, b:b + 1], xn[:, 0, b, :],
                                             ALU.mult, ALU.subtract).then_inc(s.f_xl, 1)

            def hidden(i, k):
                dve.wait_ge(s.f_silu, done(i, NH, k))
                dve.wait_ge(s.f_uh, done(i, NH, k - 2))
                dve.wait_ge(s.f_ul, done(i, NH, k - 2))
                dve.scalar_tensor_tensor(u[:, k % 2, :], (B0, B1)[k % 2][:], 1.0 / WS, act_a[:, k % 2, :],
                                         ALU.mult, ALU.mult).then_inc(s.f_u, 1)

            def hidden_lo(i, k):
                dve.wait_ge(s.f_uh, done(i, NH, k))
                dve.tensor_tensor(up[:, 1, k, :], u[:, k % 2, :], up[:, 0, k, :], ALU.subtract).then_inc(s.f_ul, 1)

            def read_scores(i):
                dve.wait_ge(s.f_gate, done(i))
                dve.tensor_scalar(sc[:], SC.rearrange("p (b e) -> p b e", b=G), 1.0 / WS, None,
                                  ALU.mult).then_inc(s.f_score, 1)

            def choose(i):
                dve.wait_ge(s.f_score, done(i))
                dve.tensor_copy(v.scores[:, bass.ds(i * G, G), :], sc[:]).then_inc(s.f_keep, 1)
                for b in range(G):
                    dve.max(top8[:, b, :], sc[:, b, 1:E]).then_inc(s.f_top, 1)
                for b in range(G):
                    wait_alone(dve, s.f_top, done(i, G, b))
                    dve.max_index(idx8[:, b, :], top8[:, b, :], sc[:, b, 1:E]).then_inc(s.f_idx, 1)
                dve.wait_ge(s.f_idx, done(i, G, G - 1))
                pick = v.picked[:, bass.ds(i * G, G), :]
                dve.tensor_scalar(pick, idx8[:, :, 0:TOPK], 1.0, None, ALU.add).then_inc(s.f_pick, 1)
                dve.tensor_copy(v.score3[:, bass.ds(i * G, G), :], top8[:, :, 0:TOPK]).then_inc(s.f_keep, 1)
                dve.wait_ge(s.f_pick, done(i))
                flat = hot[:].rearrange("p b k e -> p (b k) e")
                dve.tensor_tensor(flat,
                                  v.rows[:, 0:E].rearrange("p (o e) -> p o e", o=1).broadcast_to([P, G * TOPK, E]),
                                  pick.rearrange("p b (k u) -> p (b k) u", u=1).broadcast_to([P, G * TOPK, E]),
                                  ALU.is_equal).then_inc(s.f_hot, 1)
                dve.wait_ge(s.f_hot, done(i))
                dve.wait_ge(s.f_rank, prev(i))
                dve.tensor_tensor(mask[:], hot[:, :, 0, :], hot[:, :, 1, :], ALU.add).then_inc(s.f_m1, 1)
                dve.wait_ge(s.f_m1, done(i))
                dve.tensor_tensor(mask[:], mask[:], hot[:, :, 2, :], ALU.add).then_inc(s.f_mask, 1)
                dve.wait_ge(s.f_mask, done(i))
                for b in range(G):
                    if b == 0:
                        dve.tensor_copy(before[:, 0, :], v.chosen[:]).then_inc(s.f_run, 1)
                    else:
                        dve.tensor_tensor(before[:, b, :], before[:, b - 1, :], mask[:, b - 1, :],
                                          ALU.add).then_inc(s.f_run, 1)
                    dve.wait_ge(s.f_run, done(i, G, b))
                dve.tensor_tensor(v.chosen[:], before[:, G - 1, :], mask[:, G - 1, :], ALU.add).then_inc(s.f_keep, 1)

            def locate(i, half):
                dve.wait_ge(s.f_rank, done(i))
                dve.tensor_tensor(rank[:], RK.rearrange("p (b e) -> p b e", b=G),
                                  region[:].rearrange("p (o e) -> p o e", o=1).broadcast_to([P, G, E]),
                                  ALU.add).then_inc(s.f_place, 1)
                dve.wait_ge(s.f_place, done(i))
                for k in range(TOPK):
                    dve.tensor_tensor(hot_s[:, :, k, :], hot[:, :, k, :], rank[:], ALU.mult).then_inc(s.f_hs, 1)
                dve.wait_ge(s.f_hs, done(i, TOPK, TOPK - 1))
                dve.tensor_reduce(slot_f[:].rearrange("p b k -> p (b k)"), hot_s[:].rearrange("p b k e -> p (b k) e"),
                                  AX.X, ALU.add).then_inc(s.f_slot, 1)
                dve.wait_ge(s.f_slot, done(i))
                dve.tensor_copy(v.place[:, bass.ds(i * G, G), :], slot_f[:]).then_inc(s.f_keep, 1)
                dve.tensor_copy(slot_i[:, half], slot_f[:]).then_inc(s.f_int, 1)
                dve.wait_ge(s.f_keep, done(i, 4, 3))

            def step(tile):
                if tile(2):
                    i, half, j = tile(2)
                    dve.wait_ge(s.f_hx, done(i))
                    for k in range(2):
                        dve.wait_ge(s.f_w3, done(i, 2, k))
                        hh = v.hbuf[:, bass.ds(i * G + 2 * k, 2), :]
                        dve.scalar_tensor_tensor(hh, (Y0, Y1)[k][:, 0:2 * D].rearrange("p (b d) -> p b d", b=2),
                                                 1.0 / WS, hh, ALU.mult, ALU.add).then_inc(s.f_h, 1)
                    for b in range(G):
                        wait_alone(dve, s.f_h, done(i, 2, b // 2))
                        dve.bn_stats(stat[:, b, :], row(v.hbuf, i * G + b)).then_inc(s.f_stat, 1)
                    for b in range(G):
                        wait_alone(dve, s.f_stat, done(i, G, b))
                        dve.bn_aggr(mv[:, b, :], stat[:, b, :]).then_inc(s.f_mv, 1)
                if tile(1):
                    hidden(tile(1)[0], 0)
                if tile(2):
                    i, half, j = tile(2)
                    dve.wait_ge(s.f_rs, done(i))
                    dve.wait_ge(s.f_lo, prev(i))
                    for b in range(G):
                        dve.tensor_scalar(xf[:, b, :], row(v.hbuf, i * G + b), mv[:, b, 0:1], rs[:, b:b + 1],
                                          ALU.subtract, ALU.mult).then_inc(s.f_xf, 1)
                if tile(1):
                    hidden(tile(1)[0], 1)
                    hidden_lo(tile(1)[0], 0)
                if tile(2):
                    i, half, j = tile(2)
                    dve.wait_ge(s.f_hi, done(i))
                    dve.tensor_tensor(xp[:, half, :, D:], xf[:], xp[:, half, :, 0:D],
                                      ALU.subtract).then_inc(s.f_lo, 1)
                if tile(1):
                    hidden_lo(tile(1)[0], 1)
                    hidden(tile(1)[0], 2)
                if tile(0):
                    scaled_lo(tile(0)[0])
                    if first_group(tile(0)[0]):
                        fold_w12()
                        fold_w3()
                if tile(1):
                    hidden_lo(tile(1)[0], 2)
                if tile(2):
                    read_scores(tile(2)[0])
                if tile(1):
                    i = tile(1)[0]
                    hidden(i, 3)
                    hidden_lo(i, 3)
                if tile(2):
                    i, half, j = tile(2)
                    choose(i)
                    locate(i, half)

            pipeline(dve, step)


def experts(nc, sbuf, sems, prime, bank, v):
    v = named("Shared", v)
    with ExitStack() as ctx:
        TILES = NT + RT
        e_of = sbuf(ctx, "e_of", [1, TILES], I32)
        r_of = sbuf(ctx, "r_of", [1, TILES], I32)
        count = sbuf(ctx, "count", [P, E])
        count_i = sbuf(ctx, "count_i", [P, E], I32)
        tiles = sbuf(ctx, "tiles", [P, E])
        ends = sbuf(ctx, "ends", [P, E])
        onesE = sbuf(ctx, "onesE", [P, E])
        past = sbuf(ctx, "past", [P, 2, E - 1])
        sums = sbuf(ctx, "sums", [P, 2])
        used = sbuf(ctx, "used", [P, 1])
        table = sbuf(ctx, "table", [P, 2])
        pad_f = sbuf(ctx, "pad_f", [P, E])
        pad_i = sbuf(ctx, "pad_i", [P, E], I32)
        zero = sbuf(ctx, "zero", [P, 2 * D], F16)
        xin = sbuf(ctx, "xin", [P, 4, 2 * D], F16)
        xT = sbuf(ctx, "exT", [HD + 1, 2, 4, P], F16)
        h = sbuf(ctx, "h", [P, 2, FH])
        hp = sbuf(ctx, "hp", [P, 2, 2, FH], F16)
        hT = sbuf(ctx, "hT", [P, 2, 2, FH], F16)
        st = sbuf(ctx, "est", [P, 2, 6])
        mv = sbuf(ctx, "emv", [P, 4, 2])
        va = sbuf(ctx, "eva", [P, 4])
        rs = sbuf(ctx, "ers", [P, 4])
        y = sbuf(ctx, "y", [P, 4, D])
        slot = sbuf(ctx, "slot", [P, NT, TOPK])
        NK = NT * TOPK
        hot = v.x1buf[:, 0:NK * E // D, :].rearrange("p t d -> p (t d)").rearrange("p (n e) -> p n e", e=E)
        s = sems("t_cnt", "t_chain", "t_shared", "t_table", "t_turned", "t_ok", "t_pad", "t_zero", "t_padded", "t_slot", "e_one",
                 "e_in0", "e_in1", "e_in2", "e_in3", "e_xT", "e_xTs", "e_h", "e_gelu", "e_hi", "e_lo", "e_st",
                 "e_mv", "e_va", "e_rs", "e_hT", "e_hTa", "e_hTv", "e_y", "e_ys", "e_out0", "e_out1", "e_out2",
                 "e_out3")
        e_in = (s.e_in0, s.e_in1, s.e_in2, s.e_in3)
        e_out = (s.e_out0, s.e_out1, s.e_out2, s.e_out3)
        own = dict(dve=(s.e_xTs, s.e_lo, s.e_st, s.e_mv, s.e_hTv), act=(s.e_gelu, s.e_hi, s.e_hTa, s.e_ys),
                   pe=(s.e_xT, s.e_h, s.e_hT, s.e_y), pool=(s.e_va, s.e_rs), sp=e_in + e_out)
        XT, HP, HTA, HTV, YP = bank[0], (bank[1], bank[2]), bank[3], bank[4], (bank[5], bank[6])
        block = ctx.enter_context(nc.Block())

        def at(n):
            return slice(n, n + 1) if isinstance(n, int) else bass.ds(n, 1)

        def pipeline(eng, step, last, **options):
            run_steps(eng, step, TILES, last, **options)

        @block.sync
        def _(sp):
            prime(sp, *own["sp"])
            sp.wait_ge(s.t_shared, 1)

            def before_routed():
                sp.wait_ge(s.t_ok, 1)
                sp.wait_ge(s.t_padded, (E - 1) * 16)

            def step(tile):
                if tile(0):
                    n, k, turn = tile(0)
                    row = sp.value_load(r_of[0:1, at(n)], min_val=0, max_val=(E * REGION - P))
                    sp.wait_ge(s.e_xT, done(n) - 4)
                    sp.dma_start(xin[:, k, :], v.x_rows[bass.ds(row, P), :]).then_inc(e_in[k], 16)
                if tile(8):
                    n, k, turn = tile(8)
                    sp.wait_ge(s.e_ys, done(n))
                    routed = SHARED_FIRST <= n < SHARED_FIRST + RT if isinstance(n, int) else stores == ["routed"]
                    if routed:
                        dst = v.y_rows[bass.ds((n - SHARED_FIRST) * P, P), :]
                    elif isinstance(n, int) and n >= SHARED_FIRST + RT:
                        dst = v.y_shared[(n - RT) * P:(n - RT + 1) * P, :]
                    else:
                        dst = v.y_shared[bass.ds(n * P, P), :]
                    sp.dma_start(dst, y[:, k, :]).then_inc(e_out[k], 16)

            stores = ["shared"]

            def routed_stores():
                stores[0] = "routed"

            first = SHARED_FIRST // 4
            pipeline(sp, step, 8, pauses=((first, before_routed), (first + 2, routed_stores)),
                     loop_end=(SHARED_FIRST + RT + 8) // 4)
            for k in range(4):
                sp.wait_ge(e_out[k], dma_done((TILES - 1 - k) // 4))

        @block.gpsimd
        def _(pool):
            prime(pool, *own["pool"])
            pool.memset(zero[:], 0.0).then_inc(s.t_zero, 1)
            pool.wait_ge(s.t_pad, 1)
            pool.wait_ge(s.t_zero, 1)
            for e in range(1, E):
                pool.indirect_dma_start(v.x_rows, bass.IndirectOffsetOnAxis(ap=pad_i[:, e:e + 1], axis=0),
                                        zero[:], None).then_inc(s.t_padded, 16)

            def step(tile):
                n, k, turn = tile(0)
                scale2 = (WS * HS) ** 2
                wait_alone(pool, s.e_mv, done(n))
                pool.tensor_scalar(va[:, k:k + 1], mv[:, k, 1:2], scale2, 1e-5 * scale2,
                                   ALU.mult, ALU.add).then_inc(s.e_va, 1)
                pool.wait_ge(s.e_va, done(n))
                pool.wait_ge(s.e_ys, done(n) - 4)
                pool.tensor_tensor(rs[:, k:k + 1], va[:, k:k + 1], v.neghalf[:, 0:1], ALU.pow).then_inc(s.e_rs, 1)

                if isinstance(n, int) and n >= GATHER_FROM:
                    if n == GATHER_FROM:
                        pool.wait_ge(s.t_slot, 1)
                        for m in range(4):
                            pool.wait_ge(e_out[m], dma_done((SHARED_FIRST + RT - 1 - m) // 4))
                    for t, c in v.gathers[2 * (n - GATHER_FROM):min(2 * (n - GATHER_FROM) + 2, v.EARLY)]:
                        v.gather(pool, t, c)

            pipeline(pool, step, 0, loop_end=GATHER_FROM // 4)

        @block.tensor
        def _(pe):
            prime(pe, *own["pe"])
            pe.matmul(bank[7][:, 256:256 + E], v.ones, v.chosen[:], start=True, stop=True).then_inc(s.t_cnt, 1)
            pe.wait_ge(s.e_one, 1)
            pe.wait_ge(s.t_table, 1)
            for k in range(2):
                mm = pe.matmul(bank[7][0:1, k * P:(k + 1) * P], table[:, k:k + 1], v.ident, start=True, stop=True)
            mm.then_inc(s.t_turned, 1)
            pe.wait_ge(s.t_ok, 1)

            experts_of = {}

            def load_experts(q):
                lo, hi = (max(q * 4 - 3, 0), min(q * 4 + 3, TILES)) if isinstance(q, int) else (q * 4 - 3, q * 4 + 3)
                table = e_of[0:1, lo:hi] if isinstance(q, int) else e_of[0:1, bass.ds(lo, 6)]
                _, values = nc.values_load_multi_w_load_instructions(
                    table, engines=[mybir.EngineType.PE], min_val=0, max_val=E - 1,
                    skip_runtime_bounds_check_because="the table holds 1 + a count of at most 14, or 0")
                first = lo if isinstance(q, int) else -3
                experts_of.clear()
                experts_of.update({first + j: e for j, e in enumerate(values)})

            def step(tile):
                def key(behind):
                    n, k, turn = tile(behind)
                    return n if isinstance(n, int) else tile.slot - behind

                if tile(0):
                    n, k, turn = tile(0)
                    pe.wait_ge(e_in[k], dma_done(turn))
                    pe.wait_ge(s.e_xTs, done(n) - 1)
                    xt = half_bank(XT, 4 * P)
                    for c in range(4):
                        mm = pe.transpose(xt[0:HD, c * P:(c + 1) * P], xin[:, k, c * HD:(c + 1) * HD], v.ident16[:])
                    mm.then_inc(s.e_xT, 1)
                if tile(1):
                    n, k, turn = tile(1)
                    m = k % 2
                    w = v.W1[:, bass.ds(experts_of[key(1)], 1)].rearrange("p o a c n -> p (o a) c n")
                    pe.wait_ge(s.e_xTs, done(n))
                    pe.wait_ge(s.e_gelu, done(n) - 2)
                    for j, (a, b) in enumerate(PAIRS):
                        for c in range(2):
                            rows = HD + 1 if (a, c) == (0, 0) else HD
                            mm = pe.matmul(HP[m][:, 0:FH], xT[0:rows, m, 2 * a + c, :], w[0:rows, b, c, :],
                                           start=(j == 0 and c == 0), stop=(j == 2 and c == 1))
                    mm.then_inc(s.e_h, 1)
                if tile(3):
                    n, k, turn = tile(3)
                    m = k % 2
                    w = v.W2[:, bass.ds(experts_of[key(3)], 1)].rearrange("p o a c n -> p (o a) c n")
                    pe.wait_ge(s.e_hTa, done(n))
                    pe.wait_ge(s.e_hTv, done(n))
                    pe.wait_ge(s.e_ys, done(n) - 2)
                    for j, (a, b) in enumerate(PAIRS):
                        for c in range(FK):
                            mm = pe.matmul(YP[m][:, 0:D], hT[:, m, a, c * P:(c + 1) * P], w[:, b, c, :],
                                           start=(j == 0 and c == 0), stop=(j == 2 and c == FK - 1))
                    mm.then_inc(s.e_y, 1)
                if tile(2):
                    n, k, turn = tile(2)
                    m = k % 2
                    pe.wait_ge(s.e_lo, done(n))
                    pe.wait_ge(s.e_hTa, done(n) - 1)
                    pe.wait_ge(s.e_hTv, done(n) - 1)
                    for a, dst in enumerate((HTA, HTV)):
                        for c in range(FK):
                            mm = pe.transpose(half_bank(dst, FH)[:, c * P:(c + 1) * P],
                                              hp[:, m, a, c * P:(c + 1) * P], v.ident16[:])
                    mm.then_inc(s.e_hT, 1)

            pipeline(pe, step, 3, turn_start=load_experts)

        @block.scalar
        def _(act):
            prime(act, *own["act"])

            def step(tile):
                if tile(1):
                    n, k, turn = tile(1)
                    m = k % 2
                    act.wait_ge(s.e_h, done(n))
                    act.wait_ge(s.e_lo, done(n) - 2)
                    act.wait_ge(s.e_st, done(n) - 2)
                    act.activation(h[:, m, :], HP[m][:, 0:FH], ACT.Gelu, scale=1.0 / WS).then_inc(s.e_gelu, 1)
                    act.wait_ge(s.e_gelu, done(n))
                    act.wait_ge(s.e_hT, done(n) - 2)
                    act.activation(hp[:, m, 0, :], h[:, m, :], ACT.Copy, scale=HS).then_inc(s.e_hi, 1)
                if tile(2):
                    n, k, turn = tile(2)
                    act.wait_ge(s.e_hT, done(n))
                    act.wait_ge(s.e_y, done(n) - 2)
                    act.activation(hT[:, k % 2, 0, :], half_bank(HTA, FH), ACT.Copy).then_inc(s.e_hTa, 1)
                if tile(3):
                    n, k, turn = tile(3)
                    act.wait_ge(s.e_y, done(n))
                    act.wait_ge(s.e_rs, done(n))
                    act.wait_ge(e_out[k], prev(turn, 16))
                    act.activation(y[:, k, :], YP[k % 2][:, 0:D], ACT.Copy, scale=rs[:, k:k + 1]).then_inc(s.e_ys, 1)

            pipeline(act, step, 3)

        @block.vector
        def _(dve):
            prime(dve, *own["dve"])
            n_link = [0]

            def link(ins):
                n_link[0] += 1
                ins.then_inc(s.t_chain, 1)
                dve.wait_ge(s.t_chain, n_link[0])

            dve.memset(xT[HD:HD + 1, :, :], 1.0).then_inc(s.e_one, 1)
            link(dve.memset(e_of[:], 0))
            for at_tile, first, n in ((0, 0, SHARED_FIRST), (SHARED_FIRST + RT, SHARED_FIRST, NT - SHARED_FIRST)):
                link(dve.tensor_scalar(r_of[:, at_tile:at_tile + n], v.rows[0:1, first:first + n], float(P), None,
                                       ALU.mult))
            dve.sem_inc(s.t_shared, 1)
            dve.wait_ge(s.t_cnt, 1)
            link(dve.tensor_copy(count[:], bank[7][:, 256:256 + E]))
            link(dve.scalar_tensor_tensor(pad_f[:], v.rows[:, 0:E], float(REGION), count[:], ALU.mult, ALU.add))
            link(dve.tensor_scalar(pad_f[:], pad_f[:], v.lpos[:, NG:NG + 1], None, ALU.add))
            dve.tensor_copy(pad_i[:], pad_f[:]).then_inc(s.t_pad, 1)
            link(dve.tensor_scalar(count_i[:], count[:], float(P - 1), None, ALU.add))
            link(dve.tensor_scalar(count_i[:], count_i[:], P.bit_length() - 1, None, ALU.logical_shift_right))
            link(dve.tensor_copy(tiles[:], count_i[:]))
            link(dve.memset(onesE[:], 1.0))
            link(dve.tensor_tensor_scan(ends[:], onesE[:], tiles[:], 0.0, ALU.mult, ALU.add))
            i_col = v.lpos[:, NG:NG + 1]
            link(dve.tensor_scalar(past[:, 0, :], ends[:, 1:E], i_col, None, ALU.is_le))
            link(dve.tensor_tensor(past[:, 1, :], past[:, 0, :], tiles[:, 1:E], ALU.mult))
            link(dve.tensor_reduce(sums[:], past[:], AX.X, ALU.add))
            link(dve.tensor_scalar(used[:], ends[:, E - 1:E], i_col, None, ALU.is_gt))
            link(dve.tensor_scalar(sums[:, 0:1], sums[:, 0:1], used[:, 0:1], 1.0, ALU.mult, ALU.add))
            link(dve.tensor_scalar(sums[:, 1:2], sums[:, 1:2], i_col, used[:, 0:1], ALU.subtract, ALU.mult))
            link(dve.tensor_scalar(sums[:, 1:2], sums[:, 1:2], -float(P), None, ALU.mult))
            link(dve.tensor_copy(table[:, 0:1], sums[:, 0:1]))
            link(dve.scalar_tensor_tensor(table[:, 1:2], sums[:, 0:1], float(REGION), sums[:, 1:2],
                                          ALU.mult, ALU.add))
            dve.sem_inc(s.t_table, 1)
            dve.wait_ge(s.t_turned, 1)
            link(dve.tensor_copy(e_of[:, SHARED_FIRST:SHARED_FIRST + RT], bank[7][0:1, 0:RT]))
            link(dve.tensor_copy(r_of[:, SHARED_FIRST:SHARED_FIRST + RT], bank[7][0:1, P:P + RT]))
            dve.sem_inc(s.t_ok, 1)
            link(dve.tensor_tensor(v.y_row[:], ends[:], tiles[:], ALU.subtract))
            link(dve.tensor_scalar(v.y_row[:], v.y_row[:], float(P), None, ALU.mult))
            link(dve.scalar_tensor_tensor(v.y_row[:], v.rows[:, 0:E], -float(REGION), v.y_row[:], ALU.mult, ALU.add))

            def step(tile):
                if tile(0):
                    n, k, turn = tile(0)
                    dve.wait_ge(s.e_xT, done(n))
                    dve.wait_ge(s.e_h, done(n) - 2)
                    dve.tensor_copy(xT[0:HD, k % 2], half_bank(XT, 4 * P)[0:HD, :].rearrange("p (c t) -> p c t", c=4)
                                    ).then_inc(s.e_xTs, 1)
                if tile(1):
                    n, k, turn = tile(1)
                    m = k % 2
                    wait_alone(dve, s.e_gelu, done(n))
                    dve.bn_stats(st[:, m, :], h[:, m, :]).then_inc(s.e_st, 1)
                    dve.wait_ge(s.e_hi, done(n))
                    dve.scalar_tensor_tensor(hp[:, m, 1, :], h[:, m, :], HS, hp[:, m, 0, :],
                                             ALU.mult, ALU.subtract).then_inc(s.e_lo, 1)
                if tile(2):
                    n, k, turn = tile(2)
                    dve.wait_ge(s.e_hT, done(n))
                    dve.wait_ge(s.e_y, done(n) - 2)
                    dve.tensor_copy(hT[:, k % 2, 1, :], half_bank(HTV, FH)).then_inc(s.e_hTv, 1)
                if tile(1):
                    n, k, turn = tile(1)
                    m = k % 2
                    wait_alone(dve, s.e_st, done(n))
                    dve.wait_ge(s.e_va, done(n) - 4)
                    dve.bn_aggr(mv[:, k, :], st[:, m, :]).then_inc(s.e_mv, 1)

            ek = v.picked[:].rearrange("p t (k u) -> p (t k) u", u=1).broadcast_to([P, NK, E])
            of_all = lambda a: a.rearrange("p (o e) -> p o e", o=1).broadcast_to([P, NK, E])

            def slots_hot():
                link(dve.tensor_tensor(hot, of_all(v.rows[:, 0:E]), ek, ALU.is_equal))

            def slots_base():
                link(dve.tensor_tensor(hot, hot, of_all(v.y_row[:]), ALU.mult))

            def slots_sum():
                link(dve.tensor_reduce(slot[:].rearrange("p t k -> p (t k)"), hot, AX.X, ALU.add))

            def slots_whole():
                link(dve.tensor_tensor(slot[:], slot[:], v.place[:], ALU.add))
                dve.tensor_copy(v.slot_i[:], slot[:]).then_inc(s.t_slot, 1)

            pipeline(dve, step, 2, pauses=((5, slots_hot), (10, slots_base), (15, slots_sum), (20, slots_whole)))


def combine(nc, sbuf, sems, prime, bank, v):
    v = named("Shared", v)
    NK = NT * TOPK
    with ExitStack() as ctx:
        w3 = sbuf(ctx, "w3k", [P, NT, TOPK])
        ex = sbuf(ctx, "ex", [P, NT, E])
        sm = sbuf(ctx, "sm", [P, NT])
        rsm = sbuf(ctx, "rsm", [P, NT])
        hot = sbuf(ctx, "chot", [P, NK, E])
        tmp = sbuf(ctx, "ctmp", [P, NK, E])
        comb = sbuf(ctx, "comb", [P, NT, E])
        BUFS = 4
        ysh = sbuf(ctx, "ysh", [P, BUFS, D])
        cT = sbuf(ctx, "cT", [E, NT * P])
        o = sbuf(ctx, "o", [P, BUFS, D])
        s = sems("c_chain", "c_exp_in", "c_exp", "c_comb", "c_sh0", "c_sh1", "c_sh2", "c_sh3", "c_T",
                 "c_Ts", "c_b", "c_a1", "c_a2", "c_o", "c_out0", "c_out1", "c_out2", "c_out3")
        c_sh, c_out = (s.c_sh0, s.c_sh1, s.c_sh2, s.c_sh3), (s.c_out0, s.c_out1, s.c_out2, s.c_out3)
        block = ctx.enter_context(nc.Block())

        @block.scalar
        def _(act):
            def load(t):
                if t >= BUFS:
                    act.wait_ge(s.c_b, t - BUFS + 1)
                act.dma_start(ysh[:, t % BUFS, :], v.y_shared[t * P:(t + 1) * P, :]).then_inc(c_sh[t % BUFS], 16)

            for t in range(BUFS):
                load(t)
            act.wait_ge(s.c_exp_in, 1)
            act.activation(ex[:], ex[:], ACT.Exp).then_inc(s.c_exp, 1)
            act.activation(w3[:], w3[:], ACT.Exp).then_inc(s.c_exp, 1)
            for q in range(NT // 4):
                act.wait_ge(s.c_T, q + 1)
                act.activation(cT[:, q * 4 * P:(q + 1) * 4 * P], bank[q % 2][0:E, :], ACT.Copy).then_inc(s.c_Ts, 1)
            for t in range(BUFS, NT):
                load(t)

        @block.sync
        def _(sp):
            for t in range(NT):
                b, c = t % NB, t // NB
                sp.wait_ge(s.c_o, t + 1)
                sp.dma_start(v.out[b, c * P:(c + 1) * P, :], o[:, t % BUFS, :]).then_inc(c_out[t % BUFS], 16)
            for done_out in c_out:
                sp.wait_ge(done_out, NT // BUFS * 16)

        @block.gpsimd
        def _(pool):
            for t, k in v.gathers[min(2 * (NT + RT - GATHER_FROM), v.EARLY):]:
                v.gather(pool, t, k)

        @block.tensor
        def _(pe):
            pe.wait_ge(s.c_comb, 1)
            for q in range(NT // 4):
                if q >= 2:
                    pe.wait_ge(s.c_Ts, q - 1)
                for b in range(4):
                    mm = pe.transpose(bank[q % 2][0:E, b * P:(b + 1) * P], comb[:, q * 4 + b, :], v.ident)
                mm.then_inc(s.c_T, 1)
            for t in range(NT):
                pe.wait_ge(s.c_Ts, t // 4 + 1)
                if t >= 4:
                    pe.wait_ge(s.c_a1, t - 3)
                dst = bank[2 + t % 4][:, 0:D]
                pe.matmul(dst, cT[:, t * P:(t + 1) * P], v.B2[:], start=True, stop=False)
                pe.matmul(dst, v.ident, v.hbuf[:, t, :], start=False, stop=False)
                pe.wait_ge(c_sh[t % BUFS], (t // BUFS + 1) * 16)
                pe.matmul(dst, v.ident, ysh[:, t % BUFS, :], start=False, stop=True).then_inc(s.c_b, 1)

        @block.vector
        def _(dve):
            n = [0]

            def link(ins):
                n[0] += 1
                ins.then_inc(s.c_chain, 1)
                dve.wait_ge(s.c_chain, n[0])

            link(dve.memset(v.scores[:, :, 0:1], -1e9))
            best = v.score3[:, :, 0:1]
            link(dve.tensor_tensor(ex[:], v.scores[:], best.broadcast_to([P, NT, E]), ALU.subtract))
            link(dve.tensor_tensor(w3[:], v.score3[:], best.broadcast_to([P, NT, TOPK]), ALU.subtract))
            dve.sem_inc(s.c_exp_in, 1)
            ek = v.picked[:].rearrange("p t (k u) -> p (t k) u", u=1).broadcast_to([P, NK, E])
            link(dve.tensor_tensor(hot[:], v.rows[:, 0:E].rearrange("p (o e) -> p o e", o=1).broadcast_to([P, NK, E]),
                                   ek, ALU.is_equal))
            dve.wait_ge(s.c_exp, 2)
            link(dve.tensor_reduce(sm[:], ex[:], AX.X, ALU.add))
            link(dve.reciprocal(rsm[:], sm[:]))
            link(dve.tensor_tensor(w3[:], w3[:], rsm[:].rearrange("p (t u) -> p t u", u=1).broadcast_to([P, NT, TOPK]),
                                   ALU.mult))
            link(dve.tensor_tensor(tmp[:], hot[:],
                                   w3[:].rearrange("p t (k u) -> p (t k) u", u=1).broadcast_to([P, NK, E]), ALU.mult))
            t4 = tmp[:].rearrange("p (t k) e -> p t k e", k=TOPK)
            link(dve.tensor_tensor(comb[:], t4[:, :, 0, :], t4[:, :, 1, :], ALU.add))
            link(dve.tensor_tensor(comb[:], comb[:], t4[:, :, 2, :], ALU.add))
            link(dve.memset(comb[:, :, 0:1], 1.0))
            dve.sem_inc(s.c_comb, 1)
            for pair in range(NT // 2):
                both = (2 * pair, 2 * pair + 1)
                for t in both:
                    dve.wait_ge(s.c_b, t + 1)
                    dve.wait_ge(v.gathered[t // 4], 4 * TOPK * 16)
                    dve.scalar_tensor_tensor(v.hbuf[:, t, :], v.routed(t)[:, 0, :], w3[:, t, 0:1],
                                             bank[2 + t % 4][:, 0:D], ALU.mult, ALU.add).then_inc(s.c_a1, 1)
                for t in both:
                    hrow = v.hbuf[:, t, :]
                    dve.wait_ge(s.c_a1, t + 1)
                    dve.scalar_tensor_tensor(hrow, v.routed(t)[:, 1, :], w3[:, t, 1:2], hrow,
                                             ALU.mult, ALU.add).then_inc(s.c_a2, 1)
                for t in both:
                    m = t % BUFS
                    dve.wait_ge(s.c_a2, t + 1)
                    if t >= BUFS:
                        dve.wait_ge(c_out[m], t // BUFS * 16)
                    dve.scalar_tensor_tensor(o[:, m, :], v.routed(t)[:, 2, :], w3[:, t, 2:3], v.hbuf[:, t, :],
                                             ALU.mult, ALU.add).then_inc(s.c_o, 1)


_OUTS = [((NB, L, D), "float32")]


def shape_constants():
    f = np.float32
    p = np.arange(L, dtype=f)[:, None]
    exps = (np.floor(np.arange(D, dtype=f) / f(2)) * f(2) / f(D))[None]
    den = np.power(10000.0, exps.astype(np.float64)).astype(f)
    ang = (p / den).astype(np.float64)
    pos = np.where(np.arange(D) % 2 == 0, np.sin(ang), np.cos(ang)).astype(f)
    inv = (f(1) / np.power(10000.0, (np.arange(0, DH, 2, dtype=f) / f(DH)).astype(np.float64)).astype(f))
    fr = (p * inv[None]).astype(f).astype(np.float64)
    cos = np.concatenate([np.cos(fr), np.cos(fr)], 1)
    sin = np.concatenate([np.sin(fr), -np.sin(fr)], 1)
    rope = np.stack([cos, sin]).astype(f)
    a = np.arange(P)
    mats = np.stack([np.eye(P), a[:, None] <= a[None], a[:, None] < a[None], np.ones((P, P))], 1).astype(f)
    rows = np.arange(256, dtype=f)[None]
    lpos = np.concatenate([np.arange(NG)[None] * P + a[:, None] + 1, a[:, None]], 1).astype(f)
    return dict(c_pos=pos, c_rope=rope, c_mats=mats, c_rows=rows, c_lpos=lpos)


_INS = ["x", "mask_BS_i2_0", "L0_tok_token_table", "L0_tok_segm_table", "L0_attn_ln_w", "L0_attn_w_comp",
        "L0_attn_w_qkv", "L0_attn_w_reso", "L0_attn_qn_w", "L0_attn_kn_w", "L0_attn_w_outgate",
        "L0_attn_head_decay", "L0_attn_temperature", "L0_attn_w_proj", "L0_attn_memn_w", "L0_attn_ffn_ln_w",
        "L0_attn_w1", "L0_attn_w2", "L0_attn_w3", "L0_ffn_gate_w", "L0_ffn_gate_b", "L0_ffn_fc1_w",
        "L0_ffn_fc1_b", "L0_ffn_ln_w", "L0_ffn_ln_b", "L0_ffn_fc2_w", "L0_ffn_fc2_b"]


def kernel(**inputs):
    import numpy as _np
    import concourse.bacc as _bacc
    from concourse import mybir as _mybir
    from concourse.bass_utils import run_bass_kernel_spmd as _run

    nc = _bacc.Bacc("TRN2", target_bir_lowering=False, num_devices=1)
    arrays, args = {}, []
    consts = shape_constants()
    for name in _INS + list(consts):
        a = _np.ascontiguousarray(inputs[name] if name in inputs else consts[name])
        arrays[f"in_{name}"] = a
        args.append(nc.dram_tensor(f"in_{name}", a.shape, _mybir.dt.from_np(a.dtype), kind="ExternalInput").ap())
    for i, (shape, dtype) in enumerate(_OUTS):
        dt = _mybir.dt.from_np(_np.dtype(dtype))
        args.append(nc.dram_tensor(f"out_{i}", shape, dt, kind="ExternalOutput").ap())
    program(nc, *args)
    r = _run(nc, [arrays], core_ids=[0])
    return r.results[0]["out_0"]
```
